# Optimizing a Trainium2 kernel written in Bass

```python
import numpy as np
import jax
import jax.numpy as jnp

def _softmax(x, axis=-1):
    return jax.nn.softmax(x, axis=axis)

def _gelu(x):
    return jax.nn.gelu(x, approximate=True)

def _silu(x):
    return jax.nn.silu(x)

def _sigmoid(x):
    return jax.nn.sigmoid(x)

def _layernorm(x, axis=-1, eps=1e-05):
    m = jnp.mean(x, axis=axis, keepdims=True)
    v = jnp.var(x, axis=axis, keepdims=True)
    return (x - m) / jnp.sqrt(v + eps)

def _scatter_add(tgt, idx, src, axis=0):
    return tgt.at[idx].add(src)

def _segment_sum(src, seg, n):
    return jax.ops.segment_sum(src, seg, n)
kernel_name = 'mk_seq_preln_d4_jaxref_r8_a622f9'

def setup_inputs(seed: int=0):
    np.random.seed(seed)
    _w = jnp.asarray

    def _L0_attn_setup():
        import jax, jax.numpy as jnp
        import numpy as np
        B, S, D, H = (4, 256, 128, 512)
        EPS = 1e-12

        def _linear(x, W, b):
            return x @ W.T + b
        key = jax.random.key(seed)
        ks = jax.random.split(key, 14)
        s = lambda d: 1.0 / np.sqrt(d)
        return {'x': jax.random.normal(ks[0], (B, S, D), dtype=jnp.float32), 'Wq': jax.random.normal(ks[1], (D, D), dtype=jnp.float32) * s(D), 'bq': jax.random.normal(ks[2], (D,), dtype=jnp.float32) * 0.01, 'Wk': jax.random.normal(ks[3], (D, D), dtype=jnp.float32) * s(D), 'bk': jax.random.normal(ks[4], (D,), dtype=jnp.float32) * 0.01, 'Wv': jax.random.normal(ks[5], (D, D), dtype=jnp.float32) * s(D), 'bv': jax.random.normal(ks[6], (D,), dtype=jnp.float32) * 0.01, 'W1': jax.random.normal(ks[7], (D, D), dtype=jnp.float32) * s(D), 'b1': jax.random.normal(ks[8], (D,), dtype=jnp.float32) * 0.01, 'W2': jax.random.normal(ks[9], (H, D), dtype=jnp.float32) * s(D), 'b2': jax.random.normal(ks[10], (H,), dtype=jnp.float32) * 0.01, 'W3': jax.random.normal(ks[11], (D, H), dtype=jnp.float32) * s(H), 'b3': jax.random.normal(ks[12], (D,), dtype=jnp.float32) * 0.01}
    _L0_attn_in = _L0_attn_setup()

    def _L0_ffn_setup():
        import jax, jax.numpy as jnp
        import numpy as np
        E = 8
        K = 2
        D = 128
        F = 512

        def _selected_matmul(inp, weight, scales, one_hot):
            wq = weight * scales
            all_out = jnp.einsum('mk,bkn->bmn', inp, wq)
            return jnp.einsum('bm,bmn->mn', one_hot, all_out)
        key = jax.random.key(seed)
        ks = jax.random.split(key, 8)
        inputs = jax.random.normal(ks[0], (1, 256, D), dtype=jnp.float32)
        router_w = jax.random.normal(ks[1], (D, E), dtype=jnp.float32) * 0.02
        wv = jax.random.normal(ks[2], (E, D, F), dtype=jnp.float32) * 0.02
        sv = jax.random.uniform(ks[3], (E, 1, F), dtype=jnp.float32, minval=0.5, maxval=1.5)
        w = jax.random.normal(ks[4], (E, D, F), dtype=jnp.float32) * 0.02
        s = jax.random.uniform(ks[5], (E, 1, F), dtype=jnp.float32, minval=0.5, maxval=1.5)
        w1 = jax.random.normal(ks[6], (E, F, D), dtype=jnp.float32) * 0.02
        s1 = jax.random.uniform(ks[7], (E, 1, D), dtype=jnp.float32, minval=0.5, maxval=1.5)
        return {'inputs': inputs, 'router_w': router_w, 'wv': wv, 'sv': sv, 'w': w, 's': s, 'w1': w1, 's1': s1}
    _L0_ffn_in = _L0_ffn_setup()

    def _L1_attn_setup():
        import jax, jax.numpy as jnp
        import numpy as np
        B, N, D, H = (4, 512, 128, 16)
        DH = D // H
        M = int(DH * np.log(DH))
        EPS = 0.0001

        def softmax_kernel(t, proj, is_query):
            dn = t.shape[-1] ** (-0.25)
            ratio = proj.shape[0] ** (-0.5)
            td = jnp.einsum('bhnd,md->bhnm', t * dn, proj)
            diag = 0.5 * dn ** 2 * jnp.sum(t * t, axis=-1, keepdims=True)
            if is_query:
                mx = jnp.max(td, axis=-1, keepdims=True)
            else:
                mx = jnp.max(td, axis=(-1, -2), keepdims=True)
            return ratio * (jnp.exp(td - diag - mx) + EPS)
        key = jax.random.key(seed)
        ks = jax.random.split(key, 12)
        s = 0.02
        inp = {'x': jax.random.normal(ks[0], (B, N, D), jnp.float32), 'Wq': jax.random.normal(ks[1], (D, D), jnp.float32) * s, 'bq': jnp.zeros((D,), jnp.float32), 'Wk': jax.random.normal(ks[2], (D, D), jnp.float32) * s, 'bk': jnp.zeros((D,), jnp.float32), 'Wv': jax.random.normal(ks[3], (D, D), jnp.float32) * s, 'bv': jnp.zeros((D,), jnp.float32), 'Wo': jax.random.normal(ks[4], (D, D), jnp.float32) * s, 'bo': jnp.zeros((D,), jnp.float32), 'Wfc': jax.random.normal(ks[5], (D, D), jnp.float32) * s, 'bfc': jnp.zeros((D,), jnp.float32), 'proj': jax.random.normal(ks[6], (M, DH), jnp.float32)}
        return inp
    _L1_attn_in = _L1_attn_setup()

    def _L1_ffn_setup():
        import jax, jax.numpy as jnp
        import numpy as np
        H, E, DFF = (128, 8, 512)
        key = jax.random.key(seed)
        ks = jax.random.split(key, 7)
        s = lambda *shape: 1.0 / np.sqrt(shape[-2] if len(shape) > 1 else shape[-1])
        x = jax.random.normal(ks[0], (2, 256, H), dtype=jnp.float32)
        Wr = jax.random.normal(ks[1], (H, E), dtype=jnp.float32) * (1.0 / np.sqrt(H))
        br = jnp.zeros((E,), dtype=jnp.float32)
        W1 = jax.random.normal(ks[2], (E, H, DFF), dtype=jnp.float32) * (1.0 / np.sqrt(H))
        b1 = jnp.zeros((E, DFF), dtype=jnp.float32)
        W2 = jax.random.normal(ks[3], (E, DFF, H), dtype=jnp.float32) * (1.0 / np.sqrt(DFF))
        b2 = jnp.zeros((E, H), dtype=jnp.float32)
        return {'x': x, 'Wr': Wr, 'br': br, 'W1': W1, 'b1': b1, 'W2': W2, 'b2': b2}
    _L1_ffn_in = _L1_ffn_setup()

    def _L2_attn_setup():
        import jax, jax.numpy as jnp
        import numpy as np
        from jax import lax
        D_MODEL = 128
        D_STATE = 16
        D_CONV = 4
        EXPAND = 2
        D_INNER = EXPAND * D_MODEL
        DT_RANK = (D_MODEL + 15) // 16
        B, L = (4, 256)

        def _silu(v):
            return v * jax.nn.sigmoid(v)

        def _mamba_forward(x, ln_w, ln_b, W_in, conv_w, conv_b, W_xproj, W_dt, b_dt, A_log, D_param, W_out):
            eps = 1e-05
            mu = jnp.mean(x, axis=-1, keepdims=True)
            var = jnp.mean(jnp.square(x - mu), axis=-1, keepdims=True)
            xn = (x - mu) * lax.rsqrt(var + eps) * ln_w + ln_b
            xz = jnp.einsum('bld,de->ble', xn, W_in)
            x_in, z = jnp.split(xz, 2, axis=-1)
            xt = jnp.transpose(x_in, (0, 2, 1))
            xc = lax.conv_general_dilated(xt, conv_w, window_strides=(1,), padding=[(D_CONV - 1, 0)], feature_group_count=D_INNER, dimension_numbers=('NCH', 'OIH', 'NCH'))
            xc = _silu(xc + conv_b[None, :, None])
            xc = jnp.transpose(xc, (0, 2, 1))
            xdbl = jnp.einsum('bld,de->ble', xc, W_xproj)
            dt_r = xdbl[..., :DT_RANK]
            Bm = xdbl[..., DT_RANK:DT_RANK + D_STATE]
            Cm = xdbl[..., DT_RANK + D_STATE:]
            dt = jax.nn.softplus(jnp.einsum('blr,rd->bld', dt_r, W_dt) + b_dt)
            A = -jnp.exp(A_log)

            def step(h, inp):
                dt_t, B_t, C_t, u_t = inp
                dA = jnp.exp(dt_t[:, :, None] * A)
                h = h * dA + dt_t[:, :, None] * B_t[:, None, :] * u_t[:, :, None]
                y = jnp.einsum('bdn,bn->bd', h, C_t)
                return (h, y)
            h0 = jnp.zeros((x.shape[0], D_INNER, D_STATE), x.dtype)
            xs = (jnp.swapaxes(dt, 0, 1), jnp.swapaxes(Bm, 0, 1), jnp.swapaxes(Cm, 0, 1), jnp.swapaxes(xc, 0, 1))
            _, ys = lax.scan(step, h0, xs)
            y = jnp.swapaxes(ys, 0, 1) + xc * D_param
            y = y * _silu(z)
            out = jnp.einsum('bld,de->ble', y, W_out)
            return x + out
        key = jax.random.key(seed)
        ks = jax.random.split(key, 12)
        g = lambda k, sh, s: jax.random.normal(k, sh, dtype=jnp.float32) * s
        A_log = jnp.log(jnp.tile(jnp.arange(1, D_STATE + 1, dtype=jnp.float32)[None, :], (D_INNER, 1)))
        return {'x': g(ks[0], (B, L, D_MODEL), 1.0), 'ln_w': jnp.ones((D_MODEL,), jnp.float32), 'ln_b': jnp.zeros((D_MODEL,), jnp.float32), 'W_in': g(ks[1], (D_MODEL, 2 * D_INNER), 0.02), 'conv_w': g(ks[2], (D_INNER, 1, D_CONV), 0.1), 'conv_b': g(ks[3], (D_INNER,), 0.02), 'W_xproj': g(ks[4], (D_INNER, DT_RANK + 2 * D_STATE), 0.02), 'W_dt': g(ks[5], (DT_RANK, D_INNER), 0.02), 'b_dt': g(ks[6], (D_INNER,), 0.5), 'A_log': A_log, 'D_param': jnp.ones((D_INNER,), jnp.float32), 'W_out': g(ks[7], (D_INNER, D_MODEL), 0.02)}
    _L2_attn_in = _L2_attn_setup()

    def _L2_ffn_setup():
        import jax, jax.numpy as jnp
        import numpy as np
        NUM_EXPERTS = 8
        EXPERT_CAPACITY = 2.0
        key = jax.random.key(seed)
        k1, k2, k3, k4 = jax.random.split(key, 4)
        B, T, C, H, E = (4, 512, 128, 512, NUM_EXPERTS)
        x = jax.random.normal(k1, (B, T, C), jnp.float32)
        gate_w = jax.random.normal(k2, (C, E), jnp.float32) * 0.02
        w1 = jax.random.normal(k3, (E, C, H), jnp.float32) * 0.02
        w2 = jax.random.normal(k4, (E, H, C), jnp.float32) * 0.02
        return {'x': x, 'gate_w': gate_w, 'w1': w1, 'w2': w2}
    _L2_ffn_in = _L2_ffn_setup()

    def _L3_attn_setup():
        import jax, jax.numpy as jnp
        import numpy as np
        B, S, D = (2, 256, 128)
        H, DK = (16, 64)
        NUM_BUCKETS = 32
        MAX_DIST = 128
        SM_SCALE = 1.0 / np.sqrt(H)

        def _relative_position_buckets(qlen, klen):
            ctx = jnp.arange(qlen, dtype=jnp.int32)[:, None]
            mem = jnp.arange(klen, dtype=jnp.int32)[None, :]
            rp = mem - ctx
            nb = NUM_BUCKETS // 2
            ret = (rp > 0).astype(jnp.int32) * nb
            rpa = jnp.abs(rp)
            max_exact = nb // 2
            is_small = rpa < max_exact
            rpf = jnp.maximum(rpa, 1).astype(jnp.float32)
            large = max_exact + (jnp.log(rpf / max_exact) / np.log(MAX_DIST / max_exact) * (nb - max_exact)).astype(jnp.int32)
            large = jnp.minimum(large, nb - 1)
            return ret + jnp.where(is_small, rpa, large)
        key = jax.random.key(seed)
        ks = jax.random.split(key, 6)
        w = 0.02
        return {'hidden_states': jax.random.normal(ks[0], (B, S, D), jnp.float32), 'Wq': jax.random.normal(ks[1], (D, H * DK), jnp.float32) * w, 'Wk': jax.random.normal(ks[2], (D, H * DK), jnp.float32) * w, 'Wv': jax.random.normal(ks[3], (D, H * DK), jnp.float32) * w, 'Wo': jax.random.normal(ks[4], (H * DK, D), jnp.float32) * w, 'rel_bias': jax.random.normal(ks[5], (NUM_BUCKETS, H), jnp.float32) * w}
    _L3_attn_in = _L3_attn_setup()

    def _L3_ffn_setup():
        import jax, jax.numpy as jnp
        import numpy as np
        MAX_THRESHOLD = 0.125
        key = jax.random.key(seed)
        ks = jax.random.split(key, 5)
        B, S, D, FF, E = (2, 256, 128, 512, 8)
        sd = 1.0 / np.sqrt(D)
        sf = 1.0 / np.sqrt(FF)
        return {'inputs': jax.random.normal(ks[0], (B, S, D), dtype=jnp.float32), 'Wg': jax.random.normal(ks[1], (D, E), dtype=jnp.float32) * sd, 'bg': jnp.zeros((E,), dtype=jnp.float32), 'Wt': jax.random.normal(ks[2], (D, 1), dtype=jnp.float32) * sd, 'bt': jnp.zeros((1,), dtype=jnp.float32), 'W1': jax.random.normal(ks[3], (E, D, FF), dtype=jnp.float32) * sd, 'b1': jnp.zeros((E, FF), dtype=jnp.float32), 'W2': jax.random.normal(ks[4], (E, FF, D), dtype=jnp.float32) * sf, 'b2': jnp.zeros((E, D), dtype=jnp.float32)}
    _L3_ffn_in = _L3_ffn_setup()
    _d = {'L0_attn_x': _L0_attn_in['x'], 'L0_attn_Wq': _L0_attn_in['Wq'], 'L0_attn_bq': _L0_attn_in['bq'], 'L0_attn_Wk': _L0_attn_in['Wk'], 'L0_attn_bk': _L0_attn_in['bk'], 'L0_attn_Wv': _L0_attn_in['Wv'], 'L0_attn_bv': _L0_attn_in['bv'], 'L0_attn_W1': _L0_attn_in['W1'], 'L0_attn_b1': _L0_attn_in['b1'], 'L0_attn_W2': _L0_attn_in['W2'], 'L0_attn_b2': _L0_attn_in['b2'], 'L0_attn_W3': _L0_attn_in['W3'], 'L0_attn_b3': _L0_attn_in['b3'], 'L0_ffn_router_w': _L0_ffn_in['router_w'], 'L0_ffn_wv': _L0_ffn_in['wv'], 'L0_ffn_sv': _L0_ffn_in['sv'], 'L0_ffn_w': _L0_ffn_in['w'], 'L0_ffn_s': _L0_ffn_in['s'], 'L0_ffn_w1': _L0_ffn_in['w1'], 'L0_ffn_s1': _L0_ffn_in['s1'], 'L1_attn_Wq': _L1_attn_in['Wq'], 'L1_attn_bq': _L1_attn_in['bq'], 'L1_attn_Wk': _L1_attn_in['Wk'], 'L1_attn_bk': _L1_attn_in['bk'], 'L1_attn_Wv': _L1_attn_in['Wv'], 'L1_attn_bv': _L1_attn_in['bv'], 'L1_attn_Wo': _L1_attn_in['Wo'], 'L1_attn_bo': _L1_attn_in['bo'], 'L1_attn_Wfc': _L1_attn_in['Wfc'], 'L1_attn_bfc': _L1_attn_in['bfc'], 'L1_attn_proj': _L1_attn_in['proj'], 'L1_ffn_Wr': _L1_ffn_in['Wr'], 'L1_ffn_br': _L1_ffn_in['br'], 'L1_ffn_W1': _L1_ffn_in['W1'], 'L1_ffn_b1': _L1_ffn_in['b1'], 'L1_ffn_W2': _L1_ffn_in['W2'], 'L1_ffn_b2': _L1_ffn_in['b2'], 'L2_attn_ln_w': _L2_attn_in['ln_w'], 'L2_attn_ln_b': _L2_attn_in['ln_b'], 'L2_attn_W_in': _L2_attn_in['W_in'], 'L2_attn_conv_w': _L2_attn_in['conv_w'], 'L2_attn_conv_b': _L2_attn_in['conv_b'], 'L2_attn_W_xproj': _L2_attn_in['W_xproj'], 'L2_attn_W_dt': _L2_attn_in['W_dt'], 'L2_attn_b_dt': _L2_attn_in['b_dt'], 'L2_attn_A_log': _L2_attn_in['A_log'], 'L2_attn_D_param': _L2_attn_in['D_param'], 'L2_attn_W_out': _L2_attn_in['W_out'], 'L2_ffn_gate_w': _L2_ffn_in['gate_w'], 'L2_ffn_w1': _L2_ffn_in['w1'], 'L2_ffn_w2': _L2_ffn_in['w2'], 'L3_attn_Wq': _L3_attn_in['Wq'], 'L3_attn_Wk': _L3_attn_in['Wk'], 'L3_attn_Wv': _L3_attn_in['Wv'], 'L3_attn_Wo': _L3_attn_in['Wo'], 'L3_attn_rel_bias': _L3_attn_in['rel_bias'], 'L3_ffn_Wg': _L3_ffn_in['Wg'], 'L3_ffn_bg': _L3_ffn_in['bg'], 'L3_ffn_Wt': _L3_ffn_in['Wt'], 'L3_ffn_bt': _L3_ffn_in['bt'], 'L3_ffn_W1': _L3_ffn_in['W1'], 'L3_ffn_b1': _L3_ffn_in['b1'], 'L3_ffn_W2': _L3_ffn_in['W2'], 'L3_ffn_b2': _L3_ffn_in['b2']}
    _x0 = _d['L0_attn_x']
    _d['L0_attn_x'] = jax.random.normal(jax.random.fold_in(jax.random.key(seed), 1), (8, 512, 128), dtype=_x0.dtype)
    del _x0
    return _d

def reference(L0_attn_x, L0_attn_Wq, L0_attn_bq, L0_attn_Wk, L0_attn_bk, L0_attn_Wv, L0_attn_bv, L0_attn_W1, L0_attn_b1, L0_attn_W2, L0_attn_b2, L0_attn_W3, L0_attn_b3, L0_ffn_router_w, L0_ffn_wv, L0_ffn_sv, L0_ffn_w, L0_ffn_s, L0_ffn_w1, L0_ffn_s1, L1_attn_Wq, L1_attn_bq, L1_attn_Wk, L1_attn_bk, L1_attn_Wv, L1_attn_bv, L1_attn_Wo, L1_attn_bo, L1_attn_Wfc, L1_attn_bfc, L1_attn_proj, L1_ffn_Wr, L1_ffn_br, L1_ffn_W1, L1_ffn_b1, L1_ffn_W2, L1_ffn_b2, L2_attn_ln_w, L2_attn_ln_b, L2_attn_W_in, L2_attn_conv_w, L2_attn_conv_b, L2_attn_W_xproj, L2_attn_W_dt, L2_attn_b_dt, L2_attn_A_log, L2_attn_D_param, L2_attn_W_out, L2_ffn_gate_w, L2_ffn_w1, L2_ffn_w2, L3_attn_Wq, L3_attn_Wk, L3_attn_Wv, L3_attn_Wo, L3_attn_rel_bias, L3_ffn_Wg, L3_ffn_bg, L3_ffn_Wt, L3_ffn_bt, L3_ffn_W1, L3_ffn_b1, L3_ffn_W2, L3_ffn_b2):

    def _L0_attn_ref(x, Wq, bq, Wk, bk, Wv, bv, W1, b1, W2, b2, W3, b3):
        import jax, jax.numpy as jnp
        import numpy as np
        B, S, D, H = (4, 256, 128, 512)
        EPS = 1e-12

        def _linear(x, W, b):
            return x @ W.T + b
        Q = _linear(x, Wq, bq)
        K = _linear(x, Wk, bk)
        V = _linear(x, Wv, bv)
        Q = Q / jnp.maximum(jnp.linalg.norm(Q, axis=2, keepdims=True), EPS)
        K = K / jnp.maximum(jnp.linalg.norm(K, axis=2, keepdims=True), EPS)
        sim = jnp.einsum('bqd,bkd->bqk', Q, K)
        attn = jax.nn.softmax(sim, axis=2)
        out = jnp.einsum('bqk,bkd->bqd', attn, V)
        h = jax.nn.relu(_linear(out, W1, b1))
        h = jax.nn.relu(_linear(h, W2, b2))
        return _linear(h, W3, b3)

    def _L0_ffn_ref(inputs, router_w, wv, sv, w, s, w1, s1):
        import jax, jax.numpy as jnp
        import numpy as np
        E = 8
        K = 2
        D = 128
        F = 512

        def _selected_matmul(inp, weight, scales, one_hot):
            wq = weight * scales
            all_out = jnp.einsum('mk,bkn->bmn', inp, wq)
            return jnp.einsum('bm,bmn->mn', one_hot, all_out)
        B, S, Dm = inputs.shape
        x = inputs.reshape(B * S, Dm)
        logits = jnp.dot(x.astype(jnp.float32), router_w)
        probs = jax.nn.softmax(logits, axis=-1)
        expert_gate, expert_index = jax.lax.top_k(probs, K)
        xb = jnp.repeat(x, K, axis=0)
        one_hot = jax.nn.one_hot(expert_index.reshape(-1), E, axis=0)
        v = _selected_matmul(xb, wv, sv, one_hot)
        y = jax.nn.gelu(_selected_matmul(xb, w, s, one_hot))
        out = _selected_matmul(v * y, w1, s1, one_hot)
        out = out.reshape(B, S, K, Dm)
        out = jnp.sum(expert_gate.reshape(B, S, K, 1) * out, axis=2)
        return out

    def _L1_attn_ref(x, Wq, bq, Wk, bk, Wv, bv, Wo, bo, Wfc, bfc, proj):
        import jax, jax.numpy as jnp
        import numpy as np
        B, N, D, H = (4, 512, 128, 16)
        DH = D // H
        M = int(DH * np.log(DH))
        EPS = 0.0001

        def softmax_kernel(t, proj, is_query):
            dn = t.shape[-1] ** (-0.25)
            ratio = proj.shape[0] ** (-0.5)
            td = jnp.einsum('bhnd,md->bhnm', t * dn, proj)
            diag = 0.5 * dn ** 2 * jnp.sum(t * t, axis=-1, keepdims=True)
            if is_query:
                mx = jnp.max(td, axis=-1, keepdims=True)
            else:
                mx = jnp.max(td, axis=(-1, -2), keepdims=True)
            return ratio * (jnp.exp(td - diag - mx) + EPS)
        b, n, d = x.shape

        def heads(t):
            return t.reshape(b, n, H, DH).transpose(0, 2, 1, 3)
        q = heads(x @ Wq.T + bq)
        k = heads(x @ Wk.T + bk)
        v = heads(x @ Wv.T + bv)
        qp = softmax_kernel(q, proj, is_query=True)
        kp = softmax_kernel(k, proj, is_query=False)
        k_sum = jnp.sum(kp, axis=-2)
        d_inv = 1.0 / jnp.einsum('bhnm,bhm->bhn', qp, k_sum)
        context = jnp.einsum('bhnm,bhnd->bhmd', kp, v)
        out = jnp.einsum('bhmd,bhnm,bhn->bhnd', context, qp, d_inv)
        out = out.transpose(0, 2, 1, 3).reshape(b, n, d)
        h = out @ Wo.T + bo
        return jax.nn.relu(h @ Wfc.T + bfc)

    def _L1_ffn_ref(x, Wr, br, W1, b1, W2, b2):
        import jax, jax.numpy as jnp
        import numpy as np
        H, E, DFF = (128, 8, 512)
        B, S, Hd = x.shape
        n_exp = W1.shape[0]
        xt = x.reshape(-1, Hd)
        logits = xt @ Wr + br
        probs = jax.nn.softmax(logits, axis=-1)
        gate = jnp.max(probs, axis=-1)
        idx = jnp.argmax(probs, axis=-1)
        h1 = jnp.maximum(jnp.einsum('th,ehf->etf', xt, W1) + b1[:, None, :], 0.0)
        ye = jnp.einsum('etf,efh->eth', h1, W2) + b2[:, None, :]
        onehot = jax.nn.one_hot(idx, n_exp, dtype=xt.dtype)
        y = jnp.einsum('te,eth->th', onehot, ye) * gate[:, None]
        return y.reshape(B, S, Hd)

    def _L2_attn_ref(x, ln_w, ln_b, W_in, conv_w, conv_b, W_xproj, W_dt, b_dt, A_log, D_param, W_out):
        import jax, jax.numpy as jnp
        import numpy as np
        from jax import lax
        D_MODEL = 128
        D_STATE = 16
        D_CONV = 4
        EXPAND = 2
        D_INNER = EXPAND * D_MODEL
        DT_RANK = (D_MODEL + 15) // 16
        B, L = (4, 256)

        def _silu(v):
            return v * jax.nn.sigmoid(v)

        def _mamba_forward(x, ln_w, ln_b, W_in, conv_w, conv_b, W_xproj, W_dt, b_dt, A_log, D_param, W_out):
            eps = 1e-05
            mu = jnp.mean(x, axis=-1, keepdims=True)
            var = jnp.mean(jnp.square(x - mu), axis=-1, keepdims=True)
            xn = (x - mu) * lax.rsqrt(var + eps) * ln_w + ln_b
            xz = jnp.einsum('bld,de->ble', xn, W_in)
            x_in, z = jnp.split(xz, 2, axis=-1)
            xt = jnp.transpose(x_in, (0, 2, 1))
            xc = lax.conv_general_dilated(xt, conv_w, window_strides=(1,), padding=[(D_CONV - 1, 0)], feature_group_count=D_INNER, dimension_numbers=('NCH', 'OIH', 'NCH'))
            xc = _silu(xc + conv_b[None, :, None])
            xc = jnp.transpose(xc, (0, 2, 1))
            xdbl = jnp.einsum('bld,de->ble', xc, W_xproj)
            dt_r = xdbl[..., :DT_RANK]
            Bm = xdbl[..., DT_RANK:DT_RANK + D_STATE]
            Cm = xdbl[..., DT_RANK + D_STATE:]
            dt = jax.nn.softplus(jnp.einsum('blr,rd->bld', dt_r, W_dt) + b_dt)
            A = -jnp.exp(A_log)

            def step(h, inp):
                dt_t, B_t, C_t, u_t = inp
                dA = jnp.exp(dt_t[:, :, None] * A)
                h = h * dA + dt_t[:, :, None] * B_t[:, None, :] * u_t[:, :, None]
                y = jnp.einsum('bdn,bn->bd', h, C_t)
                return (h, y)
            h0 = jnp.zeros((x.shape[0], D_INNER, D_STATE), x.dtype)
            xs = (jnp.swapaxes(dt, 0, 1), jnp.swapaxes(Bm, 0, 1), jnp.swapaxes(Cm, 0, 1), jnp.swapaxes(xc, 0, 1))
            _, ys = lax.scan(step, h0, xs)
            y = jnp.swapaxes(ys, 0, 1) + xc * D_param
            y = y * _silu(z)
            out = jnp.einsum('bld,de->ble', y, W_out)
            return x + out
        return _mamba_forward(x, ln_w, ln_b, W_in, conv_w, conv_b, W_xproj, W_dt, b_dt, A_log, D_param, W_out)

    def _L2_ffn_ref(x, gate_w, w1, w2):
        import jax, jax.numpy as jnp
        import numpy as np
        NUM_EXPERTS = 8
        EXPERT_CAPACITY = 2.0
        B, T, C = x.shape
        E = gate_w.shape[1]
        cap = int(EXPERT_CAPACITY * T / E)
        scores = jnp.einsum('BTC,CE->BTE', x, gate_w)
        probs = jax.nn.softmax(scores, axis=-1)
        probs_et = jnp.transpose(probs, (0, 2, 1))
        top_p, top_idx = jax.lax.top_k(probs_et, cap)
        xin = jnp.take_along_axis(x[:, None, :, :], top_idx[..., None], axis=2)
        h = jax.nn.gelu(jnp.einsum('BElC,ECH->BElH', xin, w1), approximate=False)
        y = jnp.einsum('BElH,EHC->BElC', h, w2)
        y = y * top_p[..., None]
        b_idx = jnp.arange(B)[:, None, None]
        out = jnp.zeros((B, T, C), x.dtype).at[b_idx, top_idx].add(y)
        return out

    def _L3_attn_ref(hidden_states, Wq, Wk, Wv, Wo, rel_bias):
        import jax, jax.numpy as jnp
        import numpy as np
        B, S, D = (2, 256, 128)
        H, DK = (16, 64)
        NUM_BUCKETS = 32
        MAX_DIST = 128
        SM_SCALE = 1.0 / np.sqrt(H)

        def _relative_position_buckets(qlen, klen):
            ctx = jnp.arange(qlen, dtype=jnp.int32)[:, None]
            mem = jnp.arange(klen, dtype=jnp.int32)[None, :]
            rp = mem - ctx
            nb = NUM_BUCKETS // 2
            ret = (rp > 0).astype(jnp.int32) * nb
            rpa = jnp.abs(rp)
            max_exact = nb // 2
            is_small = rpa < max_exact
            rpf = jnp.maximum(rpa, 1).astype(jnp.float32)
            large = max_exact + (jnp.log(rpf / max_exact) / np.log(MAX_DIST / max_exact) * (nb - max_exact)).astype(jnp.int32)
            large = jnp.minimum(large, nb - 1)
            return ret + jnp.where(is_small, rpa, large)
        b, s, d = hidden_states.shape
        q = (hidden_states @ Wq).reshape(b, s, H, DK)
        k = (hidden_states @ Wk).reshape(b, s, H, DK)
        v = (hidden_states @ Wv).reshape(b, s, H, DK)
        buckets = _relative_position_buckets(s, s)
        bias = rel_bias[buckets]
        bias = jnp.transpose(bias, (2, 0, 1))[None]
        scores = jnp.einsum('bqhd,bkhd->bhqk', q, k) * SM_SCALE + bias
        attn = jax.nn.softmax(scores, axis=-1)
        out = jnp.einsum('bhqk,bkhd->bqhd', attn, v).reshape(b, s, H * DK)
        return out @ Wo

    def _L3_ffn_ref(inputs, Wg, bg, Wt, bt, W1, b1, W2, b2):
        import jax, jax.numpy as jnp
        import numpy as np
        MAX_THRESHOLD = 0.125
        x = inputs.reshape(-1, inputs.shape[-1])
        gate = jax.nn.softmax(x @ Wg + bg, axis=-1)
        thr = jax.nn.sigmoid(x @ Wt + bt) * MAX_THRESHOLD
        adapted = gate - thr
        mask = (adapted >= 0).astype(x.dtype)
        w = adapted * mask
        s = jnp.sum(w, axis=-1, keepdims=True)
        s = jnp.where(s == 0, jnp.ones_like(s), s)
        w = w / s
        h = jax.nn.gelu(jnp.einsum('td,edf->etf', x, W1) + b1[:, None, :])
        eo = jnp.einsum('etf,efd->etd', h, W2) + b2[:, None, :]
        out = jnp.einsum('te,etd->td', w, eo)
        return out.reshape(inputs.shape)
    x = L0_attn_x
    x = x + _L0_attn_ref(_layernorm(x, axis=-1), L0_attn_Wq, L0_attn_bq, L0_attn_Wk, L0_attn_bk, L0_attn_Wv, L0_attn_bv, L0_attn_W1, L0_attn_b1, L0_attn_W2, L0_attn_b2, L0_attn_W3, L0_attn_b3)
    x = x + _L0_ffn_ref(_layernorm(x, axis=-1), L0_ffn_router_w, L0_ffn_wv, L0_ffn_sv, L0_ffn_w, L0_ffn_s, L0_ffn_w1, L0_ffn_s1)
    x = x + _L1_attn_ref(_layernorm(x, axis=-1), L1_attn_Wq, L1_attn_bq, L1_attn_Wk, L1_attn_bk, L1_attn_Wv, L1_attn_bv, L1_attn_Wo, L1_attn_bo, L1_attn_Wfc, L1_attn_bfc, L1_attn_proj)
    x = x + _L1_ffn_ref(_layernorm(x, axis=-1), L1_ffn_Wr, L1_ffn_br, L1_ffn_W1, L1_ffn_b1, L1_ffn_W2, L1_ffn_b2)
    x = x + _L2_attn_ref(_layernorm(x, axis=-1), L2_attn_ln_w, L2_attn_ln_b, L2_attn_W_in, L2_attn_conv_w, L2_attn_conv_b, L2_attn_W_xproj, L2_attn_W_dt, L2_attn_b_dt, L2_attn_A_log, L2_attn_D_param, L2_attn_W_out)
    x = x + _L2_ffn_ref(_layernorm(x, axis=-1), L2_ffn_gate_w, L2_ffn_w1, L2_ffn_w2)
    x = x + _L3_attn_ref(_layernorm(x, axis=-1), L3_attn_Wq, L3_attn_Wk, L3_attn_Wv, L3_attn_Wo, L3_attn_rel_bias)
    x = x + _L3_ffn_ref(_layernorm(x, axis=-1), L3_ffn_Wg, L3_ffn_bg, L3_ffn_Wt, L3_ffn_bt, L3_ffn_W1, L3_ffn_b1, L3_ffn_W2, L3_ffn_b2)
    return x

_drawn_inputs = setup_inputs


def setup_inputs(seed=0):
    import zlib

    import numpy as np

    out = dict(_drawn_inputs(seed))
    spreads = {'L1_attn_bq': (0.0, 0.1),
     'L1_attn_bk': (0.0, 0.1),
     'L1_attn_bv': (0.0, 0.1),
     'L1_attn_bo': (0.0, 0.1),
     'L1_attn_bfc': (0.0, 0.1),
     'L1_ffn_br': (0.0, 0.1),
     'L1_ffn_b1': (0.0, 0.1),
     'L1_ffn_b2': (0.0, 0.1),
     'L2_attn_ln_w': (1.0, 0.2),
     'L2_attn_ln_b': (0.0, 0.1),
     'L2_attn_D_param': (1.0, 0.2),
     'L3_ffn_bg': (0.0, 0.1),
     'L3_ffn_b1': (0.0, 0.1),
     'L3_ffn_b2': (0.0, 0.1)}
    factors = {}
    for name, (base, spread) in spreads.items():
        noise = np.random.default_rng([zlib.crc32(name.encode()), seed]).standard_normal(out[name].shape)
        drawn = base * np.exp(spread * noise) if base else spread * noise
        out[name] = jnp.asarray(drawn.astype(out[name].dtype))
    for name, factor in factors.items():
        out[name] = (out[name] * factor).astype(out[name].dtype)
    return out
```

```python
from contextlib import ExitStack

import numpy as np

import concourse.bass as bass
import concourse.mybir as mybir

ALU = mybir.AluOpType
ACT = mybir.ActivationFunctionType
F32 = mybir.dt.float32
AX_X = mybir.AxisListType.X

P = 128
D = 128
B, S = 8, 512
TPS = S // P
NT = B * TPS
U = 2
LN_EPS = 1e-5
BANK = 512


class Chain:

    def __init__(self, eng, sem, per_turn=0, base=0):
        self.eng, self.sem, self.per_turn, self.turn, self.n, self.base = eng, sem, per_turn, 0, 0, base

    def start(self, turn):
        self.turn, self.n = turn, 0

    def link(self, ins):
        self.n += 1
        ins.then_inc(self.sem, 1)
        self.eng.wait_ge(self.sem, self.turn * self.per_turn + (self.n + self.base))

    def end(self):
        assert self.n == self.per_turn, (self.n, self.per_turn)


class Banks:

    def __init__(self, sem, name, order):
        self.place, self.uses = {}, {}
        for job, bank in order:
            self.place[job] = (bank, self.uses.get(bank, 0))
            self.uses[bank] = self.uses.get(bank, 0) + 1
        self.filled = {k: sem(f"{name}_bank{k}_filled") for k in self.uses}
        self.drained = {k: sem(f"{name}_bank{k}_drained") for k in self.uses}

    def open(self, eng):
        for k in self.uses:
            eng.sem_inc(self.drained[k], 1)

    def wait_drained(self, eng, job, turn):
        k, n = self.place[job]
        eng.wait_ge(self.drained[k], turn * self.uses[k] + (n + 1))

    def wait_filled(self, eng, job, turn):
        k, n = self.place[job]
        eng.wait_ge(self.filled[k], turn * self.uses[k] + (n + 1))

    def wait_read(self, eng, job, turn):
        k, n = self.place[job]
        eng.wait_ge(self.drained[k], turn * self.uses[k] + (n + 2))

    def fill(self, ins, job):
        ins.then_inc(self.filled[self.place[job][0]], 1)

    def drain(self, ins, job):
        ins.then_inc(self.drained[self.place[job][0]], 1)


class Signal:

    def __init__(self, sem, per_turn):
        self.sem, self.per_turn = sem, per_turn

    def by(self, ins):
        ins.then_inc(self.sem, 1)

    def wait(self, eng, turn, n):
        eng.wait_ge(self.sem, turn * self.per_turn + (n + 1))


class Chip:

    def __init__(self, nc, ctx):
        self.nc, self.ctx = nc, ctx
        self.x = self.sb(ctx, "x", [P, NT, D])
        self.ident = self.sb(ctx, "ident", [P, P])
        self.ones = self.sb(ctx, "ones", [P, P])
        self.ln_eps = self.sb(ctx, "ln_eps", [P, 1])
        self.apart_count = nc.alloc_semaphore(name="apart_count")
        self.counts = []
        self.psum = [ctx.enter_context(nc.psum_tensor(f"bank{k}", [P, BANK], F32)) for k in range(8)]

    def sb(self, ctx, name, shape, dt=F32):
        return ctx.enter_context(self.nc.sbuf_tensor(name, shape, dt))

    def apart(self, eng):
        eng.sem_inc(self.apart_count, 1)

    def sem(self, name):
        self.counts.append(self.nc.alloc_semaphore(name=name))
        return self.counts[-1]

    def end_layer(self):
        self.nc.clear_and_free_semaphores(self.counts)
        self.nc.all_engine_barrier()
        self.counts = []


def ln_statistics(chip, dve, chain, x_tile, stats, mv, n):
    for t in range(n):
        ins = dve.bn_stats(stats[:, t, :], x_tile(t))
    chain.link(ins)
    chip.apart(dve)
    for t in range(n):
        ins = dve.bn_aggr(mv[:, t, :], stats[:, t, :])
    return ins



def load_stage(chip, x_in, ident_in):
    nc = chip.nc
    loaded = chip.sem("x_loaded")
    with nc.Block() as block:
        @block.sync
        def _(sp):
            sp.dma_start(chip.ident[:], ident_in).then_inc(loaded, 16)
            xv = x_in.rearrange("b (t p) d -> p (b t) d", p=P)
            for c in range(2):
                h = NT // 2
                sp.dma_start(chip.x[:, c * h:(c + 1) * h, :], xv[:, c * h:(c + 1) * h, :]).then_inc(loaded, 16)
            sp.wait_ge(loaded, 48)

        @block.vector
        def _(dve):
            nc.vector.memset(chip.ones[:], 1.0)
            nc.vector.memset(chip.ln_eps[:], LN_EPS)


def store_stage(chip, out):
    nc = chip.nc
    stored = chip.sem("out_stored")
    with nc.Block() as block:
        @block.sync
        def _(sp):
            ov = out.rearrange("b (t p) d -> p (b t) d", p=P)
            for c in range(2):
                h = NT // 2
                sp.dma_start(ov[:, c * h:(c + 1) * h, :], chip.x[:, c * h:(c + 1) * h, :]).then_inc(stored, 16)
            sp.wait_ge(stored, 32)



def cosine_attention(chip, w):
    nc = chip.nc
    F = 512
    J = F // P
    QK, QKV = 2 * D, 3 * D
    ctx = ExitStack()
    with ctx:
        sb = lambda name, shape: chip.sb(ctx, f"l0a_{name}", shape)
        two = lambda name, shape: [sb(f"{name}{u}", shape) for u in range(U)]
        sem = lambda name: chip.sem(f"l0a_{name}")
        w_qkv, b_qkv = sb("w_qkv", [P, QKV]), sb("b_qkv", [P, QKV])
        w1, w2, w3 = sb("w1", [P, D]), sb("w2", [P, F]), sb("w3", [P, J, D])
        b1, b2, b3 = sb("b1", [P, 1]), sb("b2", [P, J]), sb("b3", [P, D])
        stats, mv = two("stats", [P, TPS, 6]), two("mv", [P, TPS, 2])
        std, rstd = two("std", [P, TPS]), two("rstd", [P, TPS])
        xn, xnT = two("xn", [P, TPS, D]), two("xnT", [P, S])
        qkv = two("qkv", [P, TPS, QKV + 1])
        sq, ss = two("sq", [P, TPS, 2, D]), two("ss", [P, TPS, 2])
        length, inv = two("length", [P, TPS, 2]), two("inv", [P, TPS, 2])
        qk = two("qk", [P, TPS, 2, D])
        qT, kT = two("qT", [P, S]), two("kT", [P, S])
        E, rden = two("E", [P, TPS, S]), two("rden", [P, TPS])
        o, oT = two("o", [P, TPS, D]), two("oT", [P, S])
        h1, h2 = two("h1", [P, S]), two("h2", [P, J, S])
        y = two("y", [P, TPS, D])

        order = [(("xT", u), 6 + u) for u in range(U)]
        order += [(("qkv", u, t), 4 + t % 2) for u in range(U) for t in range(TPS)]
        order += [((n, u), k) for u in range(U) for n, k in (("qT", 6), ("kT", 7))]
        order += [(("s", u, t), t) for u in range(U) for t in range(TPS)]
        order += [(("av", u, t), 4 + t % 2) for u in range(U) for t in range(TPS)]
        order += [(("oT", u), 6 + u) for u in range(U)]
        order += [(("h1", u), 6 + u) for u in range(U)]
        order += [(("h2", u, j), j) for u in range(U) for j in range(J)]
        order += [(("y", u), 4 + u) for u in range(U)]
        bk = Banks(sem, "psum", order)
        ps = lambda job: chip.psum[bk.place[job][0]]

        weights = sem("weights_loaded")
        WEIGHTS = 10
        step = lambda name, n=1: Signal(sem(name), U * n)
        mv_ready, std_ready, xn_ready, xnT_ready = step("mv_ready"), step("std_ready"), step("xn_ready"), step("xnT_ready")
        ss_ready, length_ready, qk_ready, qkT_ready = (step("ss_ready"), step("length_ready"), step("qk_ready"),
                                                       step("qkT_ready", 2))
        e_ready, o_ready, oT_ready = step("e_ready", TPS), step("o_ready"), step("oT_ready")
        h1_ready, h2_ready = step("h1_ready"), step("h2_ready", J)
        dve_order = sem("dve_order")
        TURNS = B // U

        def x_tile(i, u, t):
            return chip.x[:, bass.ds((i * U + u) * TPS + t, 1), :].rearrange("p a d -> p (a d)")

        with nc.Block() as block:
            @block.sync
            def _(sp):
                for n, nm in enumerate(["Wq", "Wk", "Wv"]):
                    sp.dma_start(w_qkv[:, n * D:(n + 1) * D], w[nm]).then_inc(weights, 16)
                    sp.dma_start(b_qkv[:, n * D:(n + 1) * D], w["b" + nm[1]].partition_broadcast(P)).then_inc(weights, 16)
                sp.dma_start(w1[:], w["W1"]).then_inc(weights, 16)
                sp.dma_start(w2[:], w["W2"]).then_inc(weights, 16)
                sp.dma_start(w3[:], w["W3"].rearrange("(j p) d -> p j d", p=P)).then_inc(weights, 16)
                sp.dma_start(b3[:], w["b3"].partition_broadcast(P)).then_inc(weights, 16)
                sp.dma_start(b1[:], w["b1"].rearrange("(p o) -> p o", o=1)).then_inc(weights, 16)
                with nc.allow_non_contiguous_dma(reason="a bias by partition"):
                    sp.dma_start(b2[:], w["b2"].rearrange("(j p) -> p j", p=P)).then_inc(weights, 16)

            @block.vector
            def _(dve):
                c = Chain(dve, dve_order, per_turn=U * 7)
                for u in range(U):
                    dve.memset(qkv[u][:, :, QKV:], 1.0)
                dve.wait_ge(weights, 16 * (WEIGHTS + 2))
                with dve.Fori(0, TURNS) as i:
                    c.start(i)
                    for u in range(U):
                        mv_ready.by(ln_statistics(chip, dve, c, lambda t: x_tile(i, u, t), stats[u], mv[u], TPS))
                    for u in range(U):
                        std_ready.wait(dve, i, u)
                        c.link(dve.reciprocal(rstd[u][:], std[u][:]))
                        for t in range(TPS):
                            ins = dve.tensor_scalar(xn[u][:, t, :], x_tile(i, u, t), mv[u][:, t, 0:1],
                                                    rstd[u][:, t:t + 1], ALU.subtract, ALU.mult)
                        xn_ready.by(ins)
                    for u in range(U):
                        for t in range(TPS):
                            bk.wait_filled(dve, ("qkv", u, t), i)
                            bk.drain(dve.tensor_tensor(qkv[u][:, t, 0:QKV], ps(("qkv", u, t))[:, 0:QKV], b_qkv[:],
                                                       ALU.add), ("qkv", u, t))
                        bk.wait_read(dve, ("qkv", u, TPS - 2), i)
                        bk.wait_read(dve, ("qkv", u, TPS - 1), i)
                        qk_in = qkv[u][:, :, 0:QK].rearrange("p t (n d) -> p t n d", n=2)
                        c.link(dve.tensor_tensor(sq[u][:], qk_in, qk_in, ALU.mult))
                        ss_ready.by(dve.tensor_reduce(ss[u][:], sq[u][:], AX_X, ALU.add))
                    for u in range(U):
                        length_ready.wait(dve, i, u)
                        c.link(dve.tensor_scalar(inv[u][:], length[u][:], 1e-12, None, ALU.max))
                        c.link(dve.reciprocal(inv[u][:], inv[u][:]))
                        for n in range(2):
                            ins = dve.tensor_tensor(qk[u][:, :, n, :], qkv[u][:, :, n * D:(n + 1) * D],
                                                    inv[u][:, :, n:n + 1].to_broadcast([P, TPS, D]), ALU.mult)
                        qk_ready.by(ins)
                    for u in range(U):
                        for t in range(TPS):
                            job = ("av", u, t)
                            bk.wait_filled(dve, job, i)
                            dve.tensor_copy(o[u][:, t, :], ps(job)[:, 0:D])
                            bk.drain(dve.tensor_copy(rden[u][:, t:t + 1], ps(job)[:, D:D + 1]), job)
                        bk.wait_read(dve, ("av", u, TPS - 2), i)
                        bk.wait_read(dve, ("av", u, TPS - 1), i)
                        c.link(dve.reciprocal(rden[u][:], rden[u][:]))
                        o_ready.by(dve.tensor_tensor(o[u][:], o[u][:],
                                                     rden[u][:].rearrange("p (t o) -> p t o", o=1).to_broadcast([P, TPS, D]), ALU.mult))
                    for u in range(U):
                        job = ("y", u)
                        bk.wait_filled(dve, job, i)
                        bk.drain(dve.tensor_tensor(y[u][:], ps(job)[:].rearrange("p (t d) -> p t d", t=TPS),
                                                   b3[:].rearrange("p (o d) -> p o d", o=1).to_broadcast([P, TPS, D]), ALU.add), job)
                        bk.wait_read(dve, job, i)
                        xs = chip.x[:, bass.ds((i * U + u) * TPS, TPS), :]
                        c.link(dve.tensor_tensor(xs, xs, y[u][:], ALU.add))
                c.end()

            @block.scalar
            def _(act):
                with act.Fori(0, TURNS) as i:
                    for u in range(U):
                        mv_ready.wait(act, i, u)
                        std_ready.by(act.activation(std[u][:], mv[u][:, :, 1], ACT.Sqrt, bias=chip.ln_eps[:]))
                    for u in range(U):
                        bk.wait_filled(act, ("xT", u), i)
                        ins = act.copy(xnT[u][:], ps(("xT", u))[:])
                        bk.drain(ins, ("xT", u))
                    for u in range(U):
                        ss_ready.wait(act, i, u)
                        length_ready.by(act.activation(length[u][:], ss[u][:], ACT.Sqrt))
                    for u in range(U):
                        for n, dst in (("qT", qT), ("kT", kT)):
                            bk.wait_filled(act, (n, u), i)
                            bk.drain(act.copy(dst[u][:], ps((n, u))[:]), (n, u))
                    for u in range(U):
                        for t in range(TPS):
                            bk.wait_filled(act, ("s", u, t), i)
                            bk.drain(act.activation(E[u][:, t, :], ps(("s", u, t))[:], ACT.Exp), ("s", u, t))
                    for u in range(U):
                        bk.wait_filled(act, ("oT", u), i)
                        bk.drain(act.copy(oT[u][:], ps(("oT", u))[:]), ("oT", u))
                    for u in range(U):
                        bk.wait_filled(act, ("h1", u), i)
                        bk.drain(act.activation(h1[u][:], ps(("h1", u))[:], ACT.Relu, bias=b1[:]), ("h1", u))
                    for u in range(U):
                        for j in range(J):
                            bk.wait_filled(act, ("h2", u, j), i)
                            bk.drain(act.activation(h2[u][:, j, :], ps(("h2", u, j))[:], ACT.Relu, bias=b2[:, j:j + 1]), ("h2", u, j))

            @block.tensor
            def _(pe):
                bk.open(pe)
                pe.wait_ge(weights, 16 * (WEIGHTS + 2))
                with pe.Fori(0, TURNS) as i:
                    for u in range(U):
                        xn_ready.wait(pe, i, u)
                        bk.wait_drained(pe, ("xT", u), i)
                        for t in range(TPS):
                            ins = pe.transpose(ps(("xT", u))[:, t * P:(t + 1) * P], xn[u][:, t, :], chip.ident[:])
                        bk.fill(ins, ("xT", u))
                    for u in range(U):
                        bk.wait_read(pe, ("xT", u), i)
                        for t in range(TPS):
                            job = ("qkv", u, t)
                            bk.wait_drained(pe, job, i)
                            bk.fill(pe.matmul(ps(job)[:, 0:QKV], xnT[u][:, t * P:(t + 1) * P], w_qkv[:], start=True, stop=True), job)
                    for u in range(U):
                        qk_ready.wait(pe, i, u)
                        for n, nm in enumerate(("qT", "kT")):
                            bk.wait_drained(pe, (nm, u), i)
                            for t in range(TPS):
                                ins = pe.transpose(ps((nm, u))[:, t * P:(t + 1) * P], qk[u][:, t, n, :], chip.ident[:])
                            bk.fill(ins, (nm, u))
                    for u in range(U):
                        bk.wait_read(pe, ("qT", u), i)
                        bk.wait_read(pe, ("kT", u), i)
                        for t in range(TPS):
                            job = ("s", u, t)
                            bk.wait_drained(pe, job, i)
                            bk.fill(pe.matmul(ps(job)[:], kT[u][:, t * P:(t + 1) * P], qT[u][:], start=True, stop=True), job)
                    for u in range(U):
                        for t in range(TPS):
                            bk.wait_read(pe, ("s", u, t), i)
                        for t in range(TPS):
                            job = ("av", u, t)
                            bk.wait_drained(pe, job, i)
                            for k in range(TPS):
                                ins = pe.matmul(ps(job)[:, 0:D + 1], E[u][:, k, t * P:(t + 1) * P], qkv[u][:, k, QK:],
                                                start=(k == 0), stop=(k == TPS - 1))
                            bk.fill(ins, job)
                    for u in range(U):
                        o_ready.wait(pe, i, u)
                        bk.wait_drained(pe, ("oT", u), i)
                        for t in range(TPS):
                            ins = pe.transpose(ps(("oT", u))[:, t * P:(t + 1) * P], o[u][:, t, :], chip.ident[:])
                        bk.fill(ins, ("oT", u))
                    for u in range(U):
                        bk.wait_read(pe, ("oT", u), i)
                        bk.wait_drained(pe, ("h1", u), i)
                        bk.fill(pe.matmul(ps(("h1", u))[:], w1[:], oT[u][:], start=True, stop=True), ("h1", u))
                    for u in range(U):
                        bk.wait_read(pe, ("h1", u), i)
                        for j in range(J):
                            bk.wait_drained(pe, ("h2", u, j), i)
                            bk.fill(pe.matmul(ps(("h2", u, j))[:], w2[:, j * P:(j + 1) * P], h1[u][:], start=True, stop=True), ("h2", u, j))
                    for u in range(U):
                        job = ("y", u)
                        for j in range(J):
                            bk.wait_read(pe, ("h2", u, j), i)
                        bk.wait_drained(pe, job, i)
                        for t in range(TPS):
                            for j in range(J):
                                ins = pe.matmul(ps(job)[:, t * D:(t + 1) * D], h2[u][:, j, t * P:(t + 1) * P], w3[:, j, :],
                                                start=(j == 0), stop=(j == J - 1))
                        bk.fill(ins, job)



E8 = 8
F = 512
J = F // P


def seq_tiles(ap, i, u):
    return ap[:, bass.ds((i * U + u) * TPS, TPS), :]


def one_tile(ap, i, u, t):
    return ap[:, bass.ds((i * U + u) * TPS + t, 1), :].rearrange("p a d -> p (a d)")


def normalise_and_route(chip, ctx, L, w_router, vectors):
    nc = chip.nc
    NR = w_router.shape[1] if w_router is not None else 0
    loads = bool(NR) + len(vectors)
    xnT_all = chip.sb(ctx, f"{L}_xnT_all", [P, NT * P])
    cols = {n: chip.sb(ctx, f"{L}_{n}", [P, E8 * J]) for n in vectors}
    with ExitStack() as inner:
        sb = lambda name, shape: chip.sb(inner, f"{L}r_{name}", shape)
        two = lambda name, shape: [sb(f"{name}{u}", shape) for u in range(U)]
        sem = lambda name: chip.sem(f"{L}r_{name}")
        step = lambda name, n=1: Signal(sem(name), U * n)
        router = sb("router", [P, NR]) if NR else None
        rows = {n: sb(f"rows_{n}", [E8 * J, P]) for n in vectors}
        stats, mv = two("stats", [P, TPS, 6]), two("mv", [P, TPS, 2])
        std, rstd = two("std", [P, TPS]), two("rstd", [P, TPS])
        xn, xnT = two("xn", [P, TPS, D]), two("xnT", [P, S])
        bk = Banks(sem, "psum", [(("xT", u), 6 + u) for u in range(U)])
        ps = lambda job: chip.psum[bk.place[job][0]]
        loaded, cols_filled = sem("loaded"), sem("cols_filled")
        mv_ready, std_ready, xn_ready = step("mv_ready"), step("std_ready"), step("xn_ready")
        routed, copied = step("routed"), step("copied")
        dve_order = sem("dve_order")
        TURNS = B // U
        with nc.Block() as block:
            @block.sync
            def _(sp):
                if NR:
                    sp.dma_start(router[:], w_router).then_inc(loaded, 16)
                for n, v in vectors.items():
                    sp.dma_start(rows[n][:], v).then_inc(loaded, 16)

            @block.vector
            def _(dve):
                c = Chain(dve, dve_order, per_turn=U * 2)
                with dve.Fori(0, TURNS) as i:
                    c.start(i)
                    for u in range(U):
                        mv_ready.by(ln_statistics(chip, dve, c, lambda t: one_tile(chip.x, i, u, t), stats[u], mv[u], TPS))
                    for u in range(U):
                        std_ready.wait(dve, i, u)
                        c.link(dve.reciprocal(rstd[u][:], std[u][:]))
                        for t in range(TPS):
                            ins = dve.tensor_scalar(xn[u][:, t, :], one_tile(chip.x, i, u, t), mv[u][:, t, 0:1],
                                                    rstd[u][:, t:t + 1], ALU.subtract, ALU.mult)
                        xn_ready.by(ins)
                c.end()
                if vectors:
                    dve.wait_ge(cols_filled, 1)
                for n, v in enumerate(vectors):
                    dve.tensor_copy(cols[v][:], chip.psum[1][:, n * E8 * J:(n + 1) * E8 * J])

            @block.scalar
            def _(act):
                with act.Fori(0, TURNS) as i:
                    for u in range(U):
                        mv_ready.wait(act, i, u)
                        std_ready.by(act.activation(std[u][:], mv[u][:, :, 1], ACT.Sqrt, bias=chip.ln_eps[:]))
                    for u in range(U):
                        bk.wait_filled(act, ("xT", u), i)
                        bk.drain(act.copy(xnT[u][:], ps(("xT", u))[:]), ("xT", u))

            @block.gpsimd
            def _(pool):
                with pool.Fori(0, TURNS) as i:
                    for u in range(U):
                        bk.wait_read(pool, ("xT", u), i)
                        copied.by(pool.tensor_copy(xnT_all[:, bass.ds((i * U + u) * S, S)], xnT[u][:]))

            @block.tensor
            def _(pe):
                bk.open(pe)
                pe.sem_inc(copied.sem, U)
                if loads:
                    pe.wait_ge(loaded, 16 * loads)
                for n, v in enumerate(vectors):
                    ins = pe.transpose(chip.psum[1][:, n * E8 * J:(n + 1) * E8 * J], rows[v][:], chip.ident[0:E8 * J, 0:E8 * J])
                if vectors:
                    ins.then_inc(cols_filled, 1)
                with pe.Fori(0, TURNS) as i:
                    for u in range(U):
                        xn_ready.wait(pe, i, u)
                        copied.wait(pe, i, u)
                        bk.wait_drained(pe, ("xT", u), i)
                        for t in range(TPS):
                            ins = pe.transpose(ps(("xT", u))[:, t * P:(t + 1) * P], xn[u][:, t, :], chip.ident[:])
                        bk.fill(ins, ("xT", u))
                    for u in range(U if NR else 0):
                        bk.wait_read(pe, ("xT", u), i)
                        for t in range(TPS):
                            ins = pe.matmul(chip.psum[0][:, bass.ds(((i * U + u) * TPS + t) * NR, NR)],
                                            xnT[u][:, t * P:(t + 1) * P], router[:], start=True, stop=True)
                        routed.by(ins)
    return xnT_all, cols


def bcast(ap2, n_before=None, n_after=None):
    m = ap2.shape[1]
    if n_before:
        return ap2.rearrange("p (o m) -> p o m", o=1).to_broadcast([ap2.shape[0], n_before, m])
    return ap2.rearrange("p (m o) -> p m o", o=1).to_broadcast([ap2.shape[0], m, n_after])


def softmax_of_experts(chip, ctx, L, NR, bias, finish):
    pass


def route(chip, ctx, L, NR, bias, top=None, capacity=None, threshold=False, b2=None):
    nc = chip.nc
    gates = chip.sb(ctx, f"{L}_gates", [P, NT, E8])
    with ExitStack() as inner:
        sb = lambda name, shape, dt=F32: chip.sb(inner, f"{L}g_{name}", shape, dt)
        sem = lambda name: chip.sem(f"{L}g_{name}")
        logits, ex = sb("logits", [P, NT, NR]), sb("ex", [P, NT, E8])
        red, a, b = sb("red", [P, NT]), sb("a", [P, NT, E8]), sb("b", [P, NT, E8])
        probs = sb("probs", [P, NT, E8])
        bias_all = sb("bias_all", [P, NR])
        order8 = sb("order8", [P, E8])
        dve_order, shifted, exp_done, loaded = sem("dve_order"), sem("shifted"), sem("exp_done"), sem("loaded")
        turned, used, back, backed = sem("turned"), sem("used"), sem("back"), sem("backed")
        if capacity:
            R = B * E8
            rows, left, sel = sb("rows", [R, S]), sb("left", [R, S]), sb("sel", [R, S])
            best = sb("best", [R, 8])
            by_place = sb("by_place", [P, TPS, R])
        if b2 is not None:
            gT, b2_rows, z = sb("gT", [E8, B, S]), sb("b2_rows", [E8, D]), sb("z", [P, NT, D])
        per_e = lambda r: bcast(r[:], n_after=E8)
        with nc.Block() as block:
            @block.sync
            def _(sp):
                if bias is not None:
                    sp.dma_start(bias_all[:], bias.partition_broadcast(P)).then_inc(loaded, 16)
                if b2 is not None:
                    sp.dma_start(b2_rows[:], b2).then_inc(loaded, 16)

            @block.vector
            def _(dve):
                c = Chain(dve, dve_order)
                raw = chip.psum[0][:, 0:NT * NR].rearrange("p (t e) -> p t e", e=NR)
                if bias is not None:
                    dve.wait_ge(loaded, 16 * (1 + (b2 is not None)))
                    c.link(dve.tensor_tensor(logits[:], raw, bcast(bias_all[:], n_before=NT), ALU.add))
                else:
                    c.link(dve.tensor_copy(logits[:], raw))
                c.link(dve.tensor_reduce(red[:], logits[:, :, 0:E8], AX_X, ALU.max))
                dve.tensor_tensor(a[:], logits[:, :, 0:E8], per_e(red), ALU.subtract).then_inc(shifted, 1)
                dve.wait_ge(exp_done, 1)
                c.link(dve.tensor_reduce(red[:], ex[:], AX_X, ALU.add))
                c.link(dve.reciprocal(red[:], red[:]))
                c.link(dve.tensor_tensor(probs[:], ex[:], per_e(red), ALU.mult))
                if top:
                    for e in range(E8):
                        ins = dve.memset(order8[:, e:e + 1], float(E8 - e))
                    c.link(ins)
                    c.link(dve.tensor_copy(b[:], probs[:]))
                    for k in range(top):
                        c.link(dve.tensor_reduce(red[:], b[:], AX_X, ALU.max))
                        c.link(dve.tensor_tensor(a[:], b[:], per_e(red), ALU.is_equal))
                        c.link(dve.tensor_tensor(a[:], a[:], bcast(order8[:], n_before=NT), ALU.mult))
                        c.link(dve.tensor_reduce(red[:], a[:], AX_X, ALU.max))
                        c.link(dve.tensor_tensor(a[:], a[:], per_e(red), ALU.is_equal))
                        c.link(dve.scalar_tensor_tensor(b[:], a[:], -4.0, b[:], ALU.mult, ALU.add))
                    c.link(dve.tensor_scalar(a[:], b[:], -1.0, None, ALU.is_lt))
                    c.link(dve.tensor_tensor(gates[:], probs[:], a[:], ALU.mult))
                if threshold:
                    thr = logits[:, :, E8]
                    dve.wait_ge(exp_done, 2)
                    c.link(dve.tensor_scalar(red[:], thr, 0.125, None, ALU.mult))
                    c.link(dve.tensor_tensor(a[:], probs[:], per_e(red), ALU.subtract))
                    c.link(dve.tensor_scalar(b[:], a[:], 0.0, None, ALU.max))
                    c.link(dve.tensor_reduce(red[:], b[:], AX_X, ALU.add))
                    c.link(dve.scalar_tensor_tensor(red[:], red[:], 0.0, red[:], ALU.is_equal, ALU.add))
                    c.link(dve.reciprocal(red[:], red[:]))
                    c.link(dve.tensor_tensor(gates[:], b[:], per_e(red), ALU.mult))
                if capacity:
                    for t in range(TPS):
                        ins = dve.tensor_copy(by_place[:, t, :].rearrange("p (b e) -> p b e", e=E8),
                                              probs[:].rearrange("p (b t) e -> p b t e", t=TPS)[:, :, t, :])
                    c.link(ins)
                dve.sem_inc(turned, 1)
                if capacity:
                    dve.wait_ge(used, 1)
                    c.link(dve.tensor_copy(rows[:], chip.psum[1][0:R, :]))
                    c.link(dve.tensor_copy(left[:], rows[:]))
                    for k in range(capacity // 8):
                        c.link(dve.max(best[:], left[:]))
                        c.link(dve.match_replace(left[:], best[:], left[:], -1.0))
                    c.link(dve.scalar_tensor_tensor(sel[:], left[:], 0.0, rows[:], ALU.is_lt, ALU.mult))
                    dve.sem_inc(back, 1)
                    dve.wait_ge(backed, 1)
                    gv = gates[:].rearrange("p (b t) e -> p b t e", t=TPS)
                    for t in range(TPS):
                        dve.tensor_copy(gv[:, :, t, :], chip.psum[2][:, t * R:(t + 1) * R].rearrange("p (b e) -> p b e", e=E8))
                if b2 is not None:
                    for q in range(B):
                        dve.wait_ge(used, q + 1)
                        dve.tensor_copy(gT[:, q, :], chip.psum[q][0:E8, :]).then_inc(back, 1)
                    for q in range(B):
                        dve.wait_ge(backed, q + 1)
                        xs = chip.x[:, q * TPS:(q + 1) * TPS, :]
                        dve.tensor_tensor(xs, chip.psum[q][:].rearrange("p (t d) -> p t d", d=D), xs, ALU.add)

            @block.scalar
            def _(act):
                act.wait_ge(shifted, 1)
                act.activation(ex[:], a[:], ACT.Exp).then_inc(exp_done, 1)
                if threshold:
                    act.activation(logits[:, :, E8], logits[:, :, E8], ACT.Sigmoid).then_inc(exp_done, 1)

            @block.tensor
            def _(pe):
                pe.wait_ge(turned, 1)
                if capacity:
                    for t in range(TPS):
                        ins = pe.transpose(chip.psum[1][0:R, t * P:(t + 1) * P], by_place[:, t, :], chip.ident[:])
                    ins.then_inc(used, 1)
                    pe.wait_ge(back, 1)
                    for t in range(TPS):
                        ins = pe.transpose(chip.psum[2][:, t * R:(t + 1) * R], sel[:, t * P:(t + 1) * P], chip.ident[0:R, 0:R])
                    ins.then_inc(backed, 1)
                if b2 is not None:
                    for q in range(B):
                        for t in range(TPS):
                            ins = pe.transpose(chip.psum[q][0:E8, t * P:(t + 1) * P], gates[:, q * TPS + t, :], chip.ident[:])
                        ins.then_inc(used, 1)
                    for q in range(B):
                        pe.wait_ge(back, q + 1)
                        for t in range(TPS):
                            ins = pe.matmul(chip.psum[q][:, t * D:(t + 1) * D], gT[:, q, t * P:(t + 1) * P], b2_rows[:],
                                            start=True, stop=True)
                        ins.then_inc(backed, 1)
    return gates


def dense_experts(chip, L, xnT_all, gates, w_in, w_out, act_fn, b1=None, glu=None):
    nc = chip.nc
    CU = 2
    CT = B // CU
    with ExitStack() as ctx:
        sb = lambda name, shape: chip.sb(ctx, f"{L}e_{name}", shape)
        two = lambda name, shape: [sb(f"{name}{u}", shape) for u in range(2)]
        sem = lambda name: chip.sem(f"{L}e_{name}")
        w1, w2 = two("w1", [P, F]), two("w2", [P, J, D])
        h = two("h", [P, J, S])
        if glu:
            w_v, s_v, s_in, s_out = glu
            wv, so, w2s, g = two("wv", [P, F]), two("so", [P, D]), two("w2s", [P, J, D]), two("g", [P, J, S])
            order = [((n, u, j), base + (u * J + j) % 3) for u in range(2) for j in range(J) for n, base in (("h", 0), ("v", 3))]
        else:
            w2s = w2
            order = [(("h", u, j), j) for u in range(2) for j in range(J)]
        order += [(("y", u), 6 + u) for u in range(2)]
        bk = Banks(sem, "psum", order)
        ps = lambda job: chip.psum[bk.place[job][0]]
        loaded = [sem(f"weights_loaded{u}") for u in range(2)]
        scaled = sem("w_out_scaled")
        g_ready, h_read = sem("g_ready"), None
        NW = 2 + 2 * bool(glu)

        def load(sp, e, eh):
            one = lambda w: w[bass.ds(e, 1)]
            sp.dma_start(w1[eh][:], one(w_in).rearrange("e k f -> (e k) f")).then_inc(loaded[eh], 16)
            sp.dma_start(w2[eh][:], one(w_out).rearrange("e (j p) d -> p (e j) d", p=P)).then_inc(loaded[eh], 16)
            if glu:
                sp.dma_start(wv[eh][:], one(w_v).rearrange("e k f -> (e k) f")).then_inc(loaded[eh], 16)
                sp.dma_start(so[eh][:], one(s_out).rearrange("e o d -> (e o) d").partition_broadcast(P)
                             if False else s_out[bass.ds(e, 1)].rearrange("e o d -> (e o d)").partition_broadcast(P)).then_inc(loaded[eh], 16)

        with nc.Block() as block:
            @block.sync
            def _(sp):
                for eh in range(2):
                    load(sp, eh, eh)
                with sp.Fori(1, E8 // 2) as ep:
                    for eh in range(2):
                        bk.wait_filled(sp, ("y", 1), ((ep - 1) * 2 + eh) * CT + (CT - 1))
                        load(sp, ep * 2 + eh, eh)

            if glu:
                @block.gpsimd
                def _(pool):
                    with pool.Fori(0, E8 // 2) as ep:
                        for eh in range(2):
                            pool.wait_ge(loaded[eh], (ep + 1) * (16 * NW))
                            pool.tensor_tensor(w2s[eh][:], w2[eh][:], bcast(so[eh][:], n_before=J), ALU.mult).then_inc(scaled, 1)

            @block.scalar
            def _(act):
                with act.Fori(0, E8 // 2) as ep:
                    for eh in range(2):
                        with act.Fori(0, CT) as cp:
                            turn = (ep * 2 + eh) * CT + cp
                            for u in range(2):
                                for j in range(J):
                                    job = ("h", u, j)
                                    bk.wait_filled(act, job, turn)
                                    chip.apart(act)
                                    col = bass.ds((ep * 2 + eh) * J + j, 1)
                                    kw = {"bias": b1[:, col]} if b1 is not None else {}
                                    if glu:
                                        kw["scale"] = s_in[:, col]
                                    dst = g if glu else h
                                    bk.drain(act.activation(dst[u][:, j, :], ps(job)[:], act_fn, **kw), job)

            @block.vector
            def _(dve):
                with dve.Fori(0, E8 // 2) as ep:
                    for eh in range(2):
                        e = ep * 2 + eh
                        with dve.Fori(0, CT) as cp:
                            turn = e * CT + cp
                            if glu:
                                for u in range(2):
                                    for j in range(J):
                                        bk.wait_filled(dve, ("v", u, j), turn)
                                        bk.wait_read(dve, ("h", u, j), turn)
                                        bk.drain(dve.scalar_tensor_tensor(h[u][:, j, :], ps(("v", u, j))[:],
                                                                          s_v[:, bass.ds(e * J + j, 1)], g[u][:, j, :],
                                                                          ALU.mult, ALU.mult), ("v", u, j))
                            for u in range(2):
                                bk.wait_filled(dve, ("y", u), turn)
                                for t in range(TPS):
                                    tile = (cp * CU + u) * TPS + t
                                    xs = chip.x[:, bass.ds(tile, 1), :].rearrange("p a d -> p (a d)")
                                    gate = gates[:, bass.ds(tile, 1), bass.ds(e, 1)].rearrange("p a e -> p (a e)")
                                    ins = dve.scalar_tensor_tensor(xs, ps(("y", u))[:, t * D:(t + 1) * D], gate, xs,
                                                                   ALU.mult, ALU.add)
                                bk.drain(ins, ("y", u))

            @block.tensor
            def _(pe):
                bk.open(pe)
                with pe.Fori(0, E8 // 2) as ep:
                    for eh in range(2):
                        pe.wait_ge(loaded[eh], (ep + 1) * (16 * NW))
                        if glu:
                            pe.wait_ge(scaled, ep * 2 + (eh + 1))
                        chip.apart(pe)
                        with pe.Fori(0, CT) as cp:
                            turn = (ep * 2 + eh) * CT + cp
                            for u in range(2):
                                rhs = xnT_all[:, bass.ds((cp * CU + u) * S, S)]
                                for j in range(J):
                                    for n, w in (("h", w1),) + ((("v", wv),) if glu else ()):
                                        bk.wait_drained(pe, (n, u, j), turn)
                                        bk.fill(pe.matmul(ps((n, u, j))[:], w[eh][:, j * P:(j + 1) * P], rhs,
                                                          start=True, stop=True), (n, u, j))
                            for u in range(2):
                                for j in range(J):
                                    bk.wait_read(pe, ("v" if glu else "h", u, j), turn)
                                bk.wait_drained(pe, ("y", u), turn)
                                for t in range(TPS):
                                    for j in range(J):
                                        ins = pe.matmul(ps(("y", u))[:, t * D:(t + 1) * D], h[u][:, j, t * P:(t + 1) * P],
                                                        w2s[eh][:, j, :], start=(j == 0), stop=(j == J - 1))
                                bk.fill(ins, ("y", u))


def by_tile(ap):
    return ap.rearrange("e (j p) -> (e j) p", p=P)


def top2_glu_experts(chip, w):
    with ExitStack() as ctx:
        flat = lambda a: a.rearrange("e o f -> (e o) f")
        xnT, cols = normalise_and_route(chip, ctx, "l0f", w["router_w"], {"sv": by_tile(flat(w["sv"])), "s": by_tile(flat(w["s"]))})
        gates = route(chip, ctx, "l0f", E8, None, top=2)
        dense_experts(chip, "l0f", xnT, gates, w["w"], w["w1"], ACT.Gelu_apprx_tanh, glu=(w["wv"], cols["sv"], cols["s"], w["s1"]))


def switch_experts(chip, w):
    with ExitStack() as ctx:
        xnT, cols = normalise_and_route(chip, ctx, "l1f", w["Wr"], {"b1": by_tile(w["b1"])})
        gates = route(chip, ctx, "l1f", E8, w["br"], top=1, b2=w["b2"])
        dense_experts(chip, "l1f", xnT, gates, w["W1"], w["W2"], ACT.Relu, b1=cols["b1"])


def expert_choice_experts(chip, w):
    with ExitStack() as ctx:
        xnT, _ = normalise_and_route(chip, ctx, "l2f", w["gate_w"], {})
        gates = route(chip, ctx, "l2f", E8, None, capacity=2 * S // E8)
        dense_experts(chip, "l2f", xnT, gates, w["w1"], w["w2"], ACT.Gelu)


def threshold_experts(chip, w):
    with ExitStack() as ctx:
        xnT, cols = normalise_and_route(chip, ctx, "l3f", w["Wgt"], {"b1": by_tile(w["b1"])})
        gates = route(chip, ctx, "l3f", E8 + 1, w["bgt"], threshold=True, b2=w["b2"])
        dense_experts(chip, "l3f", xnT, gates, w["W1"], w["W2"], ACT.Gelu_apprx_tanh, b1=cols["b1"])


def normalise_all(chip, ctx, L):
    return normalise_and_route(chip, ctx, L, None, {})[0]



H3, DK3 = 16, 64
BUCKETS = 32


def relative_position_attention(chip, w):
    nc = chip.nc
    HP = H3 // 2
    SPAN = 2 * S - 1
    GW = S + (TPS - 1) * P
    SCALE = float(H3) ** -0.5
    OP = F32
    ctx = ExitStack()
    with ctx:
        sb = lambda name, shape: chip.sb(ctx, f"l3a_{name}", shape)
        two = lambda name, shape: [sb(f"{name}{u}", shape) for u in range(2)]
        sem = lambda name: chip.sem(f"l3a_{name}")
        xnT_all = normalise_all(chip, ctx, "l3a")
        by_distance = nc.dram_tensor("l3a_by_distance", (H3, SPAN + 1), F32, kind="Internal").ap()

        by_place = nc.dram_tensor("l3a_by_place", (H3, P, SPAN + 1), F32, kind="Internal").ap()

        with ExitStack() as inner, nc.Block() as block:
            table = chip.sb(inner, "l3a_table", [BUCKETS, H3])
            onehot = chip.sb(inner, "l3a_onehot", [BUCKETS, SPAN + 1])
            line = chip.sb(inner, "l3a_line", [H3, SPAN + 1])
            loaded, summed, lined, stored = sem("table_loaded"), sem("summed"), sem("lined"), sem("line_stored")

            @block.sync
            def _(sp):
                sp.dma_start(table[:], w["rel_bias"]).then_inc(loaded, 16)
                sp.dma_start(onehot[:], w["onehot"]).then_inc(loaded, 16)
                sp.wait_ge(lined, 2)
                sp.dma_start(by_distance, line[:]).then_inc(stored, 16)
                sp.wait_ge(stored, 16)
                for h in range(H3):
                    src = bass.AP(by_distance.tensor, h * (SPAN + 1), [[0, P], [1, SPAN + 1]])
                    sp.dma_start(by_place[h], src).then_inc(stored, 16)
                sp.wait_ge(stored, 16 * (1 + H3))

            @block.tensor
            def _(pe):
                pe.wait_ge(loaded, 32)
                for c in range(2):
                    pe.matmul(chip.psum[c][0:H3, :], table[:], onehot[:, c * S:(c + 1) * S], start=True, stop=True).then_inc(summed, 1)

            @block.vector
            def _(dve):
                for c in range(2):
                    dve.wait_ge(summed, c + 1)
                    dve.tensor_copy(line[:, c * S:(c + 1) * S], chip.psum[c][0:H3, :]).then_inc(lined, 1)

        wq, wk, wv, wo = two("wq", [P, P]), two("wk", [P, P]), two("wv", [P, P]), two("wo", [P, D])
        bias = two("bias", [P, 2, GW])
        xT = two("xT", [P, S])
        qT, kT = two("qT", [P, S]), two("kT", [P, S])
        v = two("v", [P, TPS, 2, DK3 + 1])
        NSC = 4
        sc = [sb(f"sc{n}", [P, TPS, S]) for n in range(2)]
        top = [sb(f"top{n}", [P, TPS]) for n in range(2)]
        pT = [sb(f"pT{n}", [P, TPS, S]) for n in range(2)]
        rden = two("rden", [P, TPS, 2])
        o, oT = two("o", [P, TPS, P]), two("oT", [P, S])

        order = []
        for u in range(2):
            order += [(("q", u), 4), (("k", u), 4), (("v", u), 5)]
        for u in range(2):
            for hh in range(2):
                order += [(("s", u, hh, t), t % 2) for t in range(TPS)]
                order += [(("t", u, hh, t), 2 + t % 2) for t in range(TPS)]
                order += [(("av", u, hh), 6 + hh)]
        for u in range(2):
            order += [(("oT", u), 4), (("y", u), 5)]
        bk = Banks(sem, "psum", order)
        ps = lambda job: chip.psum[bk.place[job][0]]
        loaded = [sem(f"weights_loaded{u}") for u in range(2)]
        step = lambda name, n=1: Signal(sem(name), 2 * n)
        xT_ready, top_ready, less_ready, o_ready = step("xT_ready"), step("top_ready", 2), step("less_ready", 2), step("o_ready")
        dve_order = sem("dve_order")
        NW = 5 + 1
        CT = B // 2
        heads = [(u, hh) for u in range(2) for hh in range(2)]

        def load(sp, hp, hh):
            cols = bass.ds(hp * P, P)
            sp.dma_start(wq[hh][:], w["Wq"][:, cols]).then_inc(loaded[hh], 16)
            sp.dma_start(wk[hh][:], w["Wk"][:, cols]).then_inc(loaded[hh], 16)
            sp.dma_start(wv[hh][:], w["Wv"][:, cols]).then_inc(loaded[hh], 16)
            sp.dma_start(wo[hh][:], w["Wo"][cols, :]).then_inc(loaded[hh], 16)
            for n in range(2):
                src = bass.AP(by_place.tensor, (hp * 2 + n) * (P * (SPAN + 1)) + (P - 1), [[SPAN, P], [1, GW]])
                sp.dma_start(bias[hh][:, n, :], src).then_inc(loaded[hh], 16)

        with nc.Block() as block:
            @block.sync
            def _(sp):
                for hh in range(2):
                    load(sp, hh, hh)
                with sp.Fori(1, HP // 2) as pp:
                    for hh in range(2):
                        turn = ((pp - 1) * 2 + hh) * CT + (CT - 1)
                        bk.wait_read(sp, ("y", 1), turn)
                        load(sp, pp * 2 + hh, hh)

            @block.gpsimd
            def _(pool):
                with pool.Fori(0, HP // 2) as pp:
                    for wh in range(2):
                        with pool.Fori(0, CT) as cp:
                            turn = (pp * 2 + wh) * CT + cp
                            for u in range(2):
                                bk.wait_drained(pool, ("v", u), turn)
                                xT_ready.by(pool.tensor_copy(xT[u][:], xnT_all[:, bass.ds((cp * 2 + u) * S, S)]))

            @block.vector
            def _(dve):
                for u in range(2):
                    dve.memset(v[u][:, :, :, DK3:], 1.0)
                c = Chain(dve, dve_order, per_turn=2 * 2)

                def less_maximum(u, hh, wh, turn):
                    for t in range(TPS):
                        job = ("s", u, hh, t)
                        bk.wait_filled(dve, job, turn)
                        chip.apart(dve)
                        b0 = (TPS - 1 - t) * P
                        ins = dve.tensor_tensor_reduce(sc[hh][:, t, :], ps(job)[:], bias[wh][:, hh, b0:b0 + S], 1.0, -3.0e38,
                                                       ALU.add, ALU.max, top[hh][:, t:t + 1])
                        bk.drain(ins, job)
                    bk.wait_read(dve, ("s", u, hh, TPS - 2), turn)
                    bk.wait_read(dve, ("s", u, hh, TPS - 1), turn)
                    for t in range(TPS):
                        ins = dve.tensor_scalar(sc[hh][:, t, :], sc[hh][:, t, :], top[hh][:, t:t + 1], None, ALU.subtract)
                    less_ready.by(ins)

                def normalise(u, hh, c, turn):
                    job = ("av", u, hh)
                    bk.wait_filled(dve, job, turn)
                    a = ps(job)[:, 0:TPS * (DK3 + 1)].rearrange("p (t d) -> p t d", d=DK3 + 1)
                    c.link(dve.reciprocal(rden[u][:, :, hh:hh + 1], a[:, :, DK3:]))
                    ins = dve.tensor_tensor(o[u][:, :, hh * DK3:(hh + 1) * DK3], a[:, :, 0:DK3],
                                            rden[u][:, :, hh:hh + 1].to_broadcast([P, TPS, DK3]), ALU.mult)
                    bk.drain(ins, job)

                with dve.Fori(0, HP // 2) as pp:
                    for wh in range(2):
                        with dve.Fori(0, CT) as cp:
                            turn = (pp * 2 + wh) * CT + cp
                            c.start(turn)
                            for n in range(len(heads) + 2):
                                if n < len(heads):
                                    less_maximum(*heads[n], wh, turn)
                                if n >= 2:
                                    normalise(*heads[n - 2], c, turn)
                            for u in range(2):
                                job = ("y", u)
                                bk.wait_filled(dve, job, turn)
                                xs = chip.x[:, bass.ds((cp * 2 + u) * TPS, TPS), :]
                                bk.drain(dve.tensor_tensor(xs, ps(job)[:].rearrange("p (t d) -> p t d", t=TPS), xs, ALU.add), job)
                c.end()

            @block.scalar
            def _(act):
                with act.Fori(0, HP // 2) as pp:
                    for wh in range(2):
                        with act.Fori(0, CT) as cp:
                            turn = (pp * 2 + wh) * CT + cp
                            for u in range(2):
                                bk.wait_filled(act, ("q", u), turn)
                                bk.drain(act.mul(qT[u][:], ps(("q", u))[:], SCALE), ("q", u))
                                bk.wait_filled(act, ("k", u), turn)
                                bk.drain(act.copy(kT[u][:], ps(("k", u))[:]), ("k", u))
                                bk.wait_filled(act, ("v", u), turn)
                                for hh in range(2):
                                    ins = act.copy(v[u][:, :, hh, 0:DK3], ps(("v", u))[:].rearrange("p (t h d) -> p t h d", h=2, d=DK3)[:, :, hh, :])
                                bk.drain(ins, ("v", u))
                            for u in range(2):
                                for hh in range(2):
                                    for t in range(TPS):
                                        job = ("t", u, hh, t)
                                        bk.wait_filled(act, job, turn)
                                        bk.drain(act.activation(pT[hh][:, t, :], ps(job)[:], ACT.Exp), job)
                            for u in range(2):
                                bk.wait_filled(act, ("oT", u), turn)
                                bk.drain(act.copy(oT[u][:], ps(("oT", u))[:]), ("oT", u))

            @block.tensor
            def _(pe):
                bk.open(pe)

                def scores(u, hh, turn):
                    rows = slice(hh * DK3, (hh + 1) * DK3)
                    for t in range(TPS):
                        job = ("s", u, hh, t)
                        bk.wait_drained(pe, job, turn)
                        bk.fill(pe.matmul(ps(job)[:], qT[u][rows, t * P:(t + 1) * P], kT[u][rows, :], start=True, stop=True), job)

                def turn_scores(u, hh, turn):
                    less_ready.wait(pe, turn, u * 2 + hh)
                    for kt in range(TPS):
                        job = ("t", u, hh, kt)
                        bk.wait_drained(pe, job, turn)
                        for t in range(TPS):
                            ins = pe.transpose(ps(job)[:, t * P:(t + 1) * P], sc[hh][:, t, kt * P:(kt + 1) * P], chip.ident[:])
                        bk.fill(ins, job)

                def weigh(u, hh, turn):
                    job = ("av", u, hh)
                    bk.wait_drained(pe, job, turn)
                    bk.wait_read(pe, ("t", u, hh, TPS - 2), turn)
                    bk.wait_read(pe, ("t", u, hh, TPS - 1), turn)
                    for t in range(TPS):
                        for kt in range(TPS):
                            ins = pe.matmul(ps(job)[:, t * (DK3 + 1):(t + 1) * (DK3 + 1)], pT[hh][:, kt, t * P:(t + 1) * P],
                                            v[u][:, kt, hh, :], start=(kt == 0), stop=(kt == TPS - 1))
                    bk.fill(ins, job)

                with pe.Fori(0, HP // 2) as pp:
                    for wh in range(2):
                        pe.wait_ge(loaded[wh], (pp + 1) * (16 * NW))
                        chip.apart(pe)
                        with pe.Fori(0, CT) as cp:
                            turn = (pp * 2 + wh) * CT + cp
                            for u in range(2):
                                xT_ready.wait(pe, turn, u)
                                for nm, wt in (("q", wq), ("k", wk)):
                                    bk.wait_drained(pe, (nm, u), turn)
                                    bk.fill(pe.matmul(ps((nm, u))[:], wt[wh][:], xT[u][:], start=True, stop=True), (nm, u))
                                bk.wait_drained(pe, ("v", u), turn)
                                for t in range(TPS):
                                    ins = pe.matmul(ps(("v", u))[:, t * P:(t + 1) * P], xT[u][:, t * P:(t + 1) * P], wv[wh][:], start=True, stop=True)
                                bk.fill(ins, ("v", u))
                            for n, (u, hh) in enumerate(heads):
                                if hh == 0:
                                    bk.wait_read(pe, ("k", u), turn)
                                if n == 0:
                                    scores(u, hh, turn)
                                if n + 1 < len(heads):
                                    u2, hh2 = heads[n + 1]
                                    if hh2 == 0:
                                        bk.wait_read(pe, ("k", u2), turn)
                                    scores(u2, hh2, turn)
                                turn_scores(u, hh, turn)
                                bk.wait_read(pe, ("v", u), turn)
                                weigh(u, hh, turn)
                            for u in range(2):
                                for hh in range(2):
                                    bk.wait_read(pe, ("av", u, hh), turn)
                                bk.wait_drained(pe, ("oT", u), turn)
                                for t in range(TPS):
                                    ins = pe.transpose(ps(("oT", u))[:, t * P:(t + 1) * P], o[u][:, t, :], chip.ident[:])
                                bk.fill(ins, ("oT", u))
                                bk.wait_read(pe, ("oT", u), turn)
                                bk.wait_drained(pe, ("y", u), turn)
                                for t in range(TPS):
                                    ins = pe.matmul(ps(("y", u))[:, t * D:(t + 1) * D], oT[u][:, t * P:(t + 1) * P], wo[wh][:], start=True, stop=True)
                                bk.fill(ins, ("y", u))


def buckets_by_distance():
    half, exact = BUCKETS // 2, BUCKETS // 4
    hot = np.zeros((BUCKETS, 2 * S), np.float32)
    for n in range(2 * S - 1):
        far = abs(n - (S - 1))
        if far < exact:
            bucket = far
        else:
            bucket = exact
            while bucket < half - 1 and far * far >= exact * exact * 2 ** (bucket + 1 - exact):
                bucket += 1
        hot[bucket + half * (n > S - 1), n] = 1.0
    return hot



def feature_attention(chip, w):
    nc = chip.nc
    H, DH = 16, 8
    M = w["proj"].shape[1]
    HM = H * M
    NCH = HM // P
    HC = H // NCH
    DC = HC * DH
    CW = DC + HC
    DN = float(DH) ** -0.25
    RATIO = float(M) ** -0.5
    EPS = 1e-4
    HALF = TPS // 2
    ctx = ExitStack()
    with ctx:
        sb = lambda name, shape: chip.sb(ctx, f"l1a_{name}", shape)
        two = lambda name, shape: [sb(f"{name}{u}", shape) for u in range(U)]
        sem = lambda name: chip.sem(f"l1a_{name}")
        wq, wk, wv, wo, wfc = (sb(n, [P, D]) for n in ("wq", "wk", "wv", "wo", "wfc"))
        bq, bk_, bo = (sb(n, [P, 1]) for n in ("bq", "bk", "bo"))
        bv, bfc = sb("bv", [P, D]), sb("bfc", [P, D])
        proj, spread = sb("proj", [DH, M]), sb("spread", [DH, P])
        head_of, half_head, own = sb("head_of", [P, H]), sb("half_head", [P, H]), sb("own", [P, CW])
        feat = sb("feat", [P, H, M])
        stats, mv = two("stats", [P, TPS, 6]), two("mv", [P, TPS, 2])
        std, rstd = two("std", [P, TPS]), two("rstd", [P, TPS])
        xn, xnT = two("xn", [P, TPS, D]), two("xnT", [P, S])
        qk = [[sb(f"{n}{u}", [P, S]) for n in ("q", "k")] for u in range(U)]
        sqs = [[sb(f"{n}{u}", [P, S]) for n in ("qsq", "ksq")] for u in range(U)]
        v = two("v", [P, TPS, NCH, DC + 1])
        mq, mk = two("mq", [P, TPS, H]), two("mk", [P, TPS, H])
        dg, mkr = two("dg", [P, 2, TPS, H]), two("mkr", [P, H])
        mk1, mkd = two("mk1", [H, 1]), two("mkd", [H, H])
        f = [[sb(f"f{n}{u}", [P, TPS, H, M]) for n in "qk"] for u in range(U)]
        cx = two("cx", [P, NCH, CW])
        fT = two("fT", [P, NCH, S])
        rden, o, oT = two("rden", [P, TPS, NCH, HC]), two("o", [P, TPS, D]), two("oT", [P, S])
        hT, y = two("hT", [P, S]), two("y", [P, TPS, D])

        order = [(("xT", u), 6 + u) for u in range(U)]
        for u in range(U):
            order += [(("q", u), 6), (("k", u), 7), (("v", u), 4)]
        for u in range(U):
            order += [(("dg", u), 5)] + [(("f", u, n, c), 2 * n + c) for n in range(2) for c in range(2)]
            order += [(("mT", u), 4), (("mb", u), 5)]
        order += [(("cx", u), 4) for u in range(U)]
        order += [(("fT", u, c), 6 + c) for u in range(U) for c in range(NCH)]
        order += [(("o", u, c), c) for u in range(U) for c in range(2)]
        order += [(("oT", u), 2) for u in range(U)] + [(("hT", u), 3) for u in range(U)] + [(("y", u), 5) for u in range(U)]
        bk = Banks(sem, "psum", order)
        ps = lambda job: chip.psum[bk.place[job][0]]
        weights, feat_filled, feat_ready = sem("weights_loaded"), sem("feat_filled"), sem("feat_ready")
        step = lambda name, n=1: Signal(sem(name), U * n)
        mv_ready, std_ready, xn_ready = step("mv_ready"), step("std_ready"), step("xn_ready")
        qk_ready, sq_ready, shifted, f_exp, f_ready = (step("qk_ready", 2), step("sq_ready", 2), step("shifted", 2),
                                                       step("f_exp", 2), step("f_ready", 2))
        mkr_ready, mkd_ready, cx_ready, o_ready = step("mkr_ready"), step("mkd_ready"), step("cx_ready"), step("o_ready")
        dve_order = sem("dve_order")
        TURNS = B // U
        NWT = 5 + 3 + 2 + 2 + 3

        with nc.Block() as block:
            @block.sync
            def _(sp):
                for t, n in ((wq, "Wq"), (wk, "Wk"), (wv, "Wv"), (wo, "Wo"), (wfc, "Wfc"), (proj, "proj"), (spread, "spread"),
                             (head_of, "head_of"), (half_head, "half_head"), (own, "own")):
                    sp.dma_start(t[:], w[n]).then_inc(weights, 16)
                for t, n in ((bq, "bq"), (bk_, "bk"), (bo, "bo")):
                    sp.dma_start(t[:], w[n].rearrange("(p o) -> p o", o=1)).then_inc(weights, 16)
                for t, n in ((bv, "bv"), (bfc, "bfc")):
                    sp.dma_start(t[:], w[n].partition_broadcast(P)).then_inc(weights, 16)

            @block.vector
            def _(dve):
                c = Chain(dve, dve_order, per_turn=U * 10)
                for u in range(U):
                    dve.memset(v[u][:, :, :, DC:], 1.0)
                dve.wait_ge(weights, 16 * NWT)
                dve.wait_ge(feat_filled, 1)
                dve.tensor_tensor(feat[:], bcast(head_of[:], n_after=M), bcast(chip.psum[0][:, 0:M], n_before=H),
                                  ALU.mult).then_inc(feat_ready, 1)
                with dve.Fori(0, TURNS) as i:
                    c.start(i)
                    for u in range(U):
                        mv_ready.by(ln_statistics(chip, dve, c, lambda t: one_tile(chip.x, i, u, t), stats[u], mv[u], TPS))
                    for u in range(U):
                        std_ready.wait(dve, i, u)
                        c.link(dve.reciprocal(rstd[u][:], std[u][:]))
                        for t in range(TPS):
                            ins = dve.tensor_scalar(xn[u][:, t, :], one_tile(chip.x, i, u, t), mv[u][:, t, 0:1],
                                                    rstd[u][:, t:t + 1], ALU.subtract, ALU.mult)
                        xn_ready.by(ins)
                    for u in range(U):
                        for n, (nm, b_) in enumerate((("q", bq), ("k", bk_))):
                            bk.wait_filled(dve, (nm, u), i)
                            qk_ready.by(dve.tensor_scalar(qk[u][n][:], ps((nm, u))[:], b_[:], DN, ALU.add, ALU.mult))
                            qk_ready.wait(dve, i, 2 * u + n)
                            bk.drain(dve.tensor_tensor(sqs[u][n][:], qk[u][n][:], qk[u][n][:], ALU.mult), (nm, u))
                        bk.wait_filled(dve, ("v", u), i)
                        for c2 in range(NCH):
                            ins = dve.tensor_tensor(v[u][:, :, c2, 0:DC],
                                                    ps(("v", u))[:].rearrange("p (t c d) -> p t c d", t=TPS, c=NCH)[:, :, c2, :],
                                                    bcast(bv[:, c2 * DC:(c2 + 1) * DC], n_before=TPS), ALU.add)
                        bk.drain(ins, ("v", u))
                    for u in range(U):
                        bk.wait_filled(dve, ("dg", u), i)
                        bk.drain(dve.tensor_copy(dg[u][:], ps(("dg", u))[:, 0:2 * TPS * H].rearrange("p (n t h) -> p n t h", n=2, h=H)), ("dg", u))
                        bk.wait_read(dve, ("dg", u), i)
                        for n, m in ((0, mq), (1, mk)):
                            for c2 in range(2):
                                bk.wait_filled(dve, ("f", u, n, c2), i)
                                fp = ps(("f", u, n, c2))[:].rearrange("p (t h m) -> p t h m", t=HALF, h=H)
                                c.link(dve.tensor_reduce(m[u][:, c2 * HALF:(c2 + 1) * HALF, :], fp, AX_X, ALU.max))
                        mkr_ready.by(dve.tensor_reduce(mkr[u][:], mk[u][:].rearrange("p t h -> p h t"), AX_X, ALU.max))
                        c.link(dve.tensor_tensor(mq[u][:], mq[u][:], dg[u][:, 0], ALU.add))
                        for c2 in range(2):
                            fp = ps(("f", u, 0, c2))[:].rearrange("p (t m) -> p t m", m=M)
                            ts = slice(c2 * HALF, (c2 + 1) * HALF)
                            ins = dve.tensor_tensor(f[u][0][:, ts].rearrange("p t h m -> p (t h) m"), fp,
                                                    bcast(mq[u][:, ts].rearrange("p t h -> p (t h)"), n_after=M), ALU.subtract)
                            bk.drain(ins, ("f", u, 0, c2))
                        bk.wait_read(dve, ("f", u, 0, 1), i)
                        dve.sem_inc(shifted.sem, 1)
                        bk.wait_filled(dve, ("mT", u), i)
                        ins = dve.tensor_reduce(mk1[u][:], ps(("mT", u))[0:H, 0:P], AX_X, ALU.max)
                        bk.drain(ins, ("mT", u))
                        bk.wait_read(dve, ("mT", u), i)
                        mkd_ready.by(dve.tensor_scalar(mkd[u][:], chip.ident[0:H, 0:H], mk1[u][:], None, ALU.mult))
                        bk.wait_filled(dve, ("mb", u), i)
                        ins = dve.tensor_tensor(mk[u][:], dg[u][:, 1], bcast(ps(("mb", u))[:, 0:H], n_before=TPS), ALU.add)
                        bk.drain(ins, ("mb", u))
                        bk.wait_read(dve, ("mb", u), i)
                        for c2 in range(2):
                            fp = ps(("f", u, 1, c2))[:].rearrange("p (t m) -> p t m", m=M)
                            ts = slice(c2 * HALF, (c2 + 1) * HALF)
                            ins = dve.tensor_tensor(f[u][1][:, ts].rearrange("p t h m -> p (t h) m"), fp,
                                                    bcast(mk[u][:, ts].rearrange("p t h -> p (t h)"), n_after=M), ALU.subtract)
                            bk.drain(ins, ("f", u, 1, c2))
                        bk.wait_read(dve, ("f", u, 1, 1), i)
                        dve.sem_inc(shifted.sem, 1)
                    for u in range(U):
                        for n in range(2):
                            f_exp.wait(dve, i, 2 * u + n)
                            f_ready.by(dve.tensor_scalar(f[u][n][:], f[u][n][:], EPS, RATIO, ALU.add, ALU.mult))
                    for u in range(U):
                        bk.wait_filled(dve, ("cx", u), i)
                        for c2 in range(NCH):
                            a = ps(("cx", u))[:, c2 * (DC + 1):(c2 + 1) * (DC + 1)]
                            dve.tensor_tensor(cx[u][:, c2, 0:DC], a[:, 0:DC], own[:, 0:DC], ALU.mult)
                            ins = dve.tensor_tensor(cx[u][:, c2, DC:], a[:, DC:].to_broadcast([P, HC]), own[:, DC:], ALU.mult)
                        bk.drain(ins, ("cx", u))
                    for u in range(U):
                        for c2 in range(2):
                            job = ("o", u, c2)
                            bk.wait_filled(dve, job, i)
                            a = ps(job)[:, 0:HALF * NCH * CW].rearrange("p (t w) -> p t w", w=CW)
                            rd = rden[u][:, c2 * HALF:(c2 + 1) * HALF].rearrange("p t c h -> p (t c) h")
                            c.link(dve.reciprocal(rd, a[:, :, DC:]))
                            for k in range(HALF * NCH):
                                t, ch = c2 * HALF + k // NCH, k % NCH
                                ins = dve.tensor_tensor(o[u][:, t, ch * DC:(ch + 1) * DC].rearrange("p (h d) -> p h d", d=DH),
                                                        a[:, k, 0:DC].rearrange("p (h d) -> p h d", d=DH),
                                                        bcast(rd[:, k, :], n_after=DH), ALU.mult)
                            bk.drain(ins, job)
                    for u in range(U):
                        job = ("y", u)
                        bk.wait_filled(dve, job, i)
                        ins = dve.tensor_tensor(y[u][:], ps(job)[:].rearrange("p (t d) -> p t d", t=TPS), bcast(bfc[:], n_before=TPS), ALU.add)
                        bk.drain(ins, job)
                        bk.wait_read(dve, job, i)
                        xs = seq_tiles(chip.x, i, u)
                        c.link(dve.scalar_tensor_tensor(xs, y[u][:], 0.0, xs, ALU.max, ALU.add))
                c.end()

            @block.scalar
            def _(act):
                act.wait_ge(weights, 16 * NWT)
                with act.Fori(0, TURNS) as i:
                    for u in range(U):
                        mv_ready.wait(act, i, u)
                        std_ready.by(act.activation(std[u][:], mv[u][:, :, 1], ACT.Sqrt, bias=chip.ln_eps[:]))
                    for u in range(U):
                        bk.wait_filled(act, ("xT", u), i)
                        bk.drain(act.copy(xnT[u][:], ps(("xT", u))[:]), ("xT", u))
                    for u in range(U):
                        for n in range(2):
                            shifted.wait(act, i, 2 * u + n)
                            f_exp.by(act.activation(f[u][n][:], f[u][n][:], ACT.Exp))
                    for u in range(U):
                        for c2 in range(NCH):
                            bk.wait_filled(act, ("fT", u, c2), i)
                            bk.drain(act.copy(fT[u][:, c2, :], ps(("fT", u, c2))[:]), ("fT", u, c2))
                    for u in range(U):
                        bk.wait_filled(act, ("oT", u), i)
                        bk.drain(act.copy(oT[u][:], ps(("oT", u))[:]), ("oT", u))
                    for u in range(U):
                        bk.wait_filled(act, ("hT", u), i)
                        bk.drain(act.activation(hT[u][:], ps(("hT", u))[:], ACT.Identity, bias=bo[:]), ("hT", u))

            @block.tensor
            def _(pe):
                bk.open(pe)
                pe.wait_ge(weights, 16 * NWT)
                pe.matmul(chip.psum[0][:, 0:M], spread[:], proj[:], start=True, stop=True).then_inc(feat_filled, 1)
                pe.wait_ge(feat_ready, 1)
                chip.apart(pe)
                with pe.Fori(0, TURNS) as i:
                    for u in range(U):
                        xn_ready.wait(pe, i, u)
                        bk.wait_drained(pe, ("xT", u), i)
                        for t in range(TPS):
                            ins = pe.transpose(ps(("xT", u))[:, t * P:(t + 1) * P], xn[u][:, t, :], chip.ident[:])
                        bk.fill(ins, ("xT", u))
                    for u in range(U):
                        bk.wait_read(pe, ("xT", u), i)
                        for nm, wt in (("q", wq), ("k", wk)):
                            bk.wait_drained(pe, (nm, u), i)
                            bk.fill(pe.matmul(ps((nm, u))[:], wt[:], xnT[u][:], start=True, stop=True), (nm, u))
                        bk.wait_drained(pe, ("v", u), i)
                        for t in range(TPS):
                            ins = pe.matmul(ps(("v", u))[:, t * D:(t + 1) * D], xnT[u][:, t * P:(t + 1) * P], wv[:], start=True, stop=True)
                        bk.fill(ins, ("v", u))
                    for u in range(U):
                        bk.wait_read(pe, ("k", u), i)
                        bk.wait_drained(pe, ("dg", u), i)
                        for n in range(2):
                            for t in range(TPS):
                                ins = pe.matmul(ps(("dg", u))[:, (n * TPS + t) * H:(n * TPS + t + 1) * H],
                                                sqs[u][n][:, t * P:(t + 1) * P], half_head[:], start=True, stop=True)
                        bk.fill(ins, ("dg", u))
                        for n in range(2):
                            for c2 in range(2):
                                job = ("f", u, n, c2)
                                bk.wait_drained(pe, job, i)
                                for tt in range(HALF):
                                    t = c2 * HALF + tt
                                    ins = pe.matmul(ps(job)[:, tt * HM:(tt + 1) * HM], qk[u][n][:, t * P:(t + 1) * P],
                                                    feat[:].rearrange("p h m -> p (h m)"), start=True, stop=True)
                                bk.fill(ins, job)
                        mkr_ready.wait(pe, i, u)
                        bk.wait_drained(pe, ("mT", u), i)
                        bk.fill(pe.transpose(ps(("mT", u))[0:H, 0:P], mkr[u][:], chip.ident[:]), ("mT", u))
                        mkd_ready.wait(pe, i, u)
                        bk.wait_drained(pe, ("mb", u), i)
                        bk.fill(pe.matmul(ps(("mb", u))[:, 0:H], chip.ones[0:H, :], mkd[u][:], start=True, stop=True), ("mb", u))
                    for u in range(U):
                        f_ready.wait(pe, i, 2 * u + 1)
                        bk.wait_read(pe, ("v", u), i)
                        bk.wait_drained(pe, ("cx", u), i)
                        for c2 in range(NCH):
                            for t in range(TPS):
                                ins = pe.matmul(ps(("cx", u))[:, c2 * (DC + 1):(c2 + 1) * (DC + 1)],
                                                f[u][1][:, t, c2 * HC:(c2 + 1) * HC, :].rearrange("p h m -> p (h m)"),
                                                v[u][:, t, c2, :], start=(t == 0), stop=(t == TPS - 1))
                        bk.fill(ins, ("cx", u))
                    for u in range(U):
                        f_ready.wait(pe, i, 2 * u)
                        for c2 in range(NCH):
                            bk.wait_drained(pe, ("fT", u, c2), i)
                            for t in range(TPS):
                                ins = pe.transpose(ps(("fT", u, c2))[:, t * P:(t + 1) * P],
                                                   f[u][0][:, t, c2 * HC:(c2 + 1) * HC, :].rearrange("p h m -> p (h m)"), chip.ident[:])
                            bk.fill(ins, ("fT", u, c2))
                    for u in range(U):
                        bk.wait_read(pe, ("cx", u), i)
                        for c2 in range(NCH):
                            bk.wait_read(pe, ("fT", u, c2), i)
                        for c2 in range(2):
                            job = ("o", u, c2)
                            bk.wait_drained(pe, job, i)
                            for k in range(HALF * NCH):
                                t, ch = c2 * HALF + k // NCH, k % NCH
                                ins = pe.matmul(ps(job)[:, k * CW:(k + 1) * CW], fT[u][:, ch, t * P:(t + 1) * P], cx[u][:, ch, :],
                                                start=True, stop=True)
                            bk.fill(ins, job)
                    for u in range(U):
                        for c2 in range(2):
                            bk.wait_read(pe, ("o", u, c2), i)
                        bk.wait_drained(pe, ("oT", u), i)
                        for t in range(TPS):
                            ins = pe.transpose(ps(("oT", u))[:, t * P:(t + 1) * P], o[u][:, t, :], chip.ident[:])
                        bk.fill(ins, ("oT", u))
                    for u in range(U):
                        bk.wait_read(pe, ("oT", u), i)
                        bk.wait_drained(pe, ("hT", u), i)
                        bk.fill(pe.matmul(ps(("hT", u))[:], wo[:], oT[u][:], start=True, stop=True), ("hT", u))
                    for u in range(U):
                        bk.wait_read(pe, ("hT", u), i)
                        bk.wait_drained(pe, ("y", u), i)
                        for t in range(TPS):
                            ins = pe.matmul(ps(("y", u))[:, t * D:(t + 1) * D], hT[u][:, t * P:(t + 1) * P], wfc[:], start=True, stop=True)
                        bk.fill(ins, ("y", u))



def selective_scan(chip, w):
    nc = chip.nc
    DI, N, R = 256, 16, 8
    CH = DI // P
    TAPS = 4
    ctx = ExitStack()
    with ctx:
        sb = lambda name, shape: chip.sb(ctx, f"l2a_{name}", shape)
        two = lambda name, shape: [sb(f"{name}{u}", shape) for u in range(U)]
        sem = lambda name: chip.sem(f"l2a_{name}")
        w_in, w_x, w_dt, w_out = sb("w_in", [P, 2 * DI]), sb("w_x", [P, CH, R + 2 * N]), sb("w_dt", [R, DI]), sb("w_out", [P, CH, D])
        ln_w, ln_b = sb("ln_w", [P, 1]), sb("ln_b", [P, 1])
        conv_w, conv_b, b_dt, d_par = sb("conv_w", [P, CH, TAPS]), sb("conv_b", [P, CH]), sb("b_dt", [P, CH]), sb("d_par", [P, CH])
        a_log, a_neg = sb("a_log", [P, CH, N]), sb("a_neg", [P, CH, N])
        pick = sb("pick", [N, N, P])
        stats, mv = two("stats", [P, TPS, 6]), two("mv", [P, TPS, 2])
        std, rstd = two("std", [P, TPS]), two("rstd", [P, TPS])
        stats2, mv2 = two("stats2", [P, TPS, 6]), two("mv2", [P, TPS, 2])
        std2, rstd2 = two("std2", [P, TPS]), two("rstd2", [P, TPS])
        xn, xm, xmT = two("xn", [P, TPS, D]), two("xm", [P, TPS, D]), two("xmT", [P, S])
        xi = two("xi", [P, CH, S + TAPS - 1])
        conv, xc, sz = two("conv", [P, CH, S]), two("xc", [P, CH, S]), two("sz", [P, CH, S])
        dtr, bT, cT = two("dtr", [R, S]), two("bT", [N, S]), two("cT", [N, S])
        sp_a, sp_r = sb("sp_a", [P, CH, S]), sb("sp_r", [P, CH, S])
        dt, du = two("dt", [P, CH, S]), two("du", [P, CH, S])
        yT = two("yT", [P, CH, S])
        NB = 2
        dA = [sb(f"dA{n}", [P, CH, S]) for n in range(NB)]
        dBu = [sb(f"dBu{n}", [P, CH, S]) for n in range(NB)]
        h = [sb(f"h{n}", [P, CH * S]) for n in range(NB)]
        hc = [sb(f"hc{n}", [P, CH, S]) for n in range(NB)]

        rest = lambda u: ([(("xT", u), 6)] + [(("in", u, j), 6 + (j + 1) % 2) for j in range(2 * CH)] +
                          [(("dtr", u), 7), (("bT", u), 6), (("cT", u), 7)] + [(("dt", u, j), 6 + j) for j in range(CH)])
        order = []
        for u in range(U):
            order += rest(u)
            for n in range(N):
                order += [(("B", u, n), n % 2), (("C", u, n), 2 + n % 2)]
            order += [(("y", u, j), 4 + j) for j in range(CH)] + [(("out", u), 6)]
        bk = Banks(sem, "psum", order)
        ps = lambda job: chip.psum[bk.place[job][0]]
        weights, a_ready, zeroed = sem("weights_loaded"), sem("a_ready"), sem("zeroed")
        step = lambda name, n=1: Signal(sem(name), U * n)
        mv_ready, std_ready, mv2_ready, std2_ready, xm_ready = (step("mv_ready"), step("std_ready"), step("mv2_ready"),
                                                                step("std2_ready"), step("xm_ready"))
        conv_ready, xc_ready, dt_exp, dt_ready = step("conv_ready"), step("xc_ready"), step("dt_exp", CH), step("dt_ready")
        dA_ready, dBu_ready, h_ready, hc_ready = step("dA_ready", N), step("dBu_ready", N), step("h_ready", N), step("hc_ready", N)
        hc_summed, yT_ready = step("hc_summed", N), step("yT_ready")
        dve_order, act_order = sem("dve_order"), sem("act_order")
        TURNS = B // U
        NWT = 3 + CH * 5 + 2 + 1 + CH

        with nc.Block() as block:
            @block.sync
            def _(sp):
                sp.dma_start(w_in[:], w["W_in"]).then_inc(weights, 16)
                sp.dma_start(w_dt[:], w["W_dt"]).then_inc(weights, 16)
                sp.dma_start(pick[:], w["pick"]).then_inc(weights, 16)
                sp.dma_start(w_out[:], w["W_out"].rearrange("(c p) d -> p c d", p=P)).then_inc(weights, 16)
                col = lambda a: a.rearrange("(p o) -> p o", o=1)
                sp.dma_start(ln_w[:], col(w["ln_w"])).then_inc(weights, 16)
                sp.dma_start(ln_b[:], col(w["ln_b"])).then_inc(weights, 16)
                for c in range(CH):
                    rows = slice(c * P, (c + 1) * P)
                    sp.dma_start(w_x[:, c, :], w["W_xproj"][rows, :]).then_inc(weights, 16)
                    sp.dma_start(conv_w[:, c, :], w["conv_w"][rows, 0, :]).then_inc(weights, 16)
                    sp.dma_start(a_log[:, c, :], w["A_log"][rows, :]).then_inc(weights, 16)
                    for t, n in ((conv_b, "conv_b"), (b_dt, "b_dt"), (d_par, "D_param")):
                        sp.dma_start(t[:, c:c + 1], col(w[n][rows])).then_inc(weights, 16)

            @block.gpsimd
            def _(pool):
                for n in range(NB):
                    pool.memset(dA[n][:, :, 0:1], 0.0)
                for u in range(U):
                    ins = pool.memset(xi[u][:, :, 0:TAPS - 1], 0.0)
                ins.then_inc(zeroed, 1)

            @block.scalar
            def _(act):
                act.wait_ge(weights, 16 * NWT)
                act.wait_ge(zeroed, 1)
                act.activation(a_neg[:], a_log[:], ACT.Exp).then_inc(a_ready, 1)
                act.wait_ge(a_ready, 1)
                act.mul(a_neg[:], a_neg[:], -1.0).then_inc(a_ready, 1)
                act.wait_ge(a_ready, 2)
                c = Chain(act, act_order, per_turn=U * CH * 2)
                with act.Fori(0, TURNS) as i:
                    c.start(i)
                    for u in range(U):
                        mv_ready.wait(act, i, u)
                        std_ready.by(act.activation(std[u][:], mv[u][:, :, 1], ACT.Sqrt, bias=chip.ln_eps[:]))
                        mv2_ready.wait(act, i, u)
                        std2_ready.by(act.activation(std2[u][:], mv2[u][:, :, 1], ACT.Sqrt, bias=chip.ln_eps[:]))
                        bk.wait_filled(act, ("xT", u), i)
                        bk.drain(act.activation(xmT[u][:], ps(("xT", u))[:], ACT.Identity, bias=ln_b[:], scale=ln_w[:]), ("xT", u))
                        for j in range(CH):
                            bk.wait_filled(act, ("in", u, j), i)
                            bk.drain(act.copy(xi[u][:, j, TAPS - 1:], ps(("in", u, j))[:]), ("in", u, j))
                        for j in range(CH):
                            bk.wait_filled(act, ("in", u, CH + j), i)
                            bk.drain(act.activation(sz[u][:, j, :], ps(("in", u, CH + j))[:], ACT.Silu), ("in", u, CH + j))
                        conv_ready.wait(act, i, u)
                        for j in range(CH):
                            ins = act.activation(xc[u][:, j, :], conv[u][:, j, :], ACT.Silu, bias=conv_b[:, j:j + 1])
                        xc_ready.by(ins)
                        for nm, t in (("dtr", dtr), ("bT", bT), ("cT", cT)):
                            bk.wait_filled(act, (nm, u), i)
                            bk.drain(act.copy(t[u][:], ps((nm, u))[0:t[u].shape[0], :]), (nm, u))
                        for j in range(CH):
                            bk.wait_read(act, ("dt", u, j), i)
                            c.link(act.activation(sp_a[:, j, :], sp_r[:, j, :], ACT.Abs))
                            c.link(act.activation(sp_a[:, j, :], sp_a[:, j, :], ACT.Exp, scale=-1.0))
                            dt_exp.by(act.activation(sp_a[:, j, :], sp_a[:, j, :], ACT.Ln, bias=1.0))
                        dt_ready.wait(act, i, u)
                        for n in range(N):
                            if n >= NB:
                                h_ready.wait(act, i, u * N + n - NB)
                            for j in range(CH):
                                ins = act.activation(dA[n % NB][:, j, 1:], dt[u][:, j, 1:], ACT.Exp, scale=a_neg[:, j, n:n + 1])
                            dA_ready.by(ins)
                c.end()

            @block.vector
            def _(dve):
                dve.wait_ge(weights, 16 * NWT)
                c = Chain(dve, dve_order, per_turn=U * (5 + CH * (TAPS - 1) + 2))
                with dve.Fori(0, TURNS) as i:
                    c.start(i)
                    for u in range(U):
                        mv_ready.by(ln_statistics(chip, dve, c, lambda t: one_tile(chip.x, i, u, t), stats[u], mv[u], TPS))
                        std_ready.wait(dve, i, u)
                        c.link(dve.reciprocal(rstd[u][:], std[u][:]))
                        for t in range(TPS):
                            ins = dve.tensor_scalar(xn[u][:, t, :], one_tile(chip.x, i, u, t), mv[u][:, t, 0:1],
                                                    rstd[u][:, t:t + 1], ALU.subtract, ALU.mult)
                        c.link(ins)
                        mv2_ready.by(ln_statistics(chip, dve, c, lambda t: xn[u][:, t, :], stats2[u], mv2[u], TPS))
                        std2_ready.wait(dve, i, u)
                        c.link(dve.reciprocal(rstd2[u][:], std2[u][:]))
                        for t in range(TPS):
                            ins = dve.tensor_scalar(xm[u][:, t, :], xn[u][:, t, :], mv2[u][:, t, 0:1],
                                                    rstd2[u][:, t:t + 1], ALU.subtract, ALU.mult)
                        xm_ready.by(ins)
                        for j in range(CH):
                            bk.wait_read(dve, ("in", u, j), i)
                            c.link(dve.tensor_scalar(conv[u][:, j, :], xi[u][:, j, 0:S], conv_w[:, j, 0:1], None, ALU.mult))
                            for k in range(1, TAPS):
                                ins = dve.scalar_tensor_tensor(conv[u][:, j, :], xi[u][:, j, k:k + S], conv_w[:, j, k:k + 1],
                                                               conv[u][:, j, :], ALU.mult, ALU.add)
                                if k < TAPS - 1:
                                    c.link(ins)
                        conv_ready.by(ins)
                        for j in range(CH):
                            bk.wait_filled(dve, ("dt", u, j), i)
                            bk.drain(dve.tensor_scalar(sp_r[:, j, :], ps(("dt", u, j))[:], b_dt[:, j:j + 1], None, ALU.add), ("dt", u, j))
                            bk.wait_read(dve, ("dt", u, j), i)
                        for j in range(CH):
                            dt_exp.wait(dve, i, u * CH + j)
                        ins = dve.scalar_tensor_tensor(dt[u][:], sp_r[:], 0.0, sp_a[:], ALU.max, ALU.add)
                        dt_ready.by(ins)
                        dt_ready.wait(dve, i, u)
                        xc_ready.wait(dve, i, u)
                        c.link(dve.tensor_tensor(du[u][:], dt[u][:], xc[u][:], ALU.mult))
                        for n in range(N):
                            q = n % NB
                            bk.wait_filled(dve, ("B", u, n), i)
                            ins = dve.tensor_tensor(dBu[q][:], du[u][:], bcast(ps(("B", u, n))[:], n_before=CH), ALU.mult)
                            bk.drain(ins, ("B", u, n))
                            bk.wait_read(dve, ("B", u, n), i)
                            dA_ready.wait(dve, i, u * N + n)
                            h_ready.by(dve.tensor_tensor_scan(h[q][:], dA[q][:].rearrange("p c s -> p (c s)"),
                                                              dBu[q][:].rearrange("p c s -> p (c s)"), 0.0, ALU.mult, ALU.add))
                            bk.wait_filled(dve, ("C", u, n), i)
                            h_ready.wait(dve, i, u * N + n)
                            if n >= NB:
                                hc_summed.wait(dve, i, u * N + n - NB)
                            ins = dve.tensor_tensor(hc[q][:], h[q][:].rearrange("p (c s) -> p c s", c=CH), bcast(ps(("C", u, n))[:], n_before=CH), ALU.mult)
                            bk.drain(ins, ("C", u, n))
                        for j in range(CH):
                            bk.wait_filled(dve, ("y", u, j), i)
                            ins = dve.scalar_tensor_tensor(yT[u][:, j, :], xc[u][:, j, :], d_par[:, j:j + 1], ps(("y", u, j))[:], ALU.mult, ALU.add)
                            bk.drain(ins, ("y", u, j))
                        for j in range(CH):
                            bk.wait_read(dve, ("y", u, j), i)
                        yT_ready.by(dve.tensor_tensor(yT[u][:], yT[u][:], sz[u][:], ALU.mult))
                        xs = seq_tiles(chip.x, i, u)
                        c.link(dve.tensor_tensor(xs, xs, xn[u][:], ALU.add))
                        bk.wait_filled(dve, ("out", u), i)
                        ins = dve.tensor_tensor(xs, ps(("out", u))[:].rearrange("p (t d) -> p t d", t=TPS), xs, ALU.add)
                        bk.drain(ins, ("out", u))
                c.end()

            @block.tensor
            def _(pe):
                bk.open(pe)
                pe.wait_ge(weights, 16 * NWT)

                def one(job, i, *mms):
                    bk.wait_drained(pe, job, i)
                    for k, (out, lhsT, rhs) in enumerate(mms):
                        ins = pe.matmul(out, lhsT, rhs, start=(k == 0), stop=(k == len(mms) - 1))
                    bk.fill(ins, job)

                with pe.Fori(0, TURNS) as i:
                    for u in range(U):
                        xm_ready.wait(pe, i, u)
                        bk.wait_drained(pe, ("xT", u), i)
                        for t in range(TPS):
                            ins = pe.transpose(ps(("xT", u))[:, t * P:(t + 1) * P], xm[u][:, t, :], chip.ident[:])
                        bk.fill(ins, ("xT", u))
                        bk.wait_read(pe, ("xT", u), i)
                        for j in range(2 * CH):
                            one(("in", u, j), i, (ps(("in", u, j))[:], w_in[:, j * P:(j + 1) * P], xmT[u][:]))
                        xc_ready.wait(pe, i, u)
                        for nm, a, m in (("dtr", 0, R), ("bT", R, N), ("cT", R + N, N)):
                            one((nm, u), i, *((ps((nm, u))[0:m, :], w_x[:, j, a:a + m], xc[u][:, j, :]) for j in range(CH)))
                        bk.wait_read(pe, ("dtr", u), i)
                        for j in range(CH):
                            one(("dt", u, j), i, (ps(("dt", u, j))[:], w_dt[:, j * P:(j + 1) * P], dtr[u][:]))
                        bk.wait_read(pe, ("bT", u), i)
                        bk.wait_read(pe, ("cT", u), i)

                        def spread(n):
                            one(("B", u, n), i, (ps(("B", u, n))[:], pick[:, n, :], bT[u][:]))
                            one(("C", u, n), i, (ps(("C", u, n))[:], pick[:, n, :], cT[u][:]))

                        spread(0)
                        for j in range(CH):
                            bk.wait_drained(pe, ("y", u, j), i)
                        for n in range(N):
                            if n + 1 < N:
                                spread(n + 1)
                            bk.wait_read(pe, ("C", u, n), i)
                            for j in range(CH):
                                ins = pe.matmul(ps(("y", u, j))[:], chip.ident[:], hc[n % NB][:, j, :], start=(n == 0), stop=(n == N - 1))
                                if n == N - 1:
                                    bk.fill(ins, ("y", u, j))
                            if n < N - 1:
                                hc_summed.by(ins)
                        hc_summed_last = pe.sem_inc(hc_summed.sem, 1)
                        yT_ready.wait(pe, i, u)
                        bk.wait_drained(pe, ("out", u), i)
                        for t in range(TPS):
                            for j in range(CH):
                                ins = pe.matmul(ps(("out", u))[:, t * D:(t + 1) * D], yT[u][:, j, t * P:(t + 1) * P], w_out[:, j, :],
                                                start=(j == 0), stop=(j == CH - 1))
                        bk.fill(ins, ("out", u))



def build(nc, a, out, stages=range(8)):
    with ExitStack() as ctx:
        chip = Chip(nc, ctx)
        load_stage(chip, a["L0_attn_x"], a["ident"])
        chip.end_layer()
        part = lambda p: {k[len(p):]: v for k, v in a.items() if k.startswith(p)}
        layers = ((cosine_attention, "L0_attn_"), (top2_glu_experts, "L0_ffn_"),
                  (feature_attention, "L1_attn_"), (switch_experts, "L1_ffn_"),
                  (selective_scan, "L2_attn_"), (expert_choice_experts, "L2_ffn_"),
                  (relative_position_attention, "L3_attn_"), (threshold_experts, "L3_ffn_"))
        for n in stages:
            layer, prefix = layers[n]
            layer(chip, part(prefix))
            chip.end_layer()
        store_stage(chip, out)


def laid_out(inputs):
    a = {k: np.asarray(v) for k, v in inputs.items()}
    for k in ("L0_attn_Wq", "L0_attn_Wk", "L0_attn_Wv", "L0_attn_W1", "L0_attn_W2", "L0_attn_W3",
              "L1_attn_Wq", "L1_attn_Wk", "L1_attn_Wv", "L1_attn_Wo", "L1_attn_Wfc", "L1_attn_proj"):
        a[k] = a[k].T
    a["L3_ffn_Wgt"] = np.concatenate([a.pop("L3_ffn_Wg"), a.pop("L3_ffn_Wt")], axis=1)
    a["L3_ffn_bgt"] = np.concatenate([a.pop("L3_ffn_bg"), a.pop("L3_ffn_bt")])
    a["L3_attn_onehot"] = buckets_by_distance()
    row, head = np.arange(P)[:, None], np.arange(16)[None, :]
    a["L1_attn_spread"] = (np.arange(8)[:, None] == np.arange(P)[None, :] % 8).astype(np.float32)
    a["L1_attn_head_of"] = (row // 8 == head).astype(np.float32)
    a["L1_attn_half_head"] = np.where(row // 8 == head, np.float32(0.5), np.float32(0))
    a["L1_attn_own"] = (row // 16 == np.concatenate([np.arange(64) // 8, np.arange(8)])[None, :]).astype(np.float32)
    a["L2_attn_pick"] = np.broadcast_to(np.eye(16, dtype=np.float32)[:, :, None], (16, 16, P))
    a["ident"] = np.eye(P, dtype=np.float32)
    return {k: np.ascontiguousarray(v) for k, v in a.items()}


def make_program(nc, inputs, stages=range(8)):
    arrays, aps = {}, {}
    for name, v in laid_out(inputs).items():
        arrays[f"in_{name}_dram"] = v
        aps[name] = nc.dram_tensor(f"in_{name}_dram", v.shape, mybir.dt.from_np(v.dtype), kind="ExternalInput").ap()
    out = nc.dram_tensor("out_0_dram", (B, S, D), F32, kind="ExternalOutput").ap()
    build(nc, aps, out, stages)
    return arrays


def kernel(**inputs):
    import concourse.bacc as _bacc
    from concourse.bass_utils import run_bass_kernel_spmd as _run

    nc = _bacc.Bacc("TRN2", target_bir_lowering=False, num_devices=1)
    arrays = make_program(nc, inputs)
    r = _run(nc, [arrays], core_ids=[0])
    return r.results[0]["out_0_dram"]
```

```python
from contextlib import ExitStack

import numpy as np

import concourse.bass as bass
import concourse.mybir as mybir

ALU = mybir.AluOpType
ACT = mybir.ActivationFunctionType
F32 = mybir.dt.float32
AX_X = mybir.AxisListType.X

P = 128
D = 128
B, S = 8, 512
TPS = S // P
NT = B * TPS
U = 2
LN_EPS = 1e-5
BANK = 512


class Chain:

    def __init__(self, eng, sem, per_turn=0, base=0):
        self.eng, self.sem, self.per_turn, self.turn, self.n, self.base = eng, sem, per_turn, 0, 0, base

    def start(self, turn):
        self.turn, self.n = turn, 0

    def link(self, ins):
        self.n += 1
        ins.then_inc(self.sem, 1)
        self.eng.wait_ge(self.sem, self.turn * self.per_turn + (self.n + self.base))

    def end(self):
        assert self.n == self.per_turn, (self.n, self.per_turn)


class Banks:

    def __init__(self, sem, name, order):
        self.place, self.uses = {}, {}
        for job, bank in order:
            self.place[job] = (bank, self.uses.get(bank, 0))
            self.uses[bank] = self.uses.get(bank, 0) + 1
        self.filled = {k: sem(f"{name}_bank{k}_filled") for k in self.uses}
        self.drained = {k: sem(f"{name}_bank{k}_drained") for k in self.uses}

    def open(self, eng):
        for k in self.uses:
            eng.sem_inc(self.drained[k], 1)

    def wait_drained(self, eng, job, turn):
        k, n = self.place[job]
        eng.wait_ge(self.drained[k], turn * self.uses[k] + (n + 1))

    def wait_filled(self, eng, job, turn):
        k, n = self.place[job]
        eng.wait_ge(self.filled[k], turn * self.uses[k] + (n + 1))

    def wait_read(self, eng, job, turn):
        k, n = self.place[job]
        eng.wait_ge(self.drained[k], turn * self.uses[k] + (n + 2))

    def fill(self, ins, job):
        ins.then_inc(self.filled[self.place[job][0]], 1)

    def drain(self, ins, job):
        ins.then_inc(self.drained[self.place[job][0]], 1)


class Signal:

    def __init__(self, sem, per_turn):
        self.sem, self.per_turn = sem, per_turn

    def by(self, ins):
        ins.then_inc(self.sem, 1)

    def wait(self, eng, turn, n):
        eng.wait_ge(self.sem, turn * self.per_turn + (n + 1))


class Chip:

    def __init__(self, nc, ctx):
        self.nc, self.ctx = nc, ctx
        self.x = self.sb(ctx, "x", [P, NT, D])
        self.ident = self.sb(ctx, "ident", [P, P])
        self.ones = self.sb(ctx, "ones", [P, P])
        self.ln_eps = self.sb(ctx, "ln_eps", [P, 1])
        self.apart_count = nc.alloc_semaphore(name="apart_count")
        self.counts = []
        self.psum = [ctx.enter_context(nc.psum_tensor(f"bank{k}", [P, BANK], F32)) for k in range(8)]

    def sb(self, ctx, name, shape, dt=F32):
        return ctx.enter_context(self.nc.sbuf_tensor(name, shape, dt))

    def apart(self, eng):
        eng.sem_inc(self.apart_count, 1)

    def sem(self, name):
        self.counts.append(self.nc.alloc_semaphore(name=name))
        return self.counts[-1]

    def end_layer(self):
        self.nc.clear_and_free_semaphores(self.counts)
        self.nc.all_engine_barrier()
        self.counts = []


def ln_statistics(chip, dve, chain, x_tile, stats, mv, n):
    for t in range(n):
        ins = dve.bn_stats(stats[:, t, :], x_tile(t))
    chain.link(ins)
    chip.apart(dve)
    for t in range(n):
        ins = dve.bn_aggr(mv[:, t, :], stats[:, t, :])
    return ins



def load_stage(chip, x_in, ident_in):
    nc = chip.nc
    loaded = chip.sem("x_loaded")
    with nc.Block() as block:
        @block.sync
        def _(sp):
            sp.dma_start(chip.ident[:], ident_in).then_inc(loaded, 16)
            xv = x_in.rearrange("b (t p) d -> p (b t) d", p=P)
            for c in range(2):
                h = NT // 2
                sp.dma_start(chip.x[:, c * h:(c + 1) * h, :], xv[:, c * h:(c + 1) * h, :]).then_inc(loaded, 16)
            sp.wait_ge(loaded, 48)

        @block.vector
        def _(dve):
            nc.vector.memset(chip.ones[:], 1.0)
            nc.vector.memset(chip.ln_eps[:], LN_EPS)


def store_stage(chip, out):
    nc = chip.nc
    stored = chip.sem("out_stored")
    with nc.Block() as block:
        @block.sync
        def _(sp):
            ov = out.rearrange("b (t p) d -> p (b t) d", p=P)
            for c in range(2):
                h = NT // 2
                sp.dma_start(ov[:, c * h:(c + 1) * h, :], chip.x[:, c * h:(c + 1) * h, :]).then_inc(stored, 16)
            sp.wait_ge(stored, 32)



def cosine_attention(chip, w):
    nc = chip.nc
    F = 512
    J = F // P
    QK, QKV = 2 * D, 3 * D
    ctx = ExitStack()
    with ctx:
        sb = lambda name, shape: chip.sb(ctx, f"l0a_{name}", shape)
        two = lambda name, shape: [sb(f"{name}{u}", shape) for u in range(U)]
        sem = lambda name: chip.sem(f"l0a_{name}")
        w_qkv, b_qkv = sb("w_qkv", [P, QKV]), sb("b_qkv", [P, QKV])
        w1, w2, w3 = sb("w1", [P, D]), sb("w2", [P, F]), sb("w3", [P, J, D])
        b1, b2, b3 = sb("b1", [P, 1]), sb("b2", [P, J]), sb("b3", [P, D])
        stats, mv = two("stats", [P, TPS, 6]), two("mv", [P, TPS, 2])
        std, rstd = two("std", [P, TPS]), two("rstd", [P, TPS])
        xn, xnT = two("xn", [P, TPS, D]), two("xnT", [P, S])
        qkv = two("qkv", [P, TPS, QKV + 1])
        sq, ss = two("sq", [P, TPS, 2, D]), two("ss", [P, TPS, 2])
        length, inv = two("length", [P, TPS, 2]), two("inv", [P, TPS, 2])
        qk = two("qk", [P, TPS, 2, D])
        qT, kT = two("qT", [P, S]), two("kT", [P, S])
        E, rden = two("E", [P, TPS, S]), two("rden", [P, TPS])
        o, oT = two("o", [P, TPS, D]), two("oT", [P, S])
        h1, h2 = two("h1", [P, S]), two("h2", [P, J, S])
        y = two("y", [P, TPS, D])

        order = [(("xT", u), 6 + u) for u in range(U)]
        order += [(("qkv", u, t), 4 + t % 2) for u in range(U) for t in range(TPS)]
        order += [((n, u), k) for u in range(U) for n, k in (("qT", 6), ("kT", 7))]
        order += [(("s", u, t), t) for u in range(U) for t in range(TPS)]
        order += [(("av", u, t), 4 + t % 2) for u in range(U) for t in range(TPS)]
        order += [(("oT", u), 6 + u) for u in range(U)]
        order += [(("h1", u), 6 + u) for u in range(U)]
        order += [(("h2", u, j), j) for u in range(U) for j in range(J)]
        order += [(("y", u), 4 + u) for u in range(U)]
        bk = Banks(sem, "psum", order)
        ps = lambda job: chip.psum[bk.place[job][0]]

        weights = sem("weights_loaded")
        WEIGHTS = 10
        step = lambda name, n=1: Signal(sem(name), U * n)
        mv_ready, std_ready, xn_ready, xnT_ready = step("mv_ready"), step("std_ready"), step("xn_ready"), step("xnT_ready")
        ss_ready, length_ready, qk_ready, qkT_ready = (step("ss_ready"), step("length_ready"), step("qk_ready"),
                                                       step("qkT_ready", 2))
        e_ready, o_ready, oT_ready = step("e_ready", TPS), step("o_ready"), step("oT_ready")
        h1_ready, h2_ready = step("h1_ready"), step("h2_ready", J)
        dve_order = sem("dve_order")
        TURNS = B // U

        def x_tile(i, u, t):
            return chip.x[:, bass.ds((i * U + u) * TPS + t, 1), :].rearrange("p a d -> p (a d)")

        with nc.Block() as block:
            @block.sync
            def _(sp):
                for n, nm in enumerate(["Wq", "Wk", "Wv"]):
                    sp.dma_start(w_qkv[:, n * D:(n + 1) * D], w[nm]).then_inc(weights, 16)
                    sp.dma_start(b_qkv[:, n * D:(n + 1) * D], w["b" + nm[1]].partition_broadcast(P)).then_inc(weights, 16)
                sp.dma_start(w1[:], w["W1"]).then_inc(weights, 16)
                sp.dma_start(w2[:], w["W2"]).then_inc(weights, 16)
                sp.dma_start(w3[:], w["W3"].rearrange("(j p) d -> p j d", p=P)).then_inc(weights, 16)
                sp.dma_start(b3[:], w["b3"].partition_broadcast(P)).then_inc(weights, 16)
                sp.dma_start(b1[:], w["b1"].rearrange("(p o) -> p o", o=1)).then_inc(weights, 16)
                with nc.allow_non_contiguous_dma(reason="a bias by partition"):
                    sp.dma_start(b2[:], w["b2"].rearrange("(j p) -> p j", p=P)).then_inc(weights, 16)

            @block.vector
            def _(dve):
                c = Chain(dve, dve_order, per_turn=U * 7)
                for u in range(U):
                    dve.memset(qkv[u][:, :, QKV:], 1.0)
                dve.wait_ge(weights, 16 * (WEIGHTS + 2))
                with dve.Fori(0, TURNS) as i:
                    c.start(i)
                    for u in range(U):
                        mv_ready.by(ln_statistics(chip, dve, c, lambda t: x_tile(i, u, t), stats[u], mv[u], TPS))
                    for u in range(U):
                        std_ready.wait(dve, i, u)
                        c.link(dve.reciprocal(rstd[u][:], std[u][:]))
                        for t in range(TPS):
                            ins = dve.tensor_scalar(xn[u][:, t, :], x_tile(i, u, t), mv[u][:, t, 0:1],
                                                    rstd[u][:, t:t + 1], ALU.subtract, ALU.mult)
                        xn_ready.by(ins)
                    for u in range(U):
                        for t in range(TPS):
                            bk.wait_filled(dve, ("qkv", u, t), i)
                            bk.drain(dve.tensor_tensor(qkv[u][:, t, 0:QKV], ps(("qkv", u, t))[:, 0:QKV], b_qkv[:],
                                                       ALU.add), ("qkv", u, t))
                        bk.wait_read(dve, ("qkv", u, TPS - 2), i)
                        bk.wait_read(dve, ("qkv", u, TPS - 1), i)
                        qk_in = qkv[u][:, :, 0:QK].rearrange("p t (n d) -> p t n d", n=2)
                        c.link(dve.tensor_tensor(sq[u][:], qk_in, qk_in, ALU.mult))
                        ss_ready.by(dve.tensor_reduce(ss[u][:], sq[u][:], AX_X, ALU.add))
                    for u in range(U):
                        length_ready.wait(dve, i, u)
                        c.link(dve.tensor_scalar(inv[u][:], length[u][:], 1e-12, None, ALU.max))
                        c.link(dve.reciprocal(inv[u][:], inv[u][:]))
                        for n in range(2):
                            ins = dve.tensor_tensor(qk[u][:, :, n, :], qkv[u][:, :, n * D:(n + 1) * D],
                                                    inv[u][:, :, n:n + 1].to_broadcast([P, TPS, D]), ALU.mult)
                        qk_ready.by(ins)
                    for u in range(U):
                        for t in range(TPS):
                            job = ("av", u, t)
                            bk.wait_filled(dve, job, i)
                            dve.tensor_copy(o[u][:, t, :], ps(job)[:, 0:D])
                            bk.drain(dve.tensor_copy(rden[u][:, t:t + 1], ps(job)[:, D:D + 1]), job)
                        bk.wait_read(dve, ("av", u, TPS - 2), i)
                        bk.wait_read(dve, ("av", u, TPS - 1), i)
                        c.link(dve.reciprocal(rden[u][:], rden[u][:]))
                        o_ready.by(dve.tensor_tensor(o[u][:], o[u][:],
                                                     rden[u][:].rearrange("p (t o) -> p t o", o=1).to_broadcast([P, TPS, D]), ALU.mult))
                    for u in range(U):
                        job = ("y", u)
                        bk.wait_filled(dve, job, i)
                        bk.drain(dve.tensor_tensor(y[u][:], ps(job)[:].rearrange("p (t d) -> p t d", t=TPS),
                                                   b3[:].rearrange("p (o d) -> p o d", o=1).to_broadcast([P, TPS, D]), ALU.add), job)
                        bk.wait_read(dve, job, i)
                        xs = chip.x[:, bass.ds((i * U + u) * TPS, TPS), :]
                        c.link(dve.tensor_tensor(xs, xs, y[u][:], ALU.add))
                c.end()

            @block.scalar
            def _(act):
                with act.Fori(0, TURNS) as i:
                    for u in range(U):
                        mv_ready.wait(act, i, u)
                        std_ready.by(act.activation(std[u][:], mv[u][:, :, 1], ACT.Sqrt, bias=chip.ln_eps[:]))
                    for u in range(U):
                        bk.wait_filled(act, ("xT", u), i)
                        ins = act.copy(xnT[u][:], ps(("xT", u))[:])
                        bk.drain(ins, ("xT", u))
                    for u in range(U):
                        ss_ready.wait(act, i, u)
                        length_ready.by(act.activation(length[u][:], ss[u][:], ACT.Sqrt))
                    for u in range(U):
                        for n, dst in (("qT", qT), ("kT", kT)):
                            bk.wait_filled(act, (n, u), i)
                            bk.drain(act.copy(dst[u][:], ps((n, u))[:]), (n, u))
                    for u in range(U):
                        for t in range(TPS):
                            bk.wait_filled(act, ("s", u, t), i)
                            bk.drain(act.activation(E[u][:, t, :], ps(("s", u, t))[:], ACT.Exp), ("s", u, t))
                    for u in range(U):
                        bk.wait_filled(act, ("oT", u), i)
                        bk.drain(act.copy(oT[u][:], ps(("oT", u))[:]), ("oT", u))
                    for u in range(U):
                        bk.wait_filled(act, ("h1", u), i)
                        bk.drain(act.activation(h1[u][:], ps(("h1", u))[:], ACT.Relu, bias=b1[:]), ("h1", u))
                    for u in range(U):
                        for j in range(J):
                            bk.wait_filled(act, ("h2", u, j), i)
                            bk.drain(act.activation(h2[u][:, j, :], ps(("h2", u, j))[:], ACT.Relu, bias=b2[:, j:j + 1]), ("h2", u, j))

            @block.tensor
            def _(pe):
                bk.open(pe)
                pe.wait_ge(weights, 16 * (WEIGHTS + 2))
                with pe.Fori(0, TURNS) as i:
                    for u in range(U):
                        xn_ready.wait(pe, i, u)
                        bk.wait_drained(pe, ("xT", u), i)
                        for t in range(TPS):
                            ins = pe.transpose(ps(("xT", u))[:, t * P:(t + 1) * P], xn[u][:, t, :], chip.ident[:])
                        bk.fill(ins, ("xT", u))
                    for u in range(U):
                        bk.wait_read(pe, ("xT", u), i)
                        for t in range(TPS):
                            job = ("qkv", u, t)
                            bk.wait_drained(pe, job, i)
                            bk.fill(pe.matmul(ps(job)[:, 0:QKV], xnT[u][:, t * P:(t + 1) * P], w_qkv[:], start=True, stop=True), job)
                    for u in range(U):
                        qk_ready.wait(pe, i, u)
                        for n, nm in enumerate(("qT", "kT")):
                            bk.wait_drained(pe, (nm, u), i)
                            for t in range(TPS):
                                ins = pe.transpose(ps((nm, u))[:, t * P:(t + 1) * P], qk[u][:, t, n, :], chip.ident[:])
                            bk.fill(ins, (nm, u))
                    for u in range(U):
                        bk.wait_read(pe, ("qT", u), i)
                        bk.wait_read(pe, ("kT", u), i)
                        for t in range(TPS):
                            job = ("s", u, t)
                            bk.wait_drained(pe, job, i)
                            bk.fill(pe.matmul(ps(job)[:], kT[u][:, t * P:(t + 1) * P], qT[u][:], start=True, stop=True), job)
                    for u in range(U):
                        for t in range(TPS):
                            bk.wait_read(pe, ("s", u, t), i)
                        for t in range(TPS):
                            job = ("av", u, t)
                            bk.wait_drained(pe, job, i)
                            for k in range(TPS):
                                ins = pe.matmul(ps(job)[:, 0:D + 1], E[u][:, k, t * P:(t + 1) * P], qkv[u][:, k, QK:],
                                                start=(k == 0), stop=(k == TPS - 1))
                            bk.fill(ins, job)
                    for u in range(U):
                        o_ready.wait(pe, i, u)
                        bk.wait_drained(pe, ("oT", u), i)
                        for t in range(TPS):
                            ins = pe.transpose(ps(("oT", u))[:, t * P:(t + 1) * P], o[u][:, t, :], chip.ident[:])
                        bk.fill(ins, ("oT", u))
                    for u in range(U):
                        bk.wait_read(pe, ("oT", u), i)
                        bk.wait_drained(pe, ("h1", u), i)
                        bk.fill(pe.matmul(ps(("h1", u))[:], w1[:], oT[u][:], start=True, stop=True), ("h1", u))
                    for u in range(U):
                        bk.wait_read(pe, ("h1", u), i)
                        for j in range(J):
                            bk.wait_drained(pe, ("h2", u, j), i)
                            bk.fill(pe.matmul(ps(("h2", u, j))[:], w2[:, j * P:(j + 1) * P], h1[u][:], start=True, stop=True), ("h2", u, j))
                    for u in range(U):
                        job = ("y", u)
                        for j in range(J):
                            bk.wait_read(pe, ("h2", u, j), i)
                        bk.wait_drained(pe, job, i)
                        for t in range(TPS):
                            for j in range(J):
                                ins = pe.matmul(ps(job)[:, t * D:(t + 1) * D], h2[u][:, j, t * P:(t + 1) * P], w3[:, j, :],
                                                start=(j == 0), stop=(j == J - 1))
                        bk.fill(ins, job)



E8 = 8
F = 512
J = F // P


def seq_tiles(ap, i, u):
    return ap[:, bass.ds((i * U + u) * TPS, TPS), :]


def one_tile(ap, i, u, t):
    return ap[:, bass.ds((i * U + u) * TPS + t, 1), :].rearrange("p a d -> p (a d)")


def normalise_and_route(chip, ctx, L, w_router, vectors):
    nc = chip.nc
    NR = w_router.shape[1] if w_router is not None else 0
    loads = bool(NR) + len(vectors)
    xnT_all = chip.sb(ctx, f"{L}_xnT_all", [P, NT * P])
    cols = {n: chip.sb(ctx, f"{L}_{n}", [P, E8 * J]) for n in vectors}
    with ExitStack() as inner:
        sb = lambda name, shape: chip.sb(inner, f"{L}r_{name}", shape)
        two = lambda name, shape: [sb(f"{name}{u}", shape) for u in range(U)]
        sem = lambda name: chip.sem(f"{L}r_{name}")
        step = lambda name, n=1: Signal(sem(name), U * n)
        router = sb("router", [P, NR]) if NR else None
        rows = {n: sb(f"rows_{n}", [E8 * J, P]) for n in vectors}
        stats, mv = two("stats", [P, TPS, 6]), two("mv", [P, TPS, 2])
        std, rstd = two("std", [P, TPS]), two("rstd", [P, TPS])
        xn, xnT = two("xn", [P, TPS, D]), two("xnT", [P, S])
        bk = Banks(sem, "psum", [(("xT", u), 6 + u) for u in range(U)])
        ps = lambda job: chip.psum[bk.place[job][0]]
        loaded, cols_filled = sem("loaded"), sem("cols_filled")
        mv_ready, std_ready, xn_ready = step("mv_ready"), step("std_ready"), step("xn_ready")
        routed, copied = step("routed"), step("copied")
        dve_order = sem("dve_order")
        TURNS = B // U
        with nc.Block() as block:
            @block.sync
            def _(sp):
                if NR:
                    sp.dma_start(router[:], w_router).then_inc(loaded, 16)
                for n, v in vectors.items():
                    sp.dma_start(rows[n][:], v).then_inc(loaded, 16)

            @block.vector
            def _(dve):
                c = Chain(dve, dve_order, per_turn=U * 2)
                with dve.Fori(0, TURNS) as i:
                    c.start(i)
                    for u in range(U):
                        mv_ready.by(ln_statistics(chip, dve, c, lambda t: one_tile(chip.x, i, u, t), stats[u], mv[u], TPS))
                    for u in range(U):
                        std_ready.wait(dve, i, u)
                        c.link(dve.reciprocal(rstd[u][:], std[u][:]))
                        for t in range(TPS):
                            ins = dve.tensor_scalar(xn[u][:, t, :], one_tile(chip.x, i, u, t), mv[u][:, t, 0:1],
                                                    rstd[u][:, t:t + 1], ALU.subtract, ALU.mult)
                        xn_ready.by(ins)
                c.end()
                if vectors:
                    dve.wait_ge(cols_filled, 1)
                for n, v in enumerate(vectors):
                    dve.tensor_copy(cols[v][:], chip.psum[1][:, n * E8 * J:(n + 1) * E8 * J])

            @block.scalar
            def _(act):
                with act.Fori(0, TURNS) as i:
                    for u in range(U):
                        mv_ready.wait(act, i, u)
                        std_ready.by(act.activation(std[u][:], mv[u][:, :, 1], ACT.Sqrt, bias=chip.ln_eps[:]))
                    for u in range(U):
                        bk.wait_filled(act, ("xT", u), i)
                        bk.drain(act.copy(xnT[u][:], ps(("xT", u))[:]), ("xT", u))

            @block.gpsimd
            def _(pool):
                with pool.Fori(0, TURNS) as i:
                    for u in range(U):
                        bk.wait_read(pool, ("xT", u), i)
                        copied.by(pool.tensor_copy(xnT_all[:, bass.ds((i * U + u) * S, S)], xnT[u][:]))

            @block.tensor
            def _(pe):
                bk.open(pe)
                pe.sem_inc(copied.sem, U)
                if loads:
                    pe.wait_ge(loaded, 16 * loads)
                for n, v in enumerate(vectors):
                    ins = pe.transpose(chip.psum[1][:, n * E8 * J:(n + 1) * E8 * J], rows[v][:], chip.ident[0:E8 * J, 0:E8 * J])
                if vectors:
                    ins.then_inc(cols_filled, 1)
                with pe.Fori(0, TURNS) as i:
                    for u in range(U):
                        xn_ready.wait(pe, i, u)
                        copied.wait(pe, i, u)
                        bk.wait_drained(pe, ("xT", u), i)
                        for t in range(TPS):
                            ins = pe.transpose(ps(("xT", u))[:, t * P:(t + 1) * P], xn[u][:, t, :], chip.ident[:])
                        bk.fill(ins, ("xT", u))
                    for u in range(U if NR else 0):
                        bk.wait_read(pe, ("xT", u), i)
                        for t in range(TPS):
                            ins = pe.matmul(chip.psum[0][:, bass.ds(((i * U + u) * TPS + t) * NR, NR)],
                                            xnT[u][:, t * P:(t + 1) * P], router[:], start=True, stop=True)
                        routed.by(ins)
    return xnT_all, cols


def bcast(ap2, n_before=None, n_after=None):
    m = ap2.shape[1]
    if n_before:
        return ap2.rearrange("p (o m) -> p o m", o=1).to_broadcast([ap2.shape[0], n_before, m])
    return ap2.rearrange("p (m o) -> p m o", o=1).to_broadcast([ap2.shape[0], m, n_after])


def softmax_of_experts(chip, ctx, L, NR, bias, finish):
    pass


def route(chip, ctx, L, NR, bias, top=None, capacity=None, threshold=False, b2=None):
    nc = chip.nc
    gates = chip.sb(ctx, f"{L}_gates", [P, NT, E8])
    with ExitStack() as inner:
        sb = lambda name, shape, dt=F32: chip.sb(inner, f"{L}g_{name}", shape, dt)
        sem = lambda name: chip.sem(f"{L}g_{name}")
        logits, ex = sb("logits", [P, NT, NR]), sb("ex", [P, NT, E8])
        red, a, b = sb("red", [P, NT]), sb("a", [P, NT, E8]), sb("b", [P, NT, E8])
        probs = sb("probs", [P, NT, E8])
        bias_all = sb("bias_all", [P, NR])
        order8 = sb("order8", [P, E8])
        dve_order, shifted, exp_done, loaded = sem("dve_order"), sem("shifted"), sem("exp_done"), sem("loaded")
        turned, used, back, backed = sem("turned"), sem("used"), sem("back"), sem("backed")
        if capacity:
            R = B * E8
            rows, left, sel = sb("rows", [R, S]), sb("left", [R, S]), sb("sel", [R, S])
            best = sb("best", [R, 8])
            by_place = sb("by_place", [P, TPS, R])
        if b2 is not None:
            gT, b2_rows, z = sb("gT", [E8, B, S]), sb("b2_rows", [E8, D]), sb("z", [P, NT, D])
        per_e = lambda r: bcast(r[:], n_after=E8)
        with nc.Block() as block:
            @block.sync
            def _(sp):
                if bias is not None:
                    sp.dma_start(bias_all[:], bias.partition_broadcast(P)).then_inc(loaded, 16)
                if b2 is not None:
                    sp.dma_start(b2_rows[:], b2).then_inc(loaded, 16)

            @block.vector
            def _(dve):
                c = Chain(dve, dve_order)
                raw = chip.psum[0][:, 0:NT * NR].rearrange("p (t e) -> p t e", e=NR)
                if bias is not None:
                    dve.wait_ge(loaded, 16 * (1 + (b2 is not None)))
                    c.link(dve.tensor_tensor(logits[:], raw, bcast(bias_all[:], n_before=NT), ALU.add))
                else:
                    c.link(dve.tensor_copy(logits[:], raw))
                c.link(dve.tensor_reduce(red[:], logits[:, :, 0:E8], AX_X, ALU.max))
                dve.tensor_tensor(a[:], logits[:, :, 0:E8], per_e(red), ALU.subtract).then_inc(shifted, 1)
                dve.wait_ge(exp_done, 1)
                c.link(dve.tensor_reduce(red[:], ex[:], AX_X, ALU.add))
                c.link(dve.reciprocal(red[:], red[:]))
                c.link(dve.tensor_tensor(probs[:], ex[:], per_e(red), ALU.mult))
                if top:
                    for e in range(E8):
                        ins = dve.memset(order8[:, e:e + 1], float(E8 - e))
                    c.link(ins)
                    c.link(dve.tensor_copy(b[:], probs[:]))
                    for k in range(top):
                        c.link(dve.tensor_reduce(red[:], b[:], AX_X, ALU.max))
                        c.link(dve.tensor_tensor(a[:], b[:], per_e(red), ALU.is_equal))
                        c.link(dve.tensor_tensor(a[:], a[:], bcast(order8[:], n_before=NT), ALU.mult))
                        c.link(dve.tensor_reduce(red[:], a[:], AX_X, ALU.max))
                        c.link(dve.tensor_tensor(a[:], a[:], per_e(red), ALU.is_equal))
                        c.link(dve.scalar_tensor_tensor(b[:], a[:], -4.0, b[:], ALU.mult, ALU.add))
                    c.link(dve.tensor_scalar(a[:], b[:], -1.0, None, ALU.is_lt))
                    c.link(dve.tensor_tensor(gates[:], probs[:], a[:], ALU.mult))
                if threshold:
                    thr = logits[:, :, E8]
                    dve.wait_ge(exp_done, 2)
                    c.link(dve.tensor_scalar(red[:], thr, 0.125, None, ALU.mult))
                    c.link(dve.tensor_tensor(a[:], probs[:], per_e(red), ALU.subtract))
                    c.link(dve.tensor_scalar(b[:], a[:], 0.0, None, ALU.max))
                    c.link(dve.tensor_reduce(red[:], b[:], AX_X, ALU.add))
                    c.link(dve.scalar_tensor_tensor(red[:], red[:], 0.0, red[:], ALU.is_equal, ALU.add))
                    c.link(dve.reciprocal(red[:], red[:]))
                    c.link(dve.tensor_tensor(gates[:], b[:], per_e(red), ALU.mult))
                if capacity:
                    for t in range(TPS):
                        ins = dve.tensor_copy(by_place[:, t, :].rearrange("p (b e) -> p b e", e=E8),
                                              probs[:].rearrange("p (b t) e -> p b t e", t=TPS)[:, :, t, :])
                    c.link(ins)
                dve.sem_inc(turned, 1)
                if capacity:
                    dve.wait_ge(used, 1)
                    c.link(dve.tensor_copy(rows[:], chip.psum[1][0:R, :]))
                    c.link(dve.tensor_copy(left[:], rows[:]))
                    for k in range(capacity // 8):
                        c.link(dve.max(best[:], left[:]))
                        c.link(dve.match_replace(left[:], best[:], left[:], -1.0))
                    c.link(dve.scalar_tensor_tensor(sel[:], left[:], 0.0, rows[:], ALU.is_lt, ALU.mult))
                    dve.sem_inc(back, 1)
                    dve.wait_ge(backed, 1)
                    gv = gates[:].rearrange("p (b t) e -> p b t e", t=TPS)
                    for t in range(TPS):
                        dve.tensor_copy(gv[:, :, t, :], chip.psum[2][:, t * R:(t + 1) * R].rearrange("p (b e) -> p b e", e=E8))
                if b2 is not None:
                    for q in range(B):
                        dve.wait_ge(used, q + 1)
                        dve.tensor_copy(gT[:, q, :], chip.psum[q][0:E8, :]).then_inc(back, 1)
                    for q in range(B):
                        dve.wait_ge(backed, q + 1)
                        xs = chip.x[:, q * TPS:(q + 1) * TPS, :]
                        dve.tensor_tensor(xs, chip.psum[q][:].rearrange("p (t d) -> p t d", d=D), xs, ALU.add)

            @block.scalar
            def _(act):
                act.wait_ge(shifted, 1)
                act.activation(ex[:], a[:], ACT.Exp).then_inc(exp_done, 1)
                if threshold:
                    act.activation(logits[:, :, E8], logits[:, :, E8], ACT.Sigmoid).then_inc(exp_done, 1)

            @block.tensor
            def _(pe):
                pe.wait_ge(turned, 1)
                if capacity:
                    for t in range(TPS):
                        ins = pe.transpose(chip.psum[1][0:R, t * P:(t + 1) * P], by_place[:, t, :], chip.ident[:])
                    ins.then_inc(used, 1)
                    pe.wait_ge(back, 1)
                    for t in range(TPS):
                        ins = pe.transpose(chip.psum[2][:, t * R:(t + 1) * R], sel[:, t * P:(t + 1) * P], chip.ident[0:R, 0:R])
                    ins.then_inc(backed, 1)
                if b2 is not None:
                    for q in range(B):
                        for t in range(TPS):
                            ins = pe.transpose(chip.psum[q][0:E8, t * P:(t + 1) * P], gates[:, q * TPS + t, :], chip.ident[:])
                        ins.then_inc(used, 1)
                    for q in range(B):
                        pe.wait_ge(back, q + 1)
                        for t in range(TPS):
                            ins = pe.matmul(chip.psum[q][:, t * D:(t + 1) * D], gT[:, q, t * P:(t + 1) * P], b2_rows[:],
                                            start=True, stop=True)
                        ins.then_inc(backed, 1)
    return gates


def dense_experts(chip, L, xnT_all, gates, w_in, w_out, act_fn, b1=None, glu=None):
    nc = chip.nc
    CU = 2
    CT = B // CU
    with ExitStack() as ctx:
        sb = lambda name, shape: chip.sb(ctx, f"{L}e_{name}", shape)
        two = lambda name, shape: [sb(f"{name}{u}", shape) for u in range(2)]
        sem = lambda name: chip.sem(f"{L}e_{name}")
        w1, w2 = two("w1", [P, F]), two("w2", [P, J, D])
        h = two("h", [P, J, S])
        if glu:
            w_v, s_v, s_in, s_out = glu
            wv, so, w2s, g = two("wv", [P, F]), two("so", [P, D]), two("w2s", [P, J, D]), two("g", [P, J, S])
            order = [((n, u, j), base + (u * J + j) % 3) for u in range(2) for j in range(J) for n, base in (("h", 0), ("v", 3))]
        else:
            w2s = w2
            order = [(("h", u, j), j) for u in range(2) for j in range(J)]
        order += [(("y", u), 6 + u) for u in range(2)]
        bk = Banks(sem, "psum", order)
        ps = lambda job: chip.psum[bk.place[job][0]]
        loaded = [sem(f"weights_loaded{u}") for u in range(2)]
        scaled = sem("w_out_scaled")
        g_ready, h_read = sem("g_ready"), None
        NW = 2 + 2 * bool(glu)

        def load(sp, e, eh):
            one = lambda w: w[bass.ds(e, 1)]
            sp.dma_start(w1[eh][:], one(w_in).rearrange("e k f -> (e k) f")).then_inc(loaded[eh], 16)
            sp.dma_start(w2[eh][:], one(w_out).rearrange("e (j p) d -> p (e j) d", p=P)).then_inc(loaded[eh], 16)
            if glu:
                sp.dma_start(wv[eh][:], one(w_v).rearrange("e k f -> (e k) f")).then_inc(loaded[eh], 16)
                sp.dma_start(so[eh][:], one(s_out).rearrange("e o d -> (e o) d").partition_broadcast(P)
                             if False else s_out[bass.ds(e, 1)].rearrange("e o d -> (e o d)").partition_broadcast(P)).then_inc(loaded[eh], 16)

        with nc.Block() as block:
            @block.sync
            def _(sp):
                for eh in range(2):
                    load(sp, eh, eh)
                with sp.Fori(1, E8 // 2) as ep:
                    for eh in range(2):
                        bk.wait_filled(sp, ("y", 1), ((ep - 1) * 2 + eh) * CT + (CT - 1))
                        load(sp, ep * 2 + eh, eh)

            if glu:
                @block.gpsimd
                def _(pool):
                    with pool.Fori(0, E8 // 2) as ep:
                        for eh in range(2):
                            pool.wait_ge(loaded[eh], (ep + 1) * (16 * NW))
                            pool.tensor_tensor(w2s[eh][:], w2[eh][:], bcast(so[eh][:], n_before=J), ALU.mult).then_inc(scaled, 1)

            @block.scalar
            def _(act):
                with act.Fori(0, E8 // 2) as ep:
                    for eh in range(2):
                        with act.Fori(0, CT) as cp:
                            turn = (ep * 2 + eh) * CT + cp
                            for u in range(2):
                                for j in range(J):
                                    job = ("h", u, j)
                                    bk.wait_filled(act, job, turn)
                                    chip.apart(act)
                                    col = bass.ds((ep * 2 + eh) * J + j, 1)
                                    kw = {"bias": b1[:, col]} if b1 is not None else {}
                                    if glu:
                                        kw["scale"] = s_in[:, col]
                                    dst = g if glu else h
                                    bk.drain(act.activation(dst[u][:, j, :], ps(job)[:], act_fn, **kw), job)

            @block.vector
            def _(dve):
                with dve.Fori(0, E8 // 2) as ep:
                    for eh in range(2):
                        e = ep * 2 + eh
                        with dve.Fori(0, CT) as cp:
                            turn = e * CT + cp
                            if glu:
                                for u in range(2):
                                    for j in range(J):
                                        bk.wait_filled(dve, ("v", u, j), turn)
                                        bk.wait_read(dve, ("h", u, j), turn)
                                        bk.drain(dve.scalar_tensor_tensor(h[u][:, j, :], ps(("v", u, j))[:],
                                                                          s_v[:, bass.ds(e * J + j, 1)], g[u][:, j, :],
                                                                          ALU.mult, ALU.mult), ("v", u, j))
                            for u in range(2):
                                bk.wait_filled(dve, ("y", u), turn)
                                for t in range(TPS):
                                    tile = (cp * CU + u) * TPS + t
                                    xs = chip.x[:, bass.ds(tile, 1), :].rearrange("p a d -> p (a d)")
                                    gate = gates[:, bass.ds(tile, 1), bass.ds(e, 1)].rearrange("p a e -> p (a e)")
                                    ins = dve.scalar_tensor_tensor(xs, ps(("y", u))[:, t * D:(t + 1) * D], gate, xs,
                                                                   ALU.mult, ALU.add)
                                bk.drain(ins, ("y", u))

            @block.tensor
            def _(pe):
                bk.open(pe)
                with pe.Fori(0, E8 // 2) as ep:
                    for eh in range(2):
                        pe.wait_ge(loaded[eh], (ep + 1) * (16 * NW))
                        if glu:
                            pe.wait_ge(scaled, ep * 2 + (eh + 1))
                        chip.apart(pe)
                        with pe.Fori(0, CT) as cp:
                            turn = (ep * 2 + eh) * CT + cp
                            for u in range(2):
                                rhs = xnT_all[:, bass.ds((cp * CU + u) * S, S)]
                                for j in range(J):
                                    for n, w in (("h", w1),) + ((("v", wv),) if glu else ()):
                                        bk.wait_drained(pe, (n, u, j), turn)
                                        bk.fill(pe.matmul(ps((n, u, j))[:], w[eh][:, j * P:(j + 1) * P], rhs,
                                                          start=True, stop=True), (n, u, j))
                            for u in range(2):
                                for j in range(J):
                                    bk.wait_read(pe, ("v" if glu else "h", u, j), turn)
                                bk.wait_drained(pe, ("y", u), turn)
                                for t in range(TPS):
                                    for j in range(J):
                                        ins = pe.matmul(ps(("y", u))[:, t * D:(t + 1) * D], h[u][:, j, t * P:(t + 1) * P],
                                                        w2s[eh][:, j, :], start=(j == 0), stop=(j == J - 1))
                                bk.fill(ins, ("y", u))


def by_tile(ap):
    return ap.rearrange("e (j p) -> (e j) p", p=P)


def top2_glu_experts(chip, w):
    with ExitStack() as ctx:
        flat = lambda a: a.rearrange("e o f -> (e o) f")
        xnT, cols = normalise_and_route(chip, ctx, "l0f", w["router_w"], {"sv": by_tile(flat(w["sv"])), "s": by_tile(flat(w["s"]))})
        gates = route(chip, ctx, "l0f", E8, None, top=2)
        dense_experts(chip, "l0f", xnT, gates, w["w"], w["w1"], ACT.Gelu_apprx_tanh, glu=(w["wv"], cols["sv"], cols["s"], w["s1"]))


def switch_experts(chip, w):
    with ExitStack() as ctx:
        xnT, cols = normalise_and_route(chip, ctx, "l1f", w["Wr"], {"b1": by_tile(w["b1"])})
        gates = route(chip, ctx, "l1f", E8, w["br"], top=1, b2=w["b2"])
        dense_experts(chip, "l1f", xnT, gates, w["W1"], w["W2"], ACT.Relu, b1=cols["b1"])


def expert_choice_experts(chip, w):
    with ExitStack() as ctx:
        xnT, _ = normalise_and_route(chip, ctx, "l2f", w["gate_w"], {})
        gates = route(chip, ctx, "l2f", E8, None, capacity=2 * S // E8)
        dense_experts(chip, "l2f", xnT, gates, w["w1"], w["w2"], ACT.Gelu)


def threshold_experts(chip, w):
    with ExitStack() as ctx:
        xnT, cols = normalise_and_route(chip, ctx, "l3f", w["Wgt"], {"b1": by_tile(w["b1"])})
        gates = route(chip, ctx, "l3f", E8 + 1, w["bgt"], threshold=True, b2=w["b2"])
        dense_experts(chip, "l3f", xnT, gates, w["W1"], w["W2"], ACT.Gelu_apprx_tanh, b1=cols["b1"])


def normalise_all(chip, ctx, L):
    return normalise_and_route(chip, ctx, L, None, {})[0]



H3, DK3 = 16, 64
BUCKETS = 32


def relative_position_attention(chip, w):
    nc = chip.nc
    HP = H3 // 2
    UNITS = HP * B
    SPAN = 2 * S - 1
    GW = S + (TPS - 1) * P
    SCALE = float(H3) ** -0.5
    ctx = ExitStack()
    with ctx:
        sb = lambda name, shape: chip.sb(ctx, f"l3a_{name}", shape)
        two = lambda name, shape: [sb(f"{name}{u}", shape) for u in range(2)]
        sem = lambda name: chip.sem(f"l3a_{name}")
        xnT_all = normalise_all(chip, ctx, "l3a")
        by_distance = nc.dram_tensor("l3a_by_distance", (H3, SPAN + 1), F32, kind="Internal").ap()
        by_place = nc.dram_tensor("l3a_by_place", (H3, P, SPAN + 1), F32, kind="Internal").ap()

        w_qk, w_v, w_o = sb("w_qk", [P, 2, H3 * DK3]), sb("w_v", [P, H3 * DK3]), sb("w_o", [P, HP, D])
        xT, wqk = two("xT", [P, S]), two("wqk", [P, 2, P])
        q = two("q", [P, 2, S])
        kT = two("kT", [P, S])
        v = two("v", [P, TPS, 4, DK3])
        oT = two("oT", [P, S])
        bias = two("bias", [P, GW])
        sc, top, pT = two("sc", [P, TPS, S]), two("top", [P, TPS]), two("pT", [P, TPS, S])
        rden = sb("rden", [P, S])

        with ExitStack() as inner, nc.Block() as block:
            table = chip.sb(inner, "l3a_table", [BUCKETS, H3])
            onehot = chip.sb(inner, "l3a_onehot", [BUCKETS, SPAN + 1])
            line = chip.sb(inner, "l3a_line", [H3, SPAN + 1])
            loaded, summed, lined, stored = sem("table_loaded"), sem("summed"), sem("lined"), sem("line_stored")
            weights = sem("weights_loaded")

            @block.sync
            def _(sp):
                sp.dma_start(table[:], w["rel_bias"]).then_inc(loaded, 16)
                sp.dma_start(onehot[:], w["onehot"]).then_inc(loaded, 16)
                sp.wait_ge(lined, 2)
                sp.dma_start(by_distance, line[:]).then_inc(stored, 16)
                sp.wait_ge(stored, 16)
                for h in range(H3):
                    src = bass.AP(by_distance.tensor, h * (SPAN + 1), [[0, P], [1, SPAN + 1]])
                    sp.dma_start(by_place[h], src).then_inc(stored, 16)
                sp.wait_ge(stored, 16 * (1 + H3))

            @block.scalar
            def _(act):
                act.dma_start(w_qk[:, 0, :], w["Wq"]).then_inc(weights, 16)
                act.dma_start(w_qk[:, 1, :], w["Wk"]).then_inc(weights, 16)
                act.dma_start(w_v[:], w["Wv"]).then_inc(weights, 16)
                act.dma_start(w_o[:], w["Wo"].rearrange("(g p) d -> p g d", p=P)).then_inc(weights, 16)
                act.wait_ge(weights, 64)

            @block.tensor
            def _(pe):
                pe.wait_ge(loaded, 32)
                for c in range(2):
                    pe.matmul(chip.psum[c][0:H3, :], table[:], onehot[:, c * S:(c + 1) * S], start=True, stop=True).then_inc(summed, 1)

            @block.vector
            def _(dve):
                for u in range(2):
                    dve.memset(v[u][:, :, 1:3, :], 1.0)
                    dve.memset(q[u][DK3:, 0, :], 0.0)
                    dve.memset(q[u][0:DK3, 1, :], 0.0)
                dve.memset(oT[1][0:DK3, :], 0.0)
                dve.memset(v[1][:, 0, 3, :], 0.0)
                dve.memset(pT[1][:, 0, :], 1.0)
                for c in range(2):
                    dve.wait_ge(summed, c + 1)
                    dve.tensor_copy(line[:, c * S:(c + 1) * S], chip.psum[c][0:H3, :]).then_inc(lined, 1)

        order = [("q", 4), ("k", 4), ("v", 4), ("y", 5)]
        for hh in range(2):
            order += [(("s", hh, t), t % 2) for t in range(TPS)]
            order += [(("t", hh, t), 2 + t % 2) for t in range(TPS)]
            order += [(("av", hh), 6 + hh)]
        bk = Banks(sem, "psum", order)
        ps = lambda job: chip.psum[bk.place[job][0]]
        xT_ready, less_ready = Signal(sem("xT_ready"), 1), Signal(sem("less_ready"), 2)
        bias_loaded = [sem(f"bias_loaded{hh}") for hh in range(2)]
        dve_order = sem("dve_order")
        SEQ_BITS = B.bit_length() - 1
        pair = lambda g: (g >> SEQ_BITS) & (HP - 1)
        sequence = lambda g: g & (B - 1)
        rows = [slice(0, DK3), slice(DK3, P)]

        with nc.Block() as block:
            @block.sync
            def _(sp):
                def load(h, hh):
                    src = bass.AP(by_place.tensor, h * (P * (SPAN + 1)) + (P - 1), [[SPAN, P], [1, GW]])
                    sp.dma_start(bias[hh][:], src).then_inc(bias_loaded[hh], 16)

                for hh in range(2):
                    load(hh, hh)
                with sp.Fori(1, HP + 1) as hp:
                    for hh in range(2):
                        less_ready.wait(sp, hp * B - 1, hh)
                        chip.apart(sp)
                        load((hp & (HP - 1)) * 2 + hh, hh)
                for hh in range(2):
                    sp.wait_ge(bias_loaded[hh], 16 * (HP + 1))

            @block.gpsimd
            def _(pool):
                def prepare(g, u):
                    pool.tensor_copy(wqk[u][:], w_qk[:, :, bass.ds(pair(g) * P, P)])
                    xT_ready.by(pool.tensor_copy(xT[u][:], xnT_all[:, bass.ds(sequence(g) * S, S)]))

                prepare(0, 0)
                with pool.Fori(0, UNITS // 2) as i:
                    for u in range(2):
                        g = i * 2 + u
                        bk.wait_drained(pool, "v", g)
                        prepare(g + 1, 1 - u)

            @block.vector
            def _(dve):
                c = Chain(dve, dve_order, per_turn=2)

                def less_maximum(g, hh):
                    dve.wait_ge(bias_loaded[hh], ((g >> SEQ_BITS) + 1) * 16)
                    chip.apart(dve)
                    for t in range(TPS):
                        job = ("s", hh, t)
                        bk.wait_filled(dve, job, g)
                        chip.apart(dve)
                        b0 = (TPS - 1 - t) * P
                        bk.drain(dve.tensor_tensor_reduce(sc[hh][:, t, :], ps(job)[:], bias[hh][:, b0:b0 + S], 1.0, -3.0e38,
                                                          ALU.add, ALU.max, top[hh][:, t:t + 1]), job)
                    bk.wait_read(dve, ("s", hh, TPS - 2), g)
                    bk.wait_read(dve, ("s", hh, TPS - 1), g)
                    for t in range(TPS):
                        ins = dve.tensor_scalar(sc[hh][:, t, :], sc[hh][:, t, :], top[hh][:, t:t + 1], None, ALU.subtract)
                    less_ready.by(ins)

                def normalise(g, u, hh):
                    job = ("av", hh)
                    bk.wait_filled(dve, job, g)
                    c.link(dve.reciprocal(rden[rows[hh], :], ps(job)[rows[1 - hh], :]))
                    bk.drain(dve.tensor_tensor(oT[u][rows[hh], :], ps(job)[rows[hh], :], rden[rows[hh], :], ALU.mult), job)

                def add(g):
                    bk.wait_filled(dve, "y", g)
                    xs = chip.x[:, bass.ds(sequence(g + (B - 1)) * TPS, TPS), :]
                    bk.drain(dve.tensor_tensor(xs, ps("y")[:].rearrange("p (t d) -> p t d", t=TPS), xs, ALU.add), "y")

                less_maximum(0, 0)
                with dve.Fori(0, UNITS // 2) as i:
                    for u in range(2):
                        g = i * 2 + u
                        c.start(g)
                        less_maximum(g, 1)
                        normalise(g, 1 - u, 1)
                        add(g)
                        less_maximum(g + 1, 0)
                        normalise(g, u, 0)
                        c.end()
                c.start(UNITS)
                normalise(UNITS, 1, 1)
                add(UNITS)

            @block.scalar
            def _(act):
                def take(g, u, job):
                    bk.wait_filled(act, job, g)
                    a = ps(job)
                    if job == "q":
                        act.mul(q[u][rows[0], 0, :], a[rows[0], :], SCALE)
                        ins = act.mul(q[u][rows[1], 1, :], a[rows[1], :], SCALE)
                    elif job == "k":
                        ins = act.copy(kT[u][:], a[:])
                    else:
                        for hh in range(2):
                            ins = act.copy(v[u][:, :, 3 * hh, :], a[:].rearrange("p (t h d) -> p t h d", h=2, d=DK3)[:, :, hh, :])
                    bk.drain(ins, job)

                def exponentials(g, hh):
                    for t in range(TPS):
                        job = ("t", hh, t)
                        bk.wait_filled(act, job, g)
                        bk.drain(act.activation(pT[hh][:, t, :], ps(job)[:], ACT.Exp), job)

                for job in ("q", "k", "v"):
                    take(0, 0, job)
                with act.Fori(0, UNITS // 2) as i:
                    for u in range(2):
                        g = i * 2 + u
                        take(g + 1, 1 - u, "q")
                        exponentials(g, 0)
                        take(g + 1, 1 - u, "k")
                        take(g + 1, 1 - u, "v")
                        exponentials(g, 1)

            @block.tensor
            def _(pe):
                bk.open(pe)

                def project(g, u, job):
                    bk.wait_drained(pe, job, g)
                    if job == "v":
                        for t in range(TPS):
                            ins = pe.matmul(ps(job)[:, t * P:(t + 1) * P], xT[u][:, t * P:(t + 1) * P],
                                            w_v[:, bass.ds(pair(g) * P, P)], start=True, stop=True)
                    else:
                        xT_ready.wait(pe, g, 0)
                        ins = pe.matmul(ps(job)[:], wqk[u][:, int(job == "k"), :], xT[u][:], start=True, stop=True)
                    bk.fill(ins, job)

                def scores(g, u, hh):
                    bk.wait_read(pe, "k", g)
                    for t in range(TPS):
                        job = ("s", hh, t)
                        bk.wait_drained(pe, job, g)
                        bk.fill(pe.matmul(ps(job)[:], q[u][:, hh, t * P:(t + 1) * P], kT[u][:], start=True, stop=True), job)

                def turn_scores(g, hh):
                    less_ready.wait(pe, g, hh)
                    for kt in range(TPS):
                        job = ("t", hh, kt)
                        bk.wait_drained(pe, job, g)
                        for t in range(TPS):
                            ins = pe.transpose(ps(job)[:, t * P:(t + 1) * P], sc[hh][:, t, kt * P:(kt + 1) * P], chip.ident[:])
                        bk.fill(ins, job)

                def weigh(g, u, hh):
                    job = ("av", hh)
                    bk.wait_drained(pe, job, g + hh)
                    bk.wait_read(pe, "v", g)
                    for kt in range(TPS):
                        bk.wait_read(pe, ("t", hh, kt), g)
                        ins = pe.matmul(ps(job)[:], v[u][:, kt, 2 * hh:2 * hh + 2, :].rearrange("p a d -> p (a d)"),
                                        pT[hh][:, kt, :], start=(kt == 0), stop=(kt == TPS - 1))
                    bk.fill(ins, job)

                def answer(g, u):
                    bk.wait_read(pe, ("av", 0), g - 1)
                    bk.wait_read(pe, ("av", 1), g)
                    bk.wait_drained(pe, "y", g)
                    for t in range(TPS):
                        ins = pe.matmul(ps("y")[:, t * D:(t + 1) * D], oT[u][:, t * P:(t + 1) * P],
                                        w_o[:, bass.ds(pair(g + (UNITS - 1)), 1), :].rearrange("p a d -> p (a d)"), start=True, stop=True)
                    bk.fill(ins, "y")

                job = ("av", 1)
                bk.wait_drained(pe, job, 0)
                bk.fill(pe.matmul(ps(job)[:], v[1][:, 0, 2:4, :].rearrange("p a d -> p (a d)"), pT[1][:, 0, :], start=True, stop=True), job)
                for job in ("q", "k", "v"):
                    project(0, 0, job)
                scores(0, 0, 0)
                with pe.Fori(0, UNITS // 2) as i:
                    for u in range(2):
                        g = i * 2 + u
                        scores(g, u, 1)
                        project(g + 1, 1 - u, "q")
                        turn_scores(g, 0)
                        project(g + 1, 1 - u, "k")
                        weigh(g, u, 0)
                        answer(g, 1 - u)
                        scores(g + 1, 1 - u, 0)
                        project(g + 1, 1 - u, "v")
                        turn_scores(g, 1)
                        weigh(g, u, 1)
                answer(UNITS, 1)


def buckets_by_distance():
    half, exact = BUCKETS // 2, BUCKETS // 4
    hot = np.zeros((BUCKETS, 2 * S), np.float32)
    for n in range(2 * S - 1):
        far = abs(n - (S - 1))
        if far < exact:
            bucket = far
        else:
            bucket = exact
            while bucket < half - 1 and far * far >= exact * exact * 2 ** (bucket + 1 - exact):
                bucket += 1
        hot[bucket + half * (n > S - 1), n] = 1.0
    return hot



def feature_attention(chip, w):
    nc = chip.nc
    H, DH = 16, 8
    M = w["proj"].shape[1]
    HM = H * M
    NCH = HM // P
    HC = H // NCH
    DC = HC * DH
    CW = DC + HC
    DN = float(DH) ** -0.25
    RATIO = float(M) ** -0.5
    EPS = 1e-4
    HALF = TPS // 2
    ctx = ExitStack()
    with ctx:
        sb = lambda name, shape: chip.sb(ctx, f"l1a_{name}", shape)
        two = lambda name, shape: [sb(f"{name}{u}", shape) for u in range(U)]
        sem = lambda name: chip.sem(f"l1a_{name}")
        wq, wk, wv, wo, wfc = (sb(n, [P, D]) for n in ("wq", "wk", "wv", "wo", "wfc"))
        bq, bk_, bo = (sb(n, [P, 1]) for n in ("bq", "bk", "bo"))
        bv, bfc = sb("bv", [P, D]), sb("bfc", [P, D])
        proj, spread = sb("proj", [DH, M]), sb("spread", [DH, P])
        head_of, half_head, own = sb("head_of", [P, H]), sb("half_head", [P, H]), sb("own", [P, CW])
        feat = sb("feat", [P, H, M])
        stats, mv = two("stats", [P, TPS, 6]), two("mv", [P, TPS, 2])
        std, rstd = two("std", [P, TPS]), two("rstd", [P, TPS])
        xn, xnT = two("xn", [P, TPS, D]), two("xnT", [P, S])
        qk = [[sb(f"{n}{u}", [P, S]) for n in ("q", "k")] for u in range(U)]
        sqs = [[sb(f"{n}{u}", [P, S]) for n in ("qsq", "ksq")] for u in range(U)]
        v = two("v", [P, TPS, NCH, DC + 1])
        mq, mk = two("mq", [P, TPS, H]), two("mk", [P, TPS, H])
        dg, mkr = two("dg", [P, 2, TPS, H]), two("mkr", [P, H])
        mk1, mkd = two("mk1", [H, 1]), two("mkd", [H, H])
        f = [[sb(f"f{n}{u}", [P, TPS, H, M]) for n in "qk"] for u in range(U)]
        cx = two("cx", [P, NCH, CW])
        fT = two("fT", [P, NCH, S])
        rden, o, oT = two("rden", [P, TPS, NCH, HC]), two("o", [P, TPS, D]), two("oT", [P, S])
        hT, y = two("hT", [P, S]), two("y", [P, TPS, D])

        order = [(("xT", u), 6 + u) for u in range(U)]
        for u in range(U):
            order += [(("q", u), 6), (("k", u), 7), (("v", u), 4)]
        for u in range(U):
            order += [(("dg", u), 5)] + [(("f", u, n, c), 2 * n + c) for n in range(2) for c in range(2)]
            order += [(("mT", u), 4), (("mb", u), 5)]
        order += [(("cx", u), 4) for u in range(U)]
        order += [(("fT", u, c), 6 + c) for u in range(U) for c in range(NCH)]
        order += [(("o", u, c), c) for u in range(U) for c in range(2)]
        order += [(("oT", u), 2) for u in range(U)] + [(("hT", u), 3) for u in range(U)] + [(("y", u), 5) for u in range(U)]
        bk = Banks(sem, "psum", order)
        ps = lambda job: chip.psum[bk.place[job][0]]
        weights, feat_filled, feat_ready = sem("weights_loaded"), sem("feat_filled"), sem("feat_ready")
        step = lambda name, n=1: Signal(sem(name), U * n)
        mv_ready, std_ready, xn_ready = step("mv_ready"), step("std_ready"), step("xn_ready")
        qk_ready, sq_ready, shifted, f_exp, f_ready = (step("qk_ready", 2), step("sq_ready", 2), step("shifted", 2),
                                                       step("f_exp", 2), step("f_ready", 2))
        mkr_ready, mkd_ready, cx_ready, o_ready = step("mkr_ready"), step("mkd_ready"), step("cx_ready"), step("o_ready")
        dve_order = sem("dve_order")
        TURNS = B // U
        NWT = 5 + 3 + 2 + 2 + 3

        with nc.Block() as block:
            @block.sync
            def _(sp):
                for t, n in ((wq, "Wq"), (wk, "Wk"), (wv, "Wv"), (wo, "Wo"), (wfc, "Wfc"), (proj, "proj"), (spread, "spread"),
                             (head_of, "head_of"), (half_head, "half_head"), (own, "own")):
                    sp.dma_start(t[:], w[n]).then_inc(weights, 16)
                for t, n in ((bq, "bq"), (bk_, "bk"), (bo, "bo")):
                    sp.dma_start(t[:], w[n].rearrange("(p o) -> p o", o=1)).then_inc(weights, 16)
                for t, n in ((bv, "bv"), (bfc, "bfc")):
                    sp.dma_start(t[:], w[n].partition_broadcast(P)).then_inc(weights, 16)

            @block.vector
            def _(dve):
                c = Chain(dve, dve_order, per_turn=U * 10)
                for u in range(U):
                    dve.memset(v[u][:, :, :, DC:], 1.0)
                dve.wait_ge(weights, 16 * NWT)
                dve.wait_ge(feat_filled, 1)
                dve.tensor_tensor(feat[:], bcast(head_of[:], n_after=M), bcast(chip.psum[0][:, 0:M], n_before=H),
                                  ALU.mult).then_inc(feat_ready, 1)
                with dve.Fori(0, TURNS) as i:
                    c.start(i)
                    for u in range(U):
                        mv_ready.by(ln_statistics(chip, dve, c, lambda t: one_tile(chip.x, i, u, t), stats[u], mv[u], TPS))
                    for u in range(U):
                        std_ready.wait(dve, i, u)
                        c.link(dve.reciprocal(rstd[u][:], std[u][:]))
                        for t in range(TPS):
                            ins = dve.tensor_scalar(xn[u][:, t, :], one_tile(chip.x, i, u, t), mv[u][:, t, 0:1],
                                                    rstd[u][:, t:t + 1], ALU.subtract, ALU.mult)
                        xn_ready.by(ins)
                    for u in range(U):
                        for n, (nm, b_) in enumerate((("q", bq), ("k", bk_))):
                            bk.wait_filled(dve, (nm, u), i)
                            qk_ready.by(dve.tensor_scalar(qk[u][n][:], ps((nm, u))[:], b_[:], DN, ALU.add, ALU.mult))
                            qk_ready.wait(dve, i, 2 * u + n)
                            bk.drain(dve.tensor_tensor(sqs[u][n][:], qk[u][n][:], qk[u][n][:], ALU.mult), (nm, u))
                        bk.wait_filled(dve, ("v", u), i)
                        for c2 in range(NCH):
                            ins = dve.tensor_tensor(v[u][:, :, c2, 0:DC],
                                                    ps(("v", u))[:].rearrange("p (t c d) -> p t c d", t=TPS, c=NCH)[:, :, c2, :],
                                                    bcast(bv[:, c2 * DC:(c2 + 1) * DC], n_before=TPS), ALU.add)
                        bk.drain(ins, ("v", u))
                    for u in range(U):
                        bk.wait_filled(dve, ("dg", u), i)
                        bk.drain(dve.tensor_copy(dg[u][:], ps(("dg", u))[:, 0:2 * TPS * H].rearrange("p (n t h) -> p n t h", n=2, h=H)), ("dg", u))
                        bk.wait_read(dve, ("dg", u), i)
                        for n, m in ((0, mq), (1, mk)):
                            for c2 in range(2):
                                bk.wait_filled(dve, ("f", u, n, c2), i)
                                fp = ps(("f", u, n, c2))[:].rearrange("p (t h m) -> p t h m", t=HALF, h=H)
                                c.link(dve.tensor_reduce(m[u][:, c2 * HALF:(c2 + 1) * HALF, :], fp, AX_X, ALU.max))
                        mkr_ready.by(dve.tensor_reduce(mkr[u][:], mk[u][:].rearrange("p t h -> p h t"), AX_X, ALU.max))
                        c.link(dve.tensor_tensor(mq[u][:], mq[u][:], dg[u][:, 0], ALU.add))
                        for c2 in range(2):
                            fp = ps(("f", u, 0, c2))[:].rearrange("p (t m) -> p t m", m=M)
                            ts = slice(c2 * HALF, (c2 + 1) * HALF)
                            ins = dve.tensor_tensor(f[u][0][:, ts].rearrange("p t h m -> p (t h) m"), fp,
                                                    bcast(mq[u][:, ts].rearrange("p t h -> p (t h)"), n_after=M), ALU.subtract)
                            bk.drain(ins, ("f", u, 0, c2))
                        bk.wait_read(dve, ("f", u, 0, 1), i)
                        dve.sem_inc(shifted.sem, 1)
                        bk.wait_filled(dve, ("mT", u), i)
                        ins = dve.tensor_reduce(mk1[u][:], ps(("mT", u))[0:H, 0:P], AX_X, ALU.max)
                        bk.drain(ins, ("mT", u))
                        bk.wait_read(dve, ("mT", u), i)
                        mkd_ready.by(dve.tensor_scalar(mkd[u][:], chip.ident[0:H, 0:H], mk1[u][:], None, ALU.mult))
                        bk.wait_filled(dve, ("mb", u), i)
                        ins = dve.tensor_tensor(mk[u][:], dg[u][:, 1], bcast(ps(("mb", u))[:, 0:H], n_before=TPS), ALU.add)
                        bk.drain(ins, ("mb", u))
                        bk.wait_read(dve, ("mb", u), i)
                        for c2 in range(2):
                            fp = ps(("f", u, 1, c2))[:].rearrange("p (t m) -> p t m", m=M)
                            ts = slice(c2 * HALF, (c2 + 1) * HALF)
                            ins = dve.tensor_tensor(f[u][1][:, ts].rearrange("p t h m -> p (t h) m"), fp,
                                                    bcast(mk[u][:, ts].rearrange("p t h -> p (t h)"), n_after=M), ALU.subtract)
                            bk.drain(ins, ("f", u, 1, c2))
                        bk.wait_read(dve, ("f", u, 1, 1), i)
                        dve.sem_inc(shifted.sem, 1)
                    for u in range(U):
                        for n in range(2):
                            f_exp.wait(dve, i, 2 * u + n)
                            f_ready.by(dve.tensor_scalar(f[u][n][:], f[u][n][:], EPS, RATIO, ALU.add, ALU.mult))
                    for u in range(U):
                        bk.wait_filled(dve, ("cx", u), i)
                        for c2 in range(NCH):
                            a = ps(("cx", u))[:, c2 * (DC + 1):(c2 + 1) * (DC + 1)]
                            dve.tensor_tensor(cx[u][:, c2, 0:DC], a[:, 0:DC], own[:, 0:DC], ALU.mult)
                            ins = dve.tensor_tensor(cx[u][:, c2, DC:], a[:, DC:].to_broadcast([P, HC]), own[:, DC:], ALU.mult)
                        bk.drain(ins, ("cx", u))
                    for u in range(U):
                        for c2 in range(2):
                            job = ("o", u, c2)
                            bk.wait_filled(dve, job, i)
                            a = ps(job)[:, 0:HALF * NCH * CW].rearrange("p (t w) -> p t w", w=CW)
                            rd = rden[u][:, c2 * HALF:(c2 + 1) * HALF].rearrange("p t c h -> p (t c) h")
                            c.link(dve.reciprocal(rd, a[:, :, DC:]))
                            for k in range(HALF * NCH):
                                t, ch = c2 * HALF + k // NCH, k % NCH
                                ins = dve.tensor_tensor(o[u][:, t, ch * DC:(ch + 1) * DC].rearrange("p (h d) -> p h d", d=DH),
                                                        a[:, k, 0:DC].rearrange("p (h d) -> p h d", d=DH),
                                                        bcast(rd[:, k, :], n_after=DH), ALU.mult)
                            bk.drain(ins, job)
                    for u in range(U):
                        job = ("y", u)
                        bk.wait_filled(dve, job, i)
                        ins = dve.tensor_tensor(y[u][:], ps(job)[:].rearrange("p (t d) -> p t d", t=TPS), bcast(bfc[:], n_before=TPS), ALU.add)
                        bk.drain(ins, job)
                        bk.wait_read(dve, job, i)
                        xs = seq_tiles(chip.x, i, u)
                        c.link(dve.scalar_tensor_tensor(xs, y[u][:], 0.0, xs, ALU.max, ALU.add))
                c.end()

            @block.scalar
            def _(act):
                act.wait_ge(weights, 16 * NWT)
                with act.Fori(0, TURNS) as i:
                    for u in range(U):
                        mv_ready.wait(act, i, u)
                        std_ready.by(act.activation(std[u][:], mv[u][:, :, 1], ACT.Sqrt, bias=chip.ln_eps[:]))
                    for u in range(U):
                        bk.wait_filled(act, ("xT", u), i)
                        bk.drain(act.copy(xnT[u][:], ps(("xT", u))[:]), ("xT", u))
                    for u in range(U):
                        for n in range(2):
                            shifted.wait(act, i, 2 * u + n)
                            f_exp.by(act.activation(f[u][n][:], f[u][n][:], ACT.Exp))
                    for u in range(U):
                        for c2 in range(NCH):
                            bk.wait_filled(act, ("fT", u, c2), i)
                            bk.drain(act.copy(fT[u][:, c2, :], ps(("fT", u, c2))[:]), ("fT", u, c2))
                    for u in range(U):
                        bk.wait_filled(act, ("oT", u), i)
                        bk.drain(act.copy(oT[u][:], ps(("oT", u))[:]), ("oT", u))
                    for u in range(U):
                        bk.wait_filled(act, ("hT", u), i)
                        bk.drain(act.activation(hT[u][:], ps(("hT", u))[:], ACT.Identity, bias=bo[:]), ("hT", u))

            @block.tensor
            def _(pe):
                bk.open(pe)
                pe.wait_ge(weights, 16 * NWT)
                pe.matmul(chip.psum[0][:, 0:M], spread[:], proj[:], start=True, stop=True).then_inc(feat_filled, 1)
                pe.wait_ge(feat_ready, 1)
                chip.apart(pe)
                with pe.Fori(0, TURNS) as i:
                    for u in range(U):
                        xn_ready.wait(pe, i, u)
                        bk.wait_drained(pe, ("xT", u), i)
                        for t in range(TPS):
                            ins = pe.transpose(ps(("xT", u))[:, t * P:(t + 1) * P], xn[u][:, t, :], chip.ident[:])
                        bk.fill(ins, ("xT", u))
                    for u in range(U):
                        bk.wait_read(pe, ("xT", u), i)
                        for nm, wt in (("q", wq), ("k", wk)):
                            bk.wait_drained(pe, (nm, u), i)
                            bk.fill(pe.matmul(ps((nm, u))[:], wt[:], xnT[u][:], start=True, stop=True), (nm, u))
                        bk.wait_drained(pe, ("v", u), i)
                        for t in range(TPS):
                            ins = pe.matmul(ps(("v", u))[:, t * D:(t + 1) * D], xnT[u][:, t * P:(t + 1) * P], wv[:], start=True, stop=True)
                        bk.fill(ins, ("v", u))
                    for u in range(U):
                        bk.wait_read(pe, ("k", u), i)
                        bk.wait_drained(pe, ("dg", u), i)
                        for n in range(2):
                            for t in range(TPS):
                                ins = pe.matmul(ps(("dg", u))[:, (n * TPS + t) * H:(n * TPS + t + 1) * H],
                                                sqs[u][n][:, t * P:(t + 1) * P], half_head[:], start=True, stop=True)
                        bk.fill(ins, ("dg", u))
                        for n in range(2):
                            for c2 in range(2):
                                job = ("f", u, n, c2)
                                bk.wait_drained(pe, job, i)
                                for tt in range(HALF):
                                    t = c2 * HALF + tt
                                    ins = pe.matmul(ps(job)[:, tt * HM:(tt + 1) * HM], qk[u][n][:, t * P:(t + 1) * P],
                                                    feat[:].rearrange("p h m -> p (h m)"), start=True, stop=True)
                                bk.fill(ins, job)
                        mkr_ready.wait(pe, i, u)
                        bk.wait_drained(pe, ("mT", u), i)
                        bk.fill(pe.transpose(ps(("mT", u))[0:H, 0:P], mkr[u][:], chip.ident[:]), ("mT", u))
                        mkd_ready.wait(pe, i, u)
                        bk.wait_drained(pe, ("mb", u), i)
                        bk.fill(pe.matmul(ps(("mb", u))[:, 0:H], chip.ones[0:H, :], mkd[u][:], start=True, stop=True), ("mb", u))
                    for u in range(U):
                        f_ready.wait(pe, i, 2 * u + 1)
                        bk.wait_read(pe, ("v", u), i)
                        bk.wait_drained(pe, ("cx", u), i)
                        for c2 in range(NCH):
                            for t in range(TPS):
                                ins = pe.matmul(ps(("cx", u))[:, c2 * (DC + 1):(c2 + 1) * (DC + 1)],
                                                f[u][1][:, t, c2 * HC:(c2 + 1) * HC, :].rearrange("p h m -> p (h m)"),
                                                v[u][:, t, c2, :], start=(t == 0), stop=(t == TPS - 1))
                        bk.fill(ins, ("cx", u))
                    for u in range(U):
                        f_ready.wait(pe, i, 2 * u)
                        for c2 in range(NCH):
                            bk.wait_drained(pe, ("fT", u, c2), i)
                            for t in range(TPS):
                                ins = pe.transpose(ps(("fT", u, c2))[:, t * P:(t + 1) * P],
                                                   f[u][0][:, t, c2 * HC:(c2 + 1) * HC, :].rearrange("p h m -> p (h m)"), chip.ident[:])
                            bk.fill(ins, ("fT", u, c2))
                    for u in range(U):
                        bk.wait_read(pe, ("cx", u), i)
                        for c2 in range(NCH):
                            bk.wait_read(pe, ("fT", u, c2), i)
                        for c2 in range(2):
                            job = ("o", u, c2)
                            bk.wait_drained(pe, job, i)
                            for k in range(HALF * NCH):
                                t, ch = c2 * HALF + k // NCH, k % NCH
                                ins = pe.matmul(ps(job)[:, k * CW:(k + 1) * CW], fT[u][:, ch, t * P:(t + 1) * P], cx[u][:, ch, :],
                                                start=True, stop=True)
                            bk.fill(ins, job)
                    for u in range(U):
                        for c2 in range(2):
                            bk.wait_read(pe, ("o", u, c2), i)
                        bk.wait_drained(pe, ("oT", u), i)
                        for t in range(TPS):
                            ins = pe.transpose(ps(("oT", u))[:, t * P:(t + 1) * P], o[u][:, t, :], chip.ident[:])
                        bk.fill(ins, ("oT", u))
                    for u in range(U):
                        bk.wait_read(pe, ("oT", u), i)
                        bk.wait_drained(pe, ("hT", u), i)
                        bk.fill(pe.matmul(ps(("hT", u))[:], wo[:], oT[u][:], start=True, stop=True), ("hT", u))
                    for u in range(U):
                        bk.wait_read(pe, ("hT", u), i)
                        bk.wait_drained(pe, ("y", u), i)
                        for t in range(TPS):
                            ins = pe.matmul(ps(("y", u))[:, t * D:(t + 1) * D], hT[u][:, t * P:(t + 1) * P], wfc[:], start=True, stop=True)
                        bk.fill(ins, ("y", u))



def selective_scan(chip, w):
    nc = chip.nc
    DI, N, R = 256, 16, 8
    CH = DI // P
    TAPS = 4
    ctx = ExitStack()
    with ctx:
        sb = lambda name, shape: chip.sb(ctx, f"l2a_{name}", shape)
        two = lambda name, shape: [sb(f"{name}{u}", shape) for u in range(U)]
        sem = lambda name: chip.sem(f"l2a_{name}")
        w_in, w_x, w_dt, w_out = sb("w_in", [P, 2 * DI]), sb("w_x", [P, CH, R + 2 * N]), sb("w_dt", [R, DI]), sb("w_out", [P, CH, D])
        ln_w, ln_b = sb("ln_w", [P, 1]), sb("ln_b", [P, 1])
        conv_w, conv_b, b_dt, d_par = sb("conv_w", [P, CH, TAPS]), sb("conv_b", [P, CH]), sb("b_dt", [P, CH]), sb("d_par", [P, CH])
        a_log, a_neg = sb("a_log", [P, CH, N]), sb("a_neg", [P, CH, N])
        pick = sb("pick", [N, N, P])
        stats, mv = two("stats", [P, TPS, 6]), two("mv", [P, TPS, 2])
        std, rstd = two("std", [P, TPS]), two("rstd", [P, TPS])
        stats2, mv2 = two("stats2", [P, TPS, 6]), two("mv2", [P, TPS, 2])
        std2, rstd2 = two("std2", [P, TPS]), two("rstd2", [P, TPS])
        xn, xm, xmT = two("xn", [P, TPS, D]), two("xm", [P, TPS, D]), two("xmT", [P, S])
        xi = two("xi", [P, CH, S + TAPS - 1])
        conv, xc, sz = two("conv", [P, CH, S]), two("xc", [P, CH, S]), two("sz", [P, CH, S])
        dtr, bT, cT = two("dtr", [R, S]), two("bT", [N, S]), two("cT", [N, S])
        sp_a, sp_r = sb("sp_a", [P, CH, S]), sb("sp_r", [P, CH, S])
        dt, du = two("dt", [P, CH, S]), two("du", [P, CH, S])
        yT = two("yT", [P, CH, S])
        NB = 2
        dA = [sb(f"dA{n}", [P, CH, S]) for n in range(NB)]
        dBu = [sb(f"dBu{n}", [P, CH, S]) for n in range(NB)]
        h = [sb(f"h{n}", [P, CH * S]) for n in range(NB)]
        hc = [sb(f"hc{n}", [P, CH, S]) for n in range(NB)]

        rest = lambda u: ([(("xT", u), 6)] + [(("in", u, j), 6 + (j + 1) % 2) for j in range(2 * CH)] +
                          [(("dtr", u), 7), (("bT", u), 6), (("cT", u), 7)] + [(("dt", u, j), 6 + j) for j in range(CH)])
        order = []
        for u in range(U):
            order += rest(u)
            for n in range(N):
                order += [(("B", u, n), n % 2), (("C", u, n), 2 + n % 2)]
            order += [(("y", u, j), 4 + j) for j in range(CH)] + [(("out", u), 6)]
        bk = Banks(sem, "psum", order)
        ps = lambda job: chip.psum[bk.place[job][0]]
        weights, a_ready, zeroed = sem("weights_loaded"), sem("a_ready"), sem("zeroed")
        step = lambda name, n=1: Signal(sem(name), U * n)
        mv_ready, std_ready, mv2_ready, std2_ready, xm_ready = (step("mv_ready"), step("std_ready"), step("mv2_ready"),
                                                                step("std2_ready"), step("xm_ready"))
        conv_ready, xc_ready, dt_exp, dt_ready = step("conv_ready"), step("xc_ready"), step("dt_exp", CH), step("dt_ready")
        dA_ready, dBu_ready, h_ready, hc_ready = step("dA_ready", N), step("dBu_ready", N), step("h_ready", N), step("hc_ready", N)
        hc_summed, yT_ready = step("hc_summed", N), step("yT_ready")
        dve_order, act_order = sem("dve_order"), sem("act_order")
        TURNS = B // U
        NWT = 3 + CH * 5 + 2 + 1 + CH

        with nc.Block() as block:
            @block.sync
            def _(sp):
                sp.dma_start(w_in[:], w["W_in"]).then_inc(weights, 16)
                sp.dma_start(w_dt[:], w["W_dt"]).then_inc(weights, 16)
                sp.dma_start(pick[:], w["pick"]).then_inc(weights, 16)
                sp.dma_start(w_out[:], w["W_out"].rearrange("(c p) d -> p c d", p=P)).then_inc(weights, 16)
                col = lambda a: a.rearrange("(p o) -> p o", o=1)
                sp.dma_start(ln_w[:], col(w["ln_w"])).then_inc(weights, 16)
                sp.dma_start(ln_b[:], col(w["ln_b"])).then_inc(weights, 16)
                for c in range(CH):
                    rows = slice(c * P, (c + 1) * P)
                    sp.dma_start(w_x[:, c, :], w["W_xproj"][rows, :]).then_inc(weights, 16)
                    sp.dma_start(conv_w[:, c, :], w["conv_w"][rows, 0, :]).then_inc(weights, 16)
                    sp.dma_start(a_log[:, c, :], w["A_log"][rows, :]).then_inc(weights, 16)
                    for t, n in ((conv_b, "conv_b"), (b_dt, "b_dt"), (d_par, "D_param")):
                        sp.dma_start(t[:, c:c + 1], col(w[n][rows])).then_inc(weights, 16)

            @block.gpsimd
            def _(pool):
                for n in range(NB):
                    pool.memset(dA[n][:, :, 0:1], 0.0)
                for u in range(U):
                    ins = pool.memset(xi[u][:, :, 0:TAPS - 1], 0.0)
                ins.then_inc(zeroed, 1)

            @block.scalar
            def _(act):
                act.wait_ge(weights, 16 * NWT)
                act.wait_ge(zeroed, 1)
                act.activation(a_neg[:], a_log[:], ACT.Exp).then_inc(a_ready, 1)
                act.wait_ge(a_ready, 1)
                act.mul(a_neg[:], a_neg[:], -1.0).then_inc(a_ready, 1)
                act.wait_ge(a_ready, 2)
                c = Chain(act, act_order, per_turn=U * CH * 2)
                with act.Fori(0, TURNS) as i:
                    c.start(i)
                    for u in range(U):
                        mv_ready.wait(act, i, u)
                        std_ready.by(act.activation(std[u][:], mv[u][:, :, 1], ACT.Sqrt, bias=chip.ln_eps[:]))
                        mv2_ready.wait(act, i, u)
                        std2_ready.by(act.activation(std2[u][:], mv2[u][:, :, 1], ACT.Sqrt, bias=chip.ln_eps[:]))
                        bk.wait_filled(act, ("xT", u), i)
                        bk.drain(act.activation(xmT[u][:], ps(("xT", u))[:], ACT.Identity, bias=ln_b[:], scale=ln_w[:]), ("xT", u))
                        for j in range(CH):
                            bk.wait_filled(act, ("in", u, j), i)
                            bk.drain(act.copy(xi[u][:, j, TAPS - 1:], ps(("in", u, j))[:]), ("in", u, j))
                        for j in range(CH):
                            bk.wait_filled(act, ("in", u, CH + j), i)
                            bk.drain(act.activation(sz[u][:, j, :], ps(("in", u, CH + j))[:], ACT.Silu), ("in", u, CH + j))
                        conv_ready.wait(act, i, u)
                        for j in range(CH):
                            ins = act.activation(xc[u][:, j, :], conv[u][:, j, :], ACT.Silu, bias=conv_b[:, j:j + 1])
                        xc_ready.by(ins)
                        for nm, t in (("dtr", dtr), ("bT", bT), ("cT", cT)):
                            bk.wait_filled(act, (nm, u), i)
                            bk.drain(act.copy(t[u][:], ps((nm, u))[0:t[u].shape[0], :]), (nm, u))
                        for j in range(CH):
                            bk.wait_read(act, ("dt", u, j), i)
                            c.link(act.activation(sp_a[:, j, :], sp_r[:, j, :], ACT.Abs))
                            c.link(act.activation(sp_a[:, j, :], sp_a[:, j, :], ACT.Exp, scale=-1.0))
                            dt_exp.by(act.activation(sp_a[:, j, :], sp_a[:, j, :], ACT.Ln, bias=1.0))
                        dt_ready.wait(act, i, u)
                        for n in range(N):
                            if n >= NB:
                                h_ready.wait(act, i, u * N + n - NB)
                            for j in range(CH):
                                ins = act.activation(dA[n % NB][:, j, 1:], dt[u][:, j, 1:], ACT.Exp, scale=a_neg[:, j, n:n + 1])
                            dA_ready.by(ins)
                c.end()

            @block.vector
            def _(dve):
                dve.wait_ge(weights, 16 * NWT)
                c = Chain(dve, dve_order, per_turn=U * (5 + CH * (TAPS - 1) + 2))
                with dve.Fori(0, TURNS) as i:
                    c.start(i)
                    for u in range(U):
                        mv_ready.by(ln_statistics(chip, dve, c, lambda t: one_tile(chip.x, i, u, t), stats[u], mv[u], TPS))
                        std_ready.wait(dve, i, u)
                        c.link(dve.reciprocal(rstd[u][:], std[u][:]))
                        for t in range(TPS):
                            ins = dve.tensor_scalar(xn[u][:, t, :], one_tile(chip.x, i, u, t), mv[u][:, t, 0:1],
                                                    rstd[u][:, t:t + 1], ALU.subtract, ALU.mult)
                        c.link(ins)
                        mv2_ready.by(ln_statistics(chip, dve, c, lambda t: xn[u][:, t, :], stats2[u], mv2[u], TPS))
                        std2_ready.wait(dve, i, u)
                        c.link(dve.reciprocal(rstd2[u][:], std2[u][:]))
                        for t in range(TPS):
                            ins = dve.tensor_scalar(xm[u][:, t, :], xn[u][:, t, :], mv2[u][:, t, 0:1],
                                                    rstd2[u][:, t:t + 1], ALU.subtract, ALU.mult)
                        xm_ready.by(ins)
                        for j in range(CH):
                            bk.wait_read(dve, ("in", u, j), i)
                            c.link(dve.tensor_scalar(conv[u][:, j, :], xi[u][:, j, 0:S], conv_w[:, j, 0:1], None, ALU.mult))
                            for k in range(1, TAPS):
                                ins = dve.scalar_tensor_tensor(conv[u][:, j, :], xi[u][:, j, k:k + S], conv_w[:, j, k:k + 1],
                                                               conv[u][:, j, :], ALU.mult, ALU.add)
                                if k < TAPS - 1:
                                    c.link(ins)
                        conv_ready.by(ins)
                        for j in range(CH):
                            bk.wait_filled(dve, ("dt", u, j), i)
                            bk.drain(dve.tensor_scalar(sp_r[:, j, :], ps(("dt", u, j))[:], b_dt[:, j:j + 1], None, ALU.add), ("dt", u, j))
                            bk.wait_read(dve, ("dt", u, j), i)
                        for j in range(CH):
                            dt_exp.wait(dve, i, u * CH + j)
                        ins = dve.scalar_tensor_tensor(dt[u][:], sp_r[:], 0.0, sp_a[:], ALU.max, ALU.add)
                        dt_ready.by(ins)
                        dt_ready.wait(dve, i, u)
                        xc_ready.wait(dve, i, u)
                        c.link(dve.tensor_tensor(du[u][:], dt[u][:], xc[u][:], ALU.mult))
                        for n in range(N):
                            q = n % NB
                            bk.wait_filled(dve, ("B", u, n), i)
                            ins = dve.tensor_tensor(dBu[q][:], du[u][:], bcast(ps(("B", u, n))[:], n_before=CH), ALU.mult)
                            bk.drain(ins, ("B", u, n))
                            bk.wait_read(dve, ("B", u, n), i)
                            dA_ready.wait(dve, i, u * N + n)
                            h_ready.by(dve.tensor_tensor_scan(h[q][:], dA[q][:].rearrange("p c s -> p (c s)"),
                                                              dBu[q][:].rearrange("p c s -> p (c s)"), 0.0, ALU.mult, ALU.add))
                            bk.wait_filled(dve, ("C", u, n), i)
                            h_ready.wait(dve, i, u * N + n)
                            if n >= NB:
                                hc_summed.wait(dve, i, u * N + n - NB)
                            ins = dve.tensor_tensor(hc[q][:], h[q][:].rearrange("p (c s) -> p c s", c=CH), bcast(ps(("C", u, n))[:], n_before=CH), ALU.mult)
                            bk.drain(ins, ("C", u, n))
                        for j in range(CH):
                            bk.wait_filled(dve, ("y", u, j), i)
                            ins = dve.scalar_tensor_tensor(yT[u][:, j, :], xc[u][:, j, :], d_par[:, j:j + 1], ps(("y", u, j))[:], ALU.mult, ALU.add)
                            bk.drain(ins, ("y", u, j))
                        for j in range(CH):
                            bk.wait_read(dve, ("y", u, j), i)
                        yT_ready.by(dve.tensor_tensor(yT[u][:], yT[u][:], sz[u][:], ALU.mult))
                        xs = seq_tiles(chip.x, i, u)
                        c.link(dve.tensor_tensor(xs, xs, xn[u][:], ALU.add))
                        bk.wait_filled(dve, ("out", u), i)
                        ins = dve.tensor_tensor(xs, ps(("out", u))[:].rearrange("p (t d) -> p t d", t=TPS), xs, ALU.add)
                        bk.drain(ins, ("out", u))
                c.end()

            @block.tensor
            def _(pe):
                bk.open(pe)
                pe.wait_ge(weights, 16 * NWT)

                def one(job, i, *mms):
                    bk.wait_drained(pe, job, i)
                    for k, (out, lhsT, rhs) in enumerate(mms):
                        ins = pe.matmul(out, lhsT, rhs, start=(k == 0), stop=(k == len(mms) - 1))
                    bk.fill(ins, job)

                with pe.Fori(0, TURNS) as i:
                    for u in range(U):
                        xm_ready.wait(pe, i, u)
                        bk.wait_drained(pe, ("xT", u), i)
                        for t in range(TPS):
                            ins = pe.transpose(ps(("xT", u))[:, t * P:(t + 1) * P], xm[u][:, t, :], chip.ident[:])
                        bk.fill(ins, ("xT", u))
                        bk.wait_read(pe, ("xT", u), i)
                        for j in range(2 * CH):
                            one(("in", u, j), i, (ps(("in", u, j))[:], w_in[:, j * P:(j + 1) * P], xmT[u][:]))
                        xc_ready.wait(pe, i, u)
                        for nm, a, m in (("dtr", 0, R), ("bT", R, N), ("cT", R + N, N)):
                            one((nm, u), i, *((ps((nm, u))[0:m, :], w_x[:, j, a:a + m], xc[u][:, j, :]) for j in range(CH)))
                        bk.wait_read(pe, ("dtr", u), i)
                        for j in range(CH):
                            one(("dt", u, j), i, (ps(("dt", u, j))[:], w_dt[:, j * P:(j + 1) * P], dtr[u][:]))
                        bk.wait_read(pe, ("bT", u), i)
                        bk.wait_read(pe, ("cT", u), i)

                        def spread(n):
                            one(("B", u, n), i, (ps(("B", u, n))[:], pick[:, n, :], bT[u][:]))
                            one(("C", u, n), i, (ps(("C", u, n))[:], pick[:, n, :], cT[u][:]))

                        spread(0)
                        for j in range(CH):
                            bk.wait_drained(pe, ("y", u, j), i)
                        for n in range(N):
                            if n + 1 < N:
                                spread(n + 1)
                            bk.wait_read(pe, ("C", u, n), i)
                            for j in range(CH):
                                ins = pe.matmul(ps(("y", u, j))[:], chip.ident[:], hc[n % NB][:, j, :], start=(n == 0), stop=(n == N - 1))
                                if n == N - 1:
                                    bk.fill(ins, ("y", u, j))
                            if n < N - 1:
                                hc_summed.by(ins)
                        hc_summed_last = pe.sem_inc(hc_summed.sem, 1)
                        yT_ready.wait(pe, i, u)
                        bk.wait_drained(pe, ("out", u), i)
                        for t in range(TPS):
                            for j in range(CH):
                                ins = pe.matmul(ps(("out", u))[:, t * D:(t + 1) * D], yT[u][:, j, t * P:(t + 1) * P], w_out[:, j, :],
                                                start=(j == 0), stop=(j == CH - 1))
                        bk.fill(ins, ("out", u))



def build(nc, a, out, stages=range(8)):
    with ExitStack() as ctx:
        chip = Chip(nc, ctx)
        load_stage(chip, a["L0_attn_x"], a["ident"])
        chip.end_layer()
        part = lambda p: {k[len(p):]: v for k, v in a.items() if k.startswith(p)}
        layers = ((cosine_attention, "L0_attn_"), (top2_glu_experts, "L0_ffn_"),
                  (feature_attention, "L1_attn_"), (switch_experts, "L1_ffn_"),
                  (selective_scan, "L2_attn_"), (expert_choice_experts, "L2_ffn_"),
                  (relative_position_attention, "L3_attn_"), (threshold_experts, "L3_ffn_"))
        for n in stages:
            layer, prefix = layers[n]
            layer(chip, part(prefix))
            chip.end_layer()
        store_stage(chip, out)


def laid_out(inputs):
    a = {k: np.asarray(v) for k, v in inputs.items()}
    for k in ("L0_attn_Wq", "L0_attn_Wk", "L0_attn_Wv", "L0_attn_W1", "L0_attn_W2", "L0_attn_W3",
              "L1_attn_Wq", "L1_attn_Wk", "L1_attn_Wv", "L1_attn_Wo", "L1_attn_Wfc", "L1_attn_proj"):
        a[k] = a[k].T
    a["L3_ffn_Wgt"] = np.concatenate([a.pop("L3_ffn_Wg"), a.pop("L3_ffn_Wt")], axis=1)
    a["L3_ffn_bgt"] = np.concatenate([a.pop("L3_ffn_bg"), a.pop("L3_ffn_bt")])
    a["L3_attn_onehot"] = buckets_by_distance()
    row, head = np.arange(P)[:, None], np.arange(16)[None, :]
    a["L1_attn_spread"] = (np.arange(8)[:, None] == np.arange(P)[None, :] % 8).astype(np.float32)
    a["L1_attn_head_of"] = (row // 8 == head).astype(np.float32)
    a["L1_attn_half_head"] = np.where(row // 8 == head, np.float32(0.5), np.float32(0))
    a["L1_attn_own"] = (row // 16 == np.concatenate([np.arange(64) // 8, np.arange(8)])[None, :]).astype(np.float32)
    a["L2_attn_pick"] = np.broadcast_to(np.eye(16, dtype=np.float32)[:, :, None], (16, 16, P))
    a["ident"] = np.eye(P, dtype=np.float32)
    return {k: np.ascontiguousarray(v) for k, v in a.items()}


def make_program(nc, inputs, stages=range(8)):
    arrays, aps = {}, {}
    for name, v in laid_out(inputs).items():
        arrays[f"in_{name}_dram"] = v
        aps[name] = nc.dram_tensor(f"in_{name}_dram", v.shape, mybir.dt.from_np(v.dtype), kind="ExternalInput").ap()
    out = nc.dram_tensor("out_0_dram", (B, S, D), F32, kind="ExternalOutput").ap()
    build(nc, aps, out, stages)
    return arrays


def kernel(**inputs):
    import concourse.bacc as _bacc
    from concourse.bass_utils import run_bass_kernel_spmd as _run

    nc = _bacc.Bacc("TRN2", target_bir_lowering=False, num_devices=1)
    arrays = make_program(nc, inputs)
    r = _run(nc, [arrays], core_ids=[0])
    return r.results[0]["out_0_dram"]
```

```python
from contextlib import ExitStack

import numpy as np

import concourse.bass as bass
import concourse.mybir as mybir

ALU = mybir.AluOpType
ACT = mybir.ActivationFunctionType
F32 = mybir.dt.float32
U32 = mybir.dt.uint32
BF16 = mybir.dt.bfloat16
AX_X = mybir.AxisListType.X

P = 128
D = 128
B, S = 8, 512
TPS = S // P
NT = B * TPS
U = 2
LN_EPS = 1e-5
BANK = 512
SLOTS = 40 * 2 * P
ZC = 1024


class Chain:

    def __init__(self, eng, sem, per_turn=0, base=0):
        self.eng, self.sem, self.per_turn, self.turn, self.n, self.base = eng, sem, per_turn, 0, 0, base

    def start(self, turn):
        self.turn, self.n = turn, 0

    def link(self, ins):
        self.n += 1
        ins.then_inc(self.sem, 1)
        self.eng.wait_ge(self.sem, self.turn * self.per_turn + (self.n + self.base))

    def end(self):
        assert self.n == self.per_turn, (self.n, self.per_turn)


class Banks:

    def __init__(self, sem, name, order):
        self.place, self.uses = {}, {}
        for job, bank in order:
            self.place[job] = (bank, self.uses.get(bank, 0))
            self.uses[bank] = self.uses.get(bank, 0) + 1
        self.filled = {k: sem(f"{name}_bank{k}_filled") for k in self.uses}
        self.drained = {k: sem(f"{name}_bank{k}_drained") for k in self.uses}

    def open(self, eng):
        for k in self.uses:
            eng.sem_inc(self.drained[k], 1)

    def wait_drained(self, eng, job, turn):
        k, n = self.place[job]
        eng.wait_ge(self.drained[k], turn * self.uses[k] + (n + 1))

    def wait_filled(self, eng, job, turn):
        k, n = self.place[job]
        eng.wait_ge(self.filled[k], turn * self.uses[k] + (n + 1))

    def wait_read(self, eng, job, turn):
        k, n = self.place[job]
        eng.wait_ge(self.drained[k], turn * self.uses[k] + (n + 2))

    def fill(self, ins, job):
        ins.then_inc(self.filled[self.place[job][0]], 1)

    def drain(self, ins, job):
        ins.then_inc(self.drained[self.place[job][0]], 1)


class Signal:

    def __init__(self, sem, per_turn):
        self.sem, self.per_turn = sem, per_turn

    def by(self, ins):
        ins.then_inc(self.sem, 1)

    def wait(self, eng, turn, n):
        eng.wait_ge(self.sem, turn * self.per_turn + (n + 1))


class Chip:

    def __init__(self, nc, ctx):
        self.nc, self.ctx = nc, ctx
        self.x = self.sb(ctx, "x", [P, NT, D])
        self.ident = self.sb(ctx, "ident", [P, P])
        self.ones = self.sb(ctx, "ones", [P, P])
        self.ln_eps = self.sb(ctx, "ln_eps", [P, 1])
        self.before = self.sb(ctx, "before", [P, P])
        self.count = self.sb(ctx, "count", [P, P])
        self.zeros = self.sb(ctx, "zeros", [P, ZC])
        self.slot_x = nc.dram_tensor("slot_x", (SLOTS, D), F32, kind="Internal").ap()
        self.slots_zeroed = nc.alloc_semaphore(name="slots_zeroed")
        self.SLOTS_ZEROED = 16 * (SLOTS * D // (P * ZC))
        self.apart_count = nc.alloc_semaphore(name="apart_count")
        self.counts = []
        self.psum = [ctx.enter_context(nc.psum_tensor(f"bank{k}", [P, BANK], F32)) for k in range(8)]

    def sb(self, ctx, name, shape, dt=F32):
        return ctx.enter_context(self.nc.sbuf_tensor(name, shape, dt))

    def apart(self, eng):
        eng.sem_inc(self.apart_count, 1)

    def sem(self, name):
        self.counts.append(self.nc.alloc_semaphore(name=name))
        return self.counts[-1]

    def end_layer(self):
        self.nc.clear_and_free_semaphores(self.counts)
        self.nc.all_engine_barrier()
        self.counts = []


def ln_statistics(chip, dve, chain, x_tile, stats, mv, n):
    for t in range(n):
        ins = dve.bn_stats(stats[:, t, :], x_tile(t))
    chain.link(ins)
    chip.apart(dve)
    for t in range(n):
        ins = dve.bn_aggr(mv[:, t, :], stats[:, t, :])
    return ins



def load_stage(chip, x_in, ident_in, before_in, count_in):
    nc = chip.nc
    loaded, zeros_ready = chip.sem("x_loaded"), chip.sem("zeros_ready")
    with nc.Block() as block:
        @block.sync
        def _(sp):
            sp.dma_start(chip.ident[:], ident_in).then_inc(loaded, 16)
            xv = x_in.rearrange("b (t p) d -> p (b t) d", p=P)
            for c in range(2):
                h = NT // 2
                sp.dma_start(chip.x[:, c * h:(c + 1) * h, :], xv[:, c * h:(c + 1) * h, :]).then_inc(loaded, 16)
            sp.dma_start(chip.before[:], before_in).then_inc(loaded, 16)
            sp.dma_start(chip.count[:], count_in.partition_broadcast(P)).then_inc(loaded, 16)
            sp.wait_ge(loaded, 80)

        @block.vector
        def _(dve):
            nc.vector.memset(chip.ones[:], 1.0)
            nc.vector.memset(chip.ln_eps[:], LN_EPS)
            nc.vector.memset(chip.zeros[:], 0.0).then_inc(zeros_ready, 1)

        @block.gpsimd
        def _(pool):
            pool.wait_ge(zeros_ready, 1)
            rows = P * ZC // D
            for n in range(SLOTS // rows):
                dst = chip.slot_x[n * rows:(n + 1) * rows, :].rearrange("(p r) d -> p (r d)", p=P)
                pool.dma_start(dst, chip.zeros[:]).then_inc(chip.slots_zeroed, 16)


def store_stage(chip, out):
    nc = chip.nc
    stored = chip.sem("out_stored")
    with nc.Block() as block:
        @block.sync
        def _(sp):
            ov = out.rearrange("b (t p) d -> p (b t) d", p=P)
            for c in range(2):
                h = NT // 2
                sp.dma_start(ov[:, c * h:(c + 1) * h, :], chip.x[:, c * h:(c + 1) * h, :]).then_inc(stored, 16)
            sp.wait_ge(stored, 32)



def cosine_attention(chip, w):
    nc = chip.nc
    F = 512
    J = F // P
    QK, QKV = 2 * D, 3 * D
    ctx = ExitStack()
    with ctx:
        sb = lambda name, shape: chip.sb(ctx, f"l0a_{name}", shape)
        two = lambda name, shape: [sb(f"{name}{u}", shape) for u in range(U)]
        sem = lambda name: chip.sem(f"l0a_{name}")
        w_qkv, b_qkv = sb("w_qkv", [P, QKV]), sb("b_qkv", [P, QKV])
        w1, w2, w3 = sb("w1", [P, D]), sb("w2", [P, F]), sb("w3", [P, J, D])
        b1, b2, b3 = sb("b1", [P, 1]), sb("b2", [P, J]), sb("b3", [P, D])
        stats, mv = two("stats", [P, TPS, 6]), two("mv", [P, TPS, 2])
        std, rstd = two("std", [P, TPS]), two("rstd", [P, TPS])
        xn, xnT = two("xn", [P, TPS, D]), two("xnT", [P, S])
        qkv = two("qkv", [P, TPS, QKV + 1])
        sq, ss = two("sq", [P, TPS, 2, D]), two("ss", [P, TPS, 2])
        length, inv = two("length", [P, TPS, 2]), two("inv", [P, TPS, 2])
        qk = two("qk", [P, TPS, 2, D])
        qT, kT = two("qT", [P, S]), two("kT", [P, S])
        E, rden = two("E", [P, TPS, S]), two("rden", [P, TPS])
        o, oT = two("o", [P, TPS, D]), two("oT", [P, S])
        h1, h2 = two("h1", [P, S]), two("h2", [P, J, S])
        y = two("y", [P, TPS, D])

        order = [(("xT", u), 6 + u) for u in range(U)]
        order += [(("qkv", u, t), 4 + t % 2) for u in range(U) for t in range(TPS)]
        order += [((n, u), k) for u in range(U) for n, k in (("qT", 6), ("kT", 7))]
        order += [(("s", u, t), t) for u in range(U) for t in range(TPS)]
        order += [(("av", u, t), 4 + t % 2) for u in range(U) for t in range(TPS)]
        order += [(("oT", u), 6 + u) for u in range(U)]
        order += [(("h1", u), 6 + u) for u in range(U)]
        order += [(("h2", u, j), j) for u in range(U) for j in range(J)]
        order += [(("y", u), 4 + u) for u in range(U)]
        bk = Banks(sem, "psum", order)
        ps = lambda job: chip.psum[bk.place[job][0]]

        weights = sem("weights_loaded")
        WEIGHTS = 10
        step = lambda name, n=1: Signal(sem(name), U * n)
        mv_ready, std_ready, xn_ready, xnT_ready = step("mv_ready"), step("std_ready"), step("xn_ready"), step("xnT_ready")
        ss_ready, length_ready, qk_ready, qkT_ready = (step("ss_ready"), step("length_ready"), step("qk_ready"),
                                                       step("qkT_ready", 2))
        e_ready, o_ready, oT_ready = step("e_ready", TPS), step("o_ready"), step("oT_ready")
        h1_ready, h2_ready = step("h1_ready"), step("h2_ready", J)
        dve_order = sem("dve_order")
        TURNS = B // U

        def x_tile(i, u, t):
            return chip.x[:, bass.ds((i * U + u) * TPS + t, 1), :].rearrange("p a d -> p (a d)")

        with nc.Block() as block:
            @block.sync
            def _(sp):
                for n, nm in enumerate(["Wq", "Wk", "Wv"]):
                    sp.dma_start(w_qkv[:, n * D:(n + 1) * D], w[nm]).then_inc(weights, 16)
                    sp.dma_start(b_qkv[:, n * D:(n + 1) * D], w["b" + nm[1]].partition_broadcast(P)).then_inc(weights, 16)
                sp.dma_start(w1[:], w["W1"]).then_inc(weights, 16)
                sp.dma_start(w2[:], w["W2"]).then_inc(weights, 16)
                sp.dma_start(w3[:], w["W3"].rearrange("(j p) d -> p j d", p=P)).then_inc(weights, 16)
                sp.dma_start(b3[:], w["b3"].partition_broadcast(P)).then_inc(weights, 16)
                sp.dma_start(b1[:], w["b1"].rearrange("(p o) -> p o", o=1)).then_inc(weights, 16)
                with nc.allow_non_contiguous_dma(reason="a bias by partition"):
                    sp.dma_start(b2[:], w["b2"].rearrange("(j p) -> p j", p=P)).then_inc(weights, 16)

            @block.vector
            def _(dve):
                c = Chain(dve, dve_order, per_turn=U * 7)
                for u in range(U):
                    dve.memset(qkv[u][:, :, QKV:], 1.0)
                dve.wait_ge(weights, 16 * (WEIGHTS + 2))
                with dve.Fori(0, TURNS) as i:
                    c.start(i)
                    for u in range(U):
                        mv_ready.by(ln_statistics(chip, dve, c, lambda t: x_tile(i, u, t), stats[u], mv[u], TPS))
                    for u in range(U):
                        std_ready.wait(dve, i, u)
                        c.link(dve.reciprocal(rstd[u][:], std[u][:]))
                        for t in range(TPS):
                            ins = dve.tensor_scalar(xn[u][:, t, :], x_tile(i, u, t), mv[u][:, t, 0:1],
                                                    rstd[u][:, t:t + 1], ALU.subtract, ALU.mult)
                        xn_ready.by(ins)
                    for u in range(U):
                        for t in range(TPS):
                            bk.wait_filled(dve, ("qkv", u, t), i)
                            bk.drain(dve.tensor_tensor(qkv[u][:, t, 0:QKV], ps(("qkv", u, t))[:, 0:QKV], b_qkv[:],
                                                       ALU.add), ("qkv", u, t))
                        bk.wait_read(dve, ("qkv", u, TPS - 2), i)
                        bk.wait_read(dve, ("qkv", u, TPS - 1), i)
                        qk_in = qkv[u][:, :, 0:QK].rearrange("p t (n d) -> p t n d", n=2)
                        c.link(dve.tensor_tensor(sq[u][:], qk_in, qk_in, ALU.mult))
                        ss_ready.by(dve.tensor_reduce(ss[u][:], sq[u][:], AX_X, ALU.add))
                    for u in range(U):
                        length_ready.wait(dve, i, u)
                        c.link(dve.tensor_scalar(inv[u][:], length[u][:], 1e-12, None, ALU.max))
                        c.link(dve.reciprocal(inv[u][:], inv[u][:]))
                        for n in range(2):
                            ins = dve.tensor_tensor(qk[u][:, :, n, :], qkv[u][:, :, n * D:(n + 1) * D],
                                                    inv[u][:, :, n:n + 1].to_broadcast([P, TPS, D]), ALU.mult)
                        qk_ready.by(ins)
                    for u in range(U):
                        for t in range(TPS):
                            job = ("av", u, t)
                            bk.wait_filled(dve, job, i)
                            dve.tensor_copy(o[u][:, t, :], ps(job)[:, 0:D])
                            bk.drain(dve.tensor_copy(rden[u][:, t:t + 1], ps(job)[:, D:D + 1]), job)
                        bk.wait_read(dve, ("av", u, TPS - 2), i)
                        bk.wait_read(dve, ("av", u, TPS - 1), i)
                        c.link(dve.reciprocal(rden[u][:], rden[u][:]))
                        o_ready.by(dve.tensor_tensor(o[u][:], o[u][:],
                                                     rden[u][:].rearrange("p (t o) -> p t o", o=1).to_broadcast([P, TPS, D]), ALU.mult))
                    for u in range(U):
                        job = ("y", u)
                        bk.wait_filled(dve, job, i)
                        bk.drain(dve.tensor_tensor(y[u][:], ps(job)[:].rearrange("p (t d) -> p t d", t=TPS),
                                                   b3[:].rearrange("p (o d) -> p o d", o=1).to_broadcast([P, TPS, D]), ALU.add), job)
                        bk.wait_read(dve, job, i)
                        xs = chip.x[:, bass.ds((i * U + u) * TPS, TPS), :]
                        c.link(dve.tensor_tensor(xs, xs, y[u][:], ALU.add))
                c.end()

            @block.scalar
            def _(act):
                with act.Fori(0, TURNS) as i:
                    for u in range(U):
                        mv_ready.wait(act, i, u)
                        std_ready.by(act.activation(std[u][:], mv[u][:, :, 1], ACT.Sqrt, bias=chip.ln_eps[:]))
                    for u in range(U):
                        bk.wait_filled(act, ("xT", u), i)
                        ins = act.copy(xnT[u][:], ps(("xT", u))[:])
                        bk.drain(ins, ("xT", u))
                    for u in range(U):
                        ss_ready.wait(act, i, u)
                        length_ready.by(act.activation(length[u][:], ss[u][:], ACT.Sqrt))
                    for u in range(U):
                        for n, dst in (("qT", qT), ("kT", kT)):
                            bk.wait_filled(act, (n, u), i)
                            bk.drain(act.copy(dst[u][:], ps((n, u))[:]), (n, u))
                    for u in range(U):
                        for t in range(TPS):
                            bk.wait_filled(act, ("s", u, t), i)
                            bk.drain(act.activation(E[u][:, t, :], ps(("s", u, t))[:], ACT.Exp), ("s", u, t))
                    for u in range(U):
                        bk.wait_filled(act, ("oT", u), i)
                        bk.drain(act.copy(oT[u][:], ps(("oT", u))[:]), ("oT", u))
                    for u in range(U):
                        bk.wait_filled(act, ("h1", u), i)
                        bk.drain(act.activation(h1[u][:], ps(("h1", u))[:], ACT.Relu, bias=b1[:]), ("h1", u))
                    for u in range(U):
                        for j in range(J):
                            bk.wait_filled(act, ("h2", u, j), i)
                            bk.drain(act.activation(h2[u][:, j, :], ps(("h2", u, j))[:], ACT.Relu, bias=b2[:, j:j + 1]), ("h2", u, j))

            @block.tensor
            def _(pe):
                bk.open(pe)
                pe.wait_ge(weights, 16 * (WEIGHTS + 2))
                with pe.Fori(0, TURNS) as i:
                    for u in range(U):
                        xn_ready.wait(pe, i, u)
                        bk.wait_drained(pe, ("xT", u), i)
                        for t in range(TPS):
                            ins = pe.transpose(ps(("xT", u))[:, t * P:(t + 1) * P], xn[u][:, t, :], chip.ident[:])
                        bk.fill(ins, ("xT", u))
                    for u in range(U):
                        bk.wait_read(pe, ("xT", u), i)
                        for t in range(TPS):
                            job = ("qkv", u, t)
                            bk.wait_drained(pe, job, i)
                            bk.fill(pe.matmul(ps(job)[:, 0:QKV], xnT[u][:, t * P:(t + 1) * P], w_qkv[:], start=True, stop=True), job)
                    for u in range(U):
                        qk_ready.wait(pe, i, u)
                        for n, nm in enumerate(("qT", "kT")):
                            bk.wait_drained(pe, (nm, u), i)
                            for t in range(TPS):
                                ins = pe.transpose(ps((nm, u))[:, t * P:(t + 1) * P], qk[u][:, t, n, :], chip.ident[:])
                            bk.fill(ins, (nm, u))
                    for u in range(U):
                        bk.wait_read(pe, ("qT", u), i)
                        bk.wait_read(pe, ("kT", u), i)
                        for t in range(TPS):
                            job = ("s", u, t)
                            bk.wait_drained(pe, job, i)
                            bk.fill(pe.matmul(ps(job)[:], kT[u][:, t * P:(t + 1) * P], qT[u][:], start=True, stop=True), job)
                    for u in range(U):
                        for t in range(TPS):
                            bk.wait_read(pe, ("s", u, t), i)
                        for t in range(TPS):
                            job = ("av", u, t)
                            bk.wait_drained(pe, job, i)
                            for k in range(TPS):
                                ins = pe.matmul(ps(job)[:, 0:D + 1], E[u][:, k, t * P:(t + 1) * P], qkv[u][:, k, QK:],
                                                start=(k == 0), stop=(k == TPS - 1))
                            bk.fill(ins, job)
                    for u in range(U):
                        o_ready.wait(pe, i, u)
                        bk.wait_drained(pe, ("oT", u), i)
                        for t in range(TPS):
                            ins = pe.transpose(ps(("oT", u))[:, t * P:(t + 1) * P], o[u][:, t, :], chip.ident[:])
                        bk.fill(ins, ("oT", u))
                    for u in range(U):
                        bk.wait_read(pe, ("oT", u), i)
                        bk.wait_drained(pe, ("h1", u), i)
                        bk.fill(pe.matmul(ps(("h1", u))[:], w1[:], oT[u][:], start=True, stop=True), ("h1", u))
                    for u in range(U):
                        bk.wait_read(pe, ("h1", u), i)
                        for j in range(J):
                            bk.wait_drained(pe, ("h2", u, j), i)
                            bk.fill(pe.matmul(ps(("h2", u, j))[:], w2[:, j * P:(j + 1) * P], h1[u][:], start=True, stop=True), ("h2", u, j))
                    for u in range(U):
                        job = ("y", u)
                        for j in range(J):
                            bk.wait_read(pe, ("h2", u, j), i)
                        bk.wait_drained(pe, job, i)
                        for t in range(TPS):
                            for j in range(J):
                                ins = pe.matmul(ps(job)[:, t * D:(t + 1) * D], h2[u][:, j, t * P:(t + 1) * P], w3[:, j, :],
                                                start=(j == 0), stop=(j == J - 1))
                        bk.fill(ins, job)



E8 = 8
F = 512
J = F // P


def seq_tiles(ap, i, u):
    return ap[:, bass.ds((i * U + u) * TPS, TPS), :]


def one_tile(ap, i, u, t):
    return ap[:, bass.ds((i * U + u) * TPS + t, 1), :].rearrange("p a d -> p (a d)")


def normalise_and_route(chip, ctx, L, w_router, vectors, rows_out=False):
    nc = chip.nc
    NR = w_router.shape[1] if w_router is not None else 0
    loads = bool(NR) + len(vectors)
    xnT_all = chip.sb(ctx, f"{L}_xnT_all", [P, NT, D] if rows_out else [P, NT * P])
    cols = {n: chip.sb(ctx, f"{L}_{n}", [P, E8 * J]) for n in vectors}
    with ExitStack() as inner:
        sb = lambda name, shape: chip.sb(inner, f"{L}r_{name}", shape)
        two = lambda name, shape: [sb(f"{name}{u}", shape) for u in range(U)]
        sem = lambda name: chip.sem(f"{L}r_{name}")
        step = lambda name, n=1: Signal(sem(name), U * n)
        router = sb("router", [P, NR]) if NR else None
        rows = {n: sb(f"rows_{n}", [E8 * J, P]) for n in vectors}
        stats, mv = two("stats", [P, TPS, 6]), two("mv", [P, TPS, 2])
        std, rstd = two("std", [P, TPS]), two("rstd", [P, TPS])
        xn, xnT = two("xn", [P, TPS, D]), two("xnT", [P, S])
        bk = Banks(sem, "psum", [(("xT", u), 6 + u) for u in range(U)])
        ps = lambda job: chip.psum[bk.place[job][0]]
        loaded, cols_filled = sem("loaded"), sem("cols_filled")
        mv_ready, std_ready, xn_ready = step("mv_ready"), step("std_ready"), step("xn_ready")
        routed, copied = step("routed"), step("copied")
        dve_order = sem("dve_order")
        TURNS = B // U
        with nc.Block() as block:
            @block.sync
            def _(sp):
                if NR:
                    sp.dma_start(router[:], w_router).then_inc(loaded, 16)
                for n, v in vectors.items():
                    sp.dma_start(rows[n][:], v).then_inc(loaded, 16)

            @block.vector
            def _(dve):
                c = Chain(dve, dve_order, per_turn=U * 2)
                with dve.Fori(0, TURNS) as i:
                    c.start(i)
                    for u in range(U):
                        mv_ready.by(ln_statistics(chip, dve, c, lambda t: one_tile(chip.x, i, u, t), stats[u], mv[u], TPS))
                    for u in range(U):
                        std_ready.wait(dve, i, u)
                        c.link(dve.reciprocal(rstd[u][:], std[u][:]))
                        if rows_out:
                            copied.wait(dve, i, u)
                        for t in range(TPS):
                            ins = dve.tensor_scalar(xn[u][:, t, :], one_tile(chip.x, i, u, t), mv[u][:, t, 0:1],
                                                    rstd[u][:, t:t + 1], ALU.subtract, ALU.mult)
                        xn_ready.by(ins)
                c.end()
                if vectors:
                    dve.wait_ge(cols_filled, 1)
                for n, v in enumerate(vectors):
                    dve.tensor_copy(cols[v][:], chip.psum[1][:, n * E8 * J:(n + 1) * E8 * J])

            @block.scalar
            def _(act):
                with act.Fori(0, TURNS) as i:
                    for u in range(U):
                        mv_ready.wait(act, i, u)
                        std_ready.by(act.activation(std[u][:], mv[u][:, :, 1], ACT.Sqrt, bias=chip.ln_eps[:]))
                    for u in range(U):
                        bk.wait_filled(act, ("xT", u), i)
                        bk.drain(act.copy(xnT[u][:], ps(("xT", u))[:]), ("xT", u))

            @block.gpsimd
            def _(pool):
                with pool.Fori(0, TURNS) as i:
                    for u in range(U):
                        if rows_out:
                            xn_ready.wait(pool, i, u)
                            copied.by(pool.tensor_copy(seq_tiles(xnT_all, i, u), xn[u][:]))
                        else:
                            bk.wait_read(pool, ("xT", u), i)
                            copied.by(pool.tensor_copy(xnT_all[:, bass.ds((i * U + u) * S, S)], xnT[u][:]))

            @block.tensor
            def _(pe):
                bk.open(pe)
                pe.sem_inc(copied.sem, U)
                if loads:
                    pe.wait_ge(loaded, 16 * loads)
                for n, v in enumerate(vectors):
                    ins = pe.transpose(chip.psum[1][:, n * E8 * J:(n + 1) * E8 * J], rows[v][:], chip.ident[0:E8 * J, 0:E8 * J])
                if vectors:
                    ins.then_inc(cols_filled, 1)
                with pe.Fori(0, TURNS) as i:
                    for u in range(U):
                        xn_ready.wait(pe, i, u)
                        copied.wait(pe, i, u)
                        bk.wait_drained(pe, ("xT", u), i)
                        for t in range(TPS):
                            ins = pe.transpose(ps(("xT", u))[:, t * P:(t + 1) * P], xn[u][:, t, :], chip.ident[:])
                        bk.fill(ins, ("xT", u))
                    for u in range(U if NR else 0):
                        bk.wait_read(pe, ("xT", u), i)
                        for t in range(TPS):
                            ins = pe.matmul(chip.psum[0][:, bass.ds(((i * U + u) * TPS + t) * NR, NR)],
                                            xnT[u][:, t * P:(t + 1) * P], router[:], start=True, stop=True)
                        routed.by(ins)
    return xnT_all, cols


def bcast(ap2, n_before=None, n_after=None):
    m = ap2.shape[1]
    if n_before:
        return ap2.rearrange("p (o m) -> p o m", o=1).to_broadcast([ap2.shape[0], n_before, m])
    return ap2.rearrange("p (m o) -> p m o", o=1).to_broadcast([ap2.shape[0], m, n_after])


def route(chip, ctx, L, NR, bias, top=None, capacity=None, threshold=False, b2=None):
    nc = chip.nc
    gates = chip.sb(ctx, f"{L}_gates", [P, NT, E8])
    picks = [chip.sb(ctx, f"{L}_pick{k}", [P, NT, E8]) for k in range(top or 0)]
    pick_gates = chip.sb(ctx, f"{L}_pick_gates", [P, top, NT]) if top else None
    with ExitStack() as inner:
        sb = lambda name, shape, dt=F32: chip.sb(inner, f"{L}g_{name}", shape, dt)
        sem = lambda name: chip.sem(f"{L}g_{name}")
        logits, ex = sb("logits", [P, NT, NR]), sb("ex", [P, NT, E8])
        red, a, b = sb("red", [P, NT]), sb("a", [P, NT, E8]), sb("b", [P, NT, E8])
        probs = sb("probs", [P, NT, E8])
        bias_all = sb("bias_all", [P, NR])
        order8 = sb("order8", [P, E8])
        dve_order, shifted, exp_done, loaded = sem("dve_order"), sem("shifted"), sem("exp_done"), sem("loaded")
        turned, used, back, backed = sem("turned"), sem("used"), sem("back"), sem("backed")
        if capacity:
            R = B * E8
            rows, left, sel = sb("rows", [R, S]), sb("left", [R, S]), sb("sel", [R, S])
            best = sb("best", [R, 8])
            by_place = sb("by_place", [P, TPS, R])
        if b2 is not None:
            gT, b2_rows, z = sb("gT", [E8, B, S]), sb("b2_rows", [E8, D]), sb("z", [P, NT, D])
        per_e = lambda r: bcast(r[:], n_after=E8)
        with nc.Block() as block:
            @block.sync
            def _(sp):
                if bias is not None:
                    sp.dma_start(bias_all[:], bias.partition_broadcast(P)).then_inc(loaded, 16)
                if b2 is not None:
                    sp.dma_start(b2_rows[:], b2).then_inc(loaded, 16)

            @block.vector
            def _(dve):
                c = Chain(dve, dve_order)
                raw = chip.psum[0][:, 0:NT * NR].rearrange("p (t e) -> p t e", e=NR)
                if bias is not None:
                    dve.wait_ge(loaded, 16 * (1 + (b2 is not None)))
                    c.link(dve.tensor_tensor(logits[:], raw, bcast(bias_all[:], n_before=NT), ALU.add))
                else:
                    c.link(dve.tensor_copy(logits[:], raw))
                c.link(dve.tensor_reduce(red[:], logits[:, :, 0:E8], AX_X, ALU.max))
                dve.tensor_tensor(a[:], logits[:, :, 0:E8], per_e(red), ALU.subtract).then_inc(shifted, 1)
                dve.wait_ge(exp_done, 1)
                c.link(dve.tensor_reduce(red[:], ex[:], AX_X, ALU.add))
                c.link(dve.reciprocal(red[:], red[:]))
                c.link(dve.tensor_tensor(probs[:], ex[:], per_e(red), ALU.mult))
                if top:
                    for e in range(E8):
                        ins = dve.memset(order8[:, e:e + 1], float(E8 - e))
                    c.link(ins)
                    c.link(dve.tensor_copy(b[:], probs[:]))
                    for k in range(top):
                        c.link(dve.tensor_reduce(red[:], b[:], AX_X, ALU.max))
                        c.link(dve.tensor_tensor(a[:], b[:], per_e(red), ALU.is_equal))
                        c.link(dve.tensor_tensor(a[:], a[:], bcast(order8[:], n_before=NT), ALU.mult))
                        c.link(dve.tensor_reduce(red[:], a[:], AX_X, ALU.max))
                        c.link(dve.tensor_tensor(picks[k][:], a[:], per_e(red), ALU.is_equal))
                        c.link(dve.tensor_tensor(a[:], probs[:], picks[k][:], ALU.mult))
                        c.link(dve.tensor_reduce(pick_gates[:, k, :], a[:], AX_X, ALU.add))
                        c.link(dve.scalar_tensor_tensor(b[:], picks[k][:], -4.0, b[:], ALU.mult, ALU.add))
                    c.link(dve.tensor_scalar(a[:], b[:], -1.0, None, ALU.is_lt))
                    c.link(dve.tensor_tensor(gates[:], probs[:], a[:], ALU.mult))
                if threshold:
                    thr = logits[:, :, E8]
                    dve.wait_ge(exp_done, 2)
                    c.link(dve.tensor_scalar(red[:], thr, 0.125, None, ALU.mult))
                    c.link(dve.tensor_tensor(a[:], probs[:], per_e(red), ALU.subtract))
                    c.link(dve.tensor_scalar(b[:], a[:], 0.0, None, ALU.max))
                    c.link(dve.tensor_reduce(red[:], b[:], AX_X, ALU.add))
                    c.link(dve.scalar_tensor_tensor(red[:], red[:], 0.0, red[:], ALU.is_equal, ALU.add))
                    c.link(dve.reciprocal(red[:], red[:]))
                    c.link(dve.tensor_tensor(gates[:], b[:], per_e(red), ALU.mult))
                if capacity:
                    for t in range(TPS):
                        ins = dve.tensor_copy(by_place[:, t, :].rearrange("p (b e) -> p b e", e=E8),
                                              probs[:].rearrange("p (b t) e -> p b t e", t=TPS)[:, :, t, :])
                    c.link(ins)
                dve.sem_inc(turned, 1)
                if capacity:
                    dve.wait_ge(used, 1)
                    c.link(dve.tensor_copy(rows[:], chip.psum[1][0:R, :]))
                    c.link(dve.tensor_copy(left[:], rows[:]))
                    for k in range(capacity // 8):
                        c.link(dve.max(best[:], left[:]))
                        c.link(dve.match_replace(left[:], best[:], left[:], -1.0))
                    c.link(dve.scalar_tensor_tensor(sel[:], left[:], 0.0, rows[:], ALU.is_lt, ALU.mult))
                    dve.sem_inc(back, 1)
                    dve.wait_ge(backed, 1)
                    gv = gates[:].rearrange("p (b t) e -> p b t e", t=TPS)
                    for t in range(TPS):
                        dve.tensor_copy(gv[:, :, t, :], chip.psum[2][:, t * R:(t + 1) * R].rearrange("p (b e) -> p b e", e=E8))
                if b2 is not None:
                    for q in range(B):
                        dve.wait_ge(used, q + 1)
                        dve.tensor_copy(gT[:, q, :], chip.psum[q][0:E8, :]).then_inc(back, 1)
                    for q in range(B):
                        dve.wait_ge(backed, q + 1)
                        xs = chip.x[:, q * TPS:(q + 1) * TPS, :]
                        dve.tensor_tensor(xs, chip.psum[q][:].rearrange("p (t d) -> p t d", d=D), xs, ALU.add)

            @block.scalar
            def _(act):
                act.wait_ge(shifted, 1)
                act.activation(ex[:], a[:], ACT.Exp).then_inc(exp_done, 1)
                if threshold:
                    act.activation(logits[:, :, E8], logits[:, :, E8], ACT.Sigmoid).then_inc(exp_done, 1)

            @block.tensor
            def _(pe):
                pe.wait_ge(turned, 1)
                if capacity:
                    for t in range(TPS):
                        ins = pe.transpose(chip.psum[1][0:R, t * P:(t + 1) * P], by_place[:, t, :], chip.ident[:])
                    ins.then_inc(used, 1)
                    pe.wait_ge(back, 1)
                    for t in range(TPS):
                        ins = pe.transpose(chip.psum[2][:, t * R:(t + 1) * R], sel[:, t * P:(t + 1) * P], chip.ident[0:R, 0:R])
                    ins.then_inc(backed, 1)
                if b2 is not None:
                    for q in range(B):
                        for t in range(TPS):
                            ins = pe.transpose(chip.psum[q][0:E8, t * P:(t + 1) * P], gates[:, q * TPS + t, :], chip.ident[:])
                        ins.then_inc(used, 1)
                    for q in range(B):
                        pe.wait_ge(back, q + 1)
                        for t in range(TPS):
                            ins = pe.matmul(chip.psum[q][:, t * D:(t + 1) * D], gT[:, q, t * P:(t + 1) * P], b2_rows[:],
                                            start=True, stop=True)
                        ins.then_inc(backed, 1)
    return (gates, picks, pick_gates) if top else gates


def dense_experts(chip, L, xnT_all, gates, w_in, w_out, act_fn, b1=None, glu=None):
    nc = chip.nc
    CU = 2
    CT = B // CU
    with ExitStack() as ctx:
        sb = lambda name, shape: chip.sb(ctx, f"{L}e_{name}", shape)
        two = lambda name, shape: [sb(f"{name}{u}", shape) for u in range(2)]
        sem = lambda name: chip.sem(f"{L}e_{name}")
        w1, w2 = two("w1", [P, F]), two("w2", [P, J, D])
        h = two("h", [P, J, S])
        if glu:
            w_v, s_v, s_in, s_out = glu
            wv, so, w2s, g = two("wv", [P, F]), two("so", [P, D]), two("w2s", [P, J, D]), two("g", [P, J, S])
            order = [((n, u, j), base + (u * J + j) % 3) for u in range(2) for j in range(J) for n, base in (("h", 0), ("v", 3))]
        else:
            w2s = w2
            order = [(("h", u, j), j) for u in range(2) for j in range(J)]
        order += [(("y", u), 6 + u) for u in range(2)]
        bk = Banks(sem, "psum", order)
        ps = lambda job: chip.psum[bk.place[job][0]]
        loaded = [sem(f"weights_loaded{u}") for u in range(2)]
        scaled = sem("w_out_scaled")
        g_ready, h_read = sem("g_ready"), None
        NW = 2 + 2 * bool(glu)

        def load(sp, e, eh):
            one = lambda w: w[bass.ds(e, 1)]
            sp.dma_start(w1[eh][:], one(w_in).rearrange("e k f -> (e k) f")).then_inc(loaded[eh], 16)
            sp.dma_start(w2[eh][:], one(w_out).rearrange("e (j p) d -> p (e j) d", p=P)).then_inc(loaded[eh], 16)
            if glu:
                sp.dma_start(wv[eh][:], one(w_v).rearrange("e k f -> (e k) f")).then_inc(loaded[eh], 16)
                sp.dma_start(so[eh][:], one(s_out).rearrange("e o d -> (e o) d").partition_broadcast(P)
                             if False else s_out[bass.ds(e, 1)].rearrange("e o d -> (e o d)").partition_broadcast(P)).then_inc(loaded[eh], 16)

        with nc.Block() as block:
            @block.sync
            def _(sp):
                for eh in range(2):
                    load(sp, eh, eh)
                with sp.Fori(1, E8 // 2) as ep:
                    for eh in range(2):
                        bk.wait_filled(sp, ("y", 1), ((ep - 1) * 2 + eh) * CT + (CT - 1))
                        load(sp, ep * 2 + eh, eh)

            if glu:
                @block.gpsimd
                def _(pool):
                    with pool.Fori(0, E8 // 2) as ep:
                        for eh in range(2):
                            pool.wait_ge(loaded[eh], (ep + 1) * (16 * NW))
                            pool.tensor_tensor(w2s[eh][:], w2[eh][:], bcast(so[eh][:], n_before=J), ALU.mult).then_inc(scaled, 1)

            @block.scalar
            def _(act):
                with act.Fori(0, E8 // 2) as ep:
                    for eh in range(2):
                        with act.Fori(0, CT) as cp:
                            turn = (ep * 2 + eh) * CT + cp
                            for u in range(2):
                                for j in range(J):
                                    job = ("h", u, j)
                                    bk.wait_filled(act, job, turn)
                                    chip.apart(act)
                                    col = bass.ds((ep * 2 + eh) * J + j, 1)
                                    kw = {"bias": b1[:, col]} if b1 is not None else {}
                                    if glu:
                                        kw["scale"] = s_in[:, col]
                                    dst = g if glu else h
                                    bk.drain(act.activation(dst[u][:, j, :], ps(job)[:], act_fn, **kw), job)

            @block.vector
            def _(dve):
                with dve.Fori(0, E8 // 2) as ep:
                    for eh in range(2):
                        e = ep * 2 + eh
                        with dve.Fori(0, CT) as cp:
                            turn = e * CT + cp
                            if glu:
                                for u in range(2):
                                    for j in range(J):
                                        bk.wait_filled(dve, ("v", u, j), turn)
                                        bk.wait_read(dve, ("h", u, j), turn)
                                        bk.drain(dve.scalar_tensor_tensor(h[u][:, j, :], ps(("v", u, j))[:],
                                                                          s_v[:, bass.ds(e * J + j, 1)], g[u][:, j, :],
                                                                          ALU.mult, ALU.mult), ("v", u, j))
                            for u in range(2):
                                bk.wait_filled(dve, ("y", u), turn)
                                for t in range(TPS):
                                    tile = (cp * CU + u) * TPS + t
                                    xs = chip.x[:, bass.ds(tile, 1), :].rearrange("p a d -> p (a d)")
                                    gate = gates[:, bass.ds(tile, 1), bass.ds(e, 1)].rearrange("p a e -> p (a e)")
                                    ins = dve.scalar_tensor_tensor(xs, ps(("y", u))[:, t * D:(t + 1) * D], gate, xs,
                                                                   ALU.mult, ALU.add)
                                bk.drain(ins, ("y", u))

            @block.tensor
            def _(pe):
                bk.open(pe)
                with pe.Fori(0, E8 // 2) as ep:
                    for eh in range(2):
                        pe.wait_ge(loaded[eh], (ep + 1) * (16 * NW))
                        if glu:
                            pe.wait_ge(scaled, ep * 2 + (eh + 1))
                        chip.apart(pe)
                        with pe.Fori(0, CT) as cp:
                            turn = (ep * 2 + eh) * CT + cp
                            for u in range(2):
                                rhs = xnT_all[:, bass.ds((cp * CU + u) * S, S)]
                                for j in range(J):
                                    for n, w in (("h", w1),) + ((("v", wv),) if glu else ()):
                                        bk.wait_drained(pe, (n, u, j), turn)
                                        bk.fill(pe.matmul(ps((n, u, j))[:], w[eh][:, j * P:(j + 1) * P], rhs,
                                                          start=True, stop=True), (n, u, j))
                            for u in range(2):
                                for j in range(J):
                                    bk.wait_read(pe, ("v" if glu else "h", u, j), turn)
                                bk.wait_drained(pe, ("y", u), turn)
                                for t in range(TPS):
                                    for j in range(J):
                                        ins = pe.matmul(ps(("y", u))[:, t * D:(t + 1) * D], h[u][:, j, t * P:(t + 1) * P],
                                                        w2s[eh][:, j, :], start=(j == 0), stop=(j == J - 1))
                                bk.fill(ins, ("y", u))


def by_tile(ap):
    return ap.rearrange("e (j p) -> (e j) p", p=P)



GB = 2 * P


def blocks_of(top):
    return ((top * NT * P + E8 * (GB - 1)) // GB + 1) // 2 * 2


def place(chip, ctx, L, top, picks, vectors):
    nc = chip.nc
    NB = blocks_of(top)
    MOST = NT * P // GB
    slots = chip.sb(ctx, f"{L}_slots", [P, NT, top], U32)
    expert = chip.sb(ctx, f"{L}_expert", [P, NB], U32)
    cols = {n: chip.sb(ctx, f"{L}_{n}_of_block", [P, NB, J]) for n in vectors}
    with ExitStack() as inner:
        sb = lambda name, shape: chip.sb(inner, f"{L}p_{name}", shape)
        sem = lambda name: chip.sem(f"{L}p_{name}")
        taken = sb("taken", [P, NT, E8])
        total, sums, keep = sb("total", [P, E8, NT]), sb("sums", [P, E8, NT]), sb("keep", [P, E8, NT])
        full, blocks, ends, base, one8 = (sb("full", [P, E8, MOST]), sb("blocks", [P, E8]), sb("ends", [P, E8]),
                                          sb("base", [P, E8]), sb("one8", [P, E8]))
        where, mine, slot = sb("where", [P, NT, E8]), sb("mine", [P, NT, E8]), sb("slot", [P, top, NT])
        past, number = sb("past", [P, NB, E8]), sb("number", [P, NB])
        part = sb("part", [P, NB, J])
        dve_order, marked, counted = sem("dve_order"), sem("marked"), sem("counted")
        flat = lambda a: a[:].rearrange("p a b -> p (a b)")
        with nc.Block() as block:
            @block.tensor
            def _(pe):
                pe.wait_ge(marked, 1)
                pe.matmul(chip.psum[1][:, 0:NT * E8], chip.before[:], flat(taken), start=True, stop=True)
                pe.matmul(chip.psum[2][:, 0:NT * E8], chip.ones[:], flat(taken), start=True, stop=True).then_inc(counted, 1)

            @block.vector
            def _(dve):
                c = Chain(dve, dve_order)
                dve.memset(keep[:], 1.0)
                dve.memset(one8[:], 1.0)
                if top == 1:
                    ins = dve.tensor_copy(taken[:], picks[0][:])
                else:
                    ins = dve.tensor_tensor(taken[:], picks[0][:], picks[1][:], ALU.add)
                ins.then_inc(marked, 1)
                dve.wait_ge(marked, 1)
                c.link(dve.memset(keep[:, :, 0:1], 0.0))
                dve.wait_ge(counted, 1)
                c.link(dve.tensor_copy(total[:], chip.psum[2][:, 0:NT * E8].rearrange("p (t e) -> p e t", e=E8)))
                c.link(dve.tensor_tensor_scan(flat(sums), flat(keep), flat(total), 0.0, ALU.mult, ALU.add))
                c.link(dve.tensor_scalar(ends[:], sums[:, :, NT - 1], 1.0 / GB, None, ALU.mult))
                c.link(dve.tensor_tensor(full[:], bcast(ends[:], n_after=MOST), bcast(chip.count[:, 0:MOST], n_before=E8), ALU.is_gt))
                c.link(dve.tensor_reduce(blocks[:], full[:], AX_X, ALU.add))
                c.link(dve.tensor_tensor_scan(ends[:], one8[:], blocks[:], 0.0, ALU.mult, ALU.add))
                c.link(dve.tensor_tensor(base[:], ends[:], blocks[:], ALU.subtract))
                c.link(dve.tensor_scalar(base[:], base[:], float(GB), None, ALU.mult))
                c.link(dve.tensor_tensor(sums[:], sums[:], total[:], ALU.subtract))
                c.link(dve.tensor_tensor(sums[:], sums[:], bcast(base[:], n_after=NT), ALU.add))
                c.link(dve.tensor_tensor(where[:], chip.psum[1][:, 0:NT * E8].rearrange("p (t e) -> p t e", e=E8),
                                         sums[:].rearrange("p e t -> p t e"), ALU.add))
                for k in range(top):
                    c.link(dve.tensor_tensor(mine[:], where[:], picks[k][:], ALU.mult))
                    c.link(dve.tensor_reduce(slot[:, k, :], mine[:], AX_X, ALU.add))
                    dve.tensor_copy(slots[:, :, k], slot[:, k, :])
                c.link(dve.tensor_tensor(past[:], bcast(ends[:], n_before=NB), bcast(chip.count[:, 0:NB], n_after=E8), ALU.is_le))
                c.link(dve.tensor_reduce(number[:], past[:], AX_X, ALU.add))
                c.link(dve.tensor_scalar(number[:], number[:], float(E8 - 1), None, ALU.min))
                dve.tensor_copy(expert[:], number[:])
                if vectors:
                    c.link(dve.tensor_tensor(past[:], bcast(number[:], n_after=E8), bcast(chip.count[:, 0:E8], n_before=NB), ALU.is_equal))
                for n, v in vectors.items():
                    for e in range(E8):
                        dst = cols[n] if e == 0 else part
                        c.link(dve.tensor_tensor(dst[:], past[:, :, e:e + 1].to_broadcast([P, NB, J]),
                                                 bcast(v[:, e * J:(e + 1) * J], n_before=NB), ALU.mult))
                        if e:
                            c.link(dve.tensor_tensor(cols[n][:], cols[n][:], part[:], ALU.add))
    return slots, expert, cols


def send_to_slots(chip, ctx, L, top, xn_all, slots):
    nc = chip.nc
    with ExitStack() as inner:
        two = lambda name, shape, dt=F32: [chip.sb(inner, f"{L}s_{name}{u}", shape, dt) for u in range(2)]
        rows, to = two("rows", [P, TPS, D]), two("to", [P, TPS, top], U32)
        rows_ready, to_ready, sent = (Signal(chip.sem(f"{L}s_rows_ready"), 2), Signal(chip.sem(f"{L}s_to_ready"), 2),
                                      [chip.sem(f"{L}s_sent{u}") for u in range(2)])
        buffers_free = [chip.sem(f"{L}s_buffers_free{u}") for u in range(2)]
        SENDS = TPS * top
        with nc.Block() as block:
            def free(eng, i, u):
                eng.wait_ge(buffers_free[u], i + 1)

            @block.sync
            def _(sp):
                for u in range(2):
                    sp.sem_inc(buffers_free[u], 1)
                with sp.Fori(0, B // 2) as i:
                    for u in range(2):
                        sp.wait_ge(sent[u], (i + 1) * (16 * SENDS))
                        sp.sem_inc(buffers_free[u], 1)

            @block.scalar
            def _(act):
                with act.Fori(0, B // 2) as i:
                    for u in range(2):
                        free(act, i, u)
                        chip.apart(act)
                        rows_ready.by(act.copy(rows[u][:], seq_tiles(xn_all, i, u)))

            @block.vector
            def _(dve):
                with dve.Fori(0, B // 2) as i:
                    for u in range(2):
                        free(dve, i, u)
                        chip.apart(dve)
                        to_ready.by(dve.tensor_copy(to[u][:], seq_tiles(slots, i, u)))

            @block.gpsimd
            def _(pool):
                pool.wait_ge(chip.slots_zeroed, chip.SLOTS_ZEROED)
                with pool.Fori(0, B // 2) as i:
                    for u in range(2):
                        rows_ready.wait(pool, i, u)
                        to_ready.wait(pool, i, u)
                        chip.apart(pool)
                        for t in range(TPS):
                            for k in range(top):
                                pool.indirect_dma_start(chip.slot_x, bass.IndirectOffsetOnAxis(ap=to[u][:, t, k:k + 1], axis=0),
                                                        rows[u][:, t, :], None, bounds_check=SLOTS - 1).then_inc(sent[u], 16)
                for u in range(2):
                    pool.wait_ge(sent[u], (B // 2) * (16 * SENDS))


def block_experts(chip, L, NB, slot_y, expert, cols, w_in, w_out, act_fn, glu=None):
    nc = chip.nc
    Q = GB // P
    with ExitStack() as ctx:
        sb = lambda name, shape: chip.sb(ctx, f"{L}e_{name}", shape)
        two = lambda name, shape: [sb(f"{name}{u}", shape) for u in range(2)]
        sem = lambda name: chip.sem(f"{L}e_{name}")
        w1, w2 = two("w1", [P, F]), two("w2", [P, J, D])
        xs, xT, h, y = two("xs", [P, Q, D]), two("xT", [P, GB]), two("h", [P, J, GB]), two("y", [P, Q, D])
        order = [(("xT", u), 6 + u) for u in range(2)] + [(("y", u), 4 + u) for u in range(2)]
        warm, warmed = sb("warm", [P, 1]), sem("warmed")
        PAIRS = J // 2
        if glu:
            w_v, s_out = glu
            wv, so, w2s, g = two("wv", [P, F]), two("so", [P, D]), two("w2s", [P, J, D]), two("g", [P, J, GB])
            order += [((n, u, jj), base + jj) for u in range(2) for jj in range(PAIRS) for n, base in (("h", 0), ("v", 2))]
        else:
            w2s = w2
            order += [(("h", u, jj), 2 * u + jj) for u in range(2) for jj in range(PAIRS)]
        bk = Banks(sem, "psum", order)
        ps = lambda job: chip.psum[bk.place[job][0]]
        weights_in = [sem(f"weights_in_loaded{u}") for u in range(2)]
        weights_out = [sem(f"weights_out_loaded{u}") for u in range(2)]
        rows, stored = [sem(f"rows_loaded{u}") for u in range(2)], [sem(f"y_stored{u}") for u in range(2)]
        y_free = [sem(f"y_free{u}") for u in range(2)]
        scaled = Signal(sem("w_out_scaled"), 2)
        NW = 1 + bool(glu)
        last = "v" if glu else "h"
        one = lambda w, e: w[bass.ds(e, 1)]
        slot_rows = lambda a, i, u: a[bass.ds((i * 2 + u) * GB, GB), :].rearrange("(q p) d -> p q d", p=P)

        with nc.Block() as block:
            @block.sync
            def _(sp):
                def load_rows(i, u):
                    sp.dma_start(xs[u][:], slot_rows(chip.slot_x, i, u)).then_inc(rows[u], 16)
                    return sp.value_load(expert[0:1, bass.ds(i * 2 + u, 1)], min_val=0, max_val=E8 - 1)

                def load_in(e, u):
                    sp.dma_start(w1[u][:], one(w_in, e).rearrange("e k f -> (e k) f")).then_inc(weights_in[u], 16)
                    if glu:
                        sp.dma_start(wv[u][:], one(w_v, e).rearrange("e k f -> (e k) f")).then_inc(weights_in[u], 16)

                def load_out(e, u):
                    sp.dma_start(w2[u][:], one(w_out, e).rearrange("e (j p) d -> p (e j) d", p=P)).then_inc(weights_out[u], 16)
                    if glu:
                        sp.dma_start(so[u][:], one(s_out, e).rearrange("e o d -> (e o) d").partition_broadcast(P)).then_inc(weights_out[u], 16)

                for u in range(2):
                    e = load_rows(0, u)
                    load_in(e, u)
                    load_out(e, u)
                with sp.Fori(0, NB // 2 - 1) as i:
                    experts = []
                    for u in range(2):
                        bk.wait_filled(sp, ("xT", u), i)
                        chip.apart(sp)
                        experts.append(load_rows(i + 1, u))
                        bk.wait_filled(sp, (last, u, PAIRS - 1), i)
                        chip.apart(sp)
                        load_in(experts[u], u)
                    for u in range(2):
                        bk.wait_filled(sp, ("y", u), i)
                        chip.apart(sp)
                        load_out(experts[u], u)

            @block.gpsimd
            def _(pool):
                for u in range(2):
                    pool.sem_inc(y_free[u], 1)
                with pool.Fori(0, NB // 2) as i:
                    if glu:
                        for u in range(2):
                            pool.wait_ge(weights_out[u], (i + 1) * (16 * NW))
                            scaled.by(pool.tensor_tensor(w2s[u][:], w2[u][:], bcast(so[u][:], n_before=J), ALU.mult))
                    for u in range(2):
                        bk.wait_read(pool, ("y", u), i)
                        chip.apart(pool)
                        pool.dma_start(slot_rows(slot_y, i, u), y[u][:]).then_inc(stored[u], 16)
                    for u in range(2):
                        pool.wait_ge(stored[u], (i + 1) * 16)
                        pool.sem_inc(y_free[u], 1)

            @block.scalar
            def _(act):
                act.sem_inc(warmed, 1)
                with act.Fori(0, NB // 2) as i:
                    act.wait_ge(warmed, i + 1)
                    chip.apart(act)
                    act.activation(warm[:], chip.ones[:, 0:1], act_fn).then_inc(warmed, 1)
                    for u in range(2):
                        for jj in range(PAIRS):
                            job = ("h", u, jj)
                            bk.wait_filled(act, job, i)
                            chip.apart(act)
                            for j in (2 * jj, 2 * jj + 1):
                                col = lambda n: cols[n][:, bass.ds(i * 2 + u, 1), j:j + 1].rearrange("p a b -> p (a b)")
                                kw = {"scale": col("s")} if glu else {"bias": col("b1")}
                                ins = act.activation((g if glu else h)[u][:, j, :], ps(job)[:, (j % 2) * GB:(j % 2 + 1) * GB], act_fn, **kw)
                            bk.drain(ins, job)

            @block.vector
            def _(dve):
                with dve.Fori(0, NB // 2) as i:
                    for u in range(2):
                        job = ("xT", u)
                        bk.wait_filled(dve, job, i)
                        bk.drain(dve.tensor_copy(xT[u][:], ps(job)[:, 0:GB]), job)
                    for u in range(2 if glu else 0):
                        for jj in range(PAIRS):
                            job = ("v", u, jj)
                            bk.wait_filled(dve, job, i)
                            bk.wait_read(dve, ("h", u, jj), i)
                            for j in (2 * jj, 2 * jj + 1):
                                sv = cols["sv"][:, bass.ds(i * 2 + u, 1), j:j + 1].rearrange("p a b -> p (a b)")
                                ins = dve.scalar_tensor_tensor(h[u][:, j, :], ps(job)[:, (j % 2) * GB:(j % 2 + 1) * GB], sv,
                                                               g[u][:, j, :], ALU.mult, ALU.mult)
                            bk.drain(ins, job)
                    for u in range(2):
                        job = ("y", u)
                        dve.wait_ge(y_free[u], i + 1)
                        bk.wait_filled(dve, job, i)
                        bk.drain(dve.tensor_copy(y[u][:], ps(job)[:, 0:GB].rearrange("p (q d) -> p q d", q=Q)), job)

            @block.tensor
            def _(pe):
                bk.open(pe)
                with pe.Fori(0, NB // 2) as i:
                    for u in range(2):
                        job = ("xT", u)
                        pe.wait_ge(rows[u], (i + 1) * 16)
                        bk.wait_drained(pe, job, i)
                        for q in range(Q):
                            ins = pe.transpose(ps(job)[:, q * P:(q + 1) * P], xs[u][:, q, :], chip.ident[:])
                        bk.fill(ins, job)
                    for u in range(2):
                        bk.wait_read(pe, ("xT", u), i)
                        pe.wait_ge(weights_in[u], (i + 1) * (16 * NW))
                        for jj in range(PAIRS):
                            for n, w in (("h", w1),) + ((("v", wv),) if glu else ()):
                                job = (n, u, jj)
                                bk.wait_drained(pe, job, i)
                                for j in (2 * jj, 2 * jj + 1):
                                    ins = pe.matmul(ps(job)[:, (j % 2) * GB:(j % 2 + 1) * GB], w[u][:, j * P:(j + 1) * P], xT[u][:],
                                                    start=True, stop=True)
                                bk.fill(ins, job)
                    for u in range(2):
                        if glu:
                            scaled.wait(pe, i, u)
                        else:
                            pe.wait_ge(weights_out[u], (i + 1) * (16 * NW))
                        for jj in range(PAIRS):
                            bk.wait_read(pe, (last, u, jj), i)
                        job = ("y", u)
                        bk.wait_drained(pe, job, i)
                        for q in range(Q):
                            for j in range(J):
                                ins = pe.matmul(ps(job)[:, q * D:(q + 1) * D], h[u][:, j, q * P:(q + 1) * P], w2s[u][:, j, :],
                                                start=(j == 0), stop=(j == J - 1))
                        bk.fill(ins, job)


def fetch_answers(chip, L, top, slot_y, slots, pick_gates):
    nc = chip.nc
    with ExitStack() as inner:
        two = lambda name, shape, dt=F32: [chip.sb(inner, f"{L}f_{name}{u}", shape, dt) for u in range(2)]
        rows, at = two("rows", [P, top, TPS, D]), two("at", [P, TPS, top], U32)
        at_ready, added = Signal(chip.sem(f"{L}f_at_ready"), 2), Signal(chip.sem(f"{L}f_added"), 2 * top)
        fetched, dve_order = [chip.sem(f"{L}f_fetched{u}") for u in range(2)], chip.sem(f"{L}f_order")
        with nc.Block() as block:
            @block.scalar
            def _(act):
                act.sem_inc(added.sem, 2 * top)
                with act.Fori(0, B // 2) as i:
                    for u in range(2):
                        added.wait(act, i, u * top + top - 1)
                        chip.apart(act)
                        at_ready.by(act.copy(at[u][:], seq_tiles(slots, i, u)))

            @block.gpsimd
            def _(pool):
                with pool.Fori(0, B // 2) as i:
                    for u in range(2):
                        at_ready.wait(pool, i, u)
                        chip.apart(pool)
                        for k in range(top):
                            for t in range(TPS):
                                pool.indirect_dma_start(rows[u][:, k, t, :], None, slot_y,
                                                        bass.IndirectOffsetOnAxis(ap=at[u][:, t, k:k + 1], axis=0),
                                                        bounds_check=slot_y.shape[0] - 1).then_inc(fetched[u], 16)

            @block.vector
            def _(dve):
                with dve.Fori(0, B // 2) as i:
                    for u in range(2):
                        for k in range(top):
                            dve.wait_ge(fetched[u], i * (16 * TPS * top) + 16 * TPS * top)
                            if k:
                                added.wait(dve, i + 1, u * top + k - 1)
                            chip.apart(dve)
                            for t in range(TPS):
                                xs = one_tile(chip.x, i, u, t)
                                gate = pick_gates[:, k, bass.ds((i * 2 + u) * TPS + t, 1)]
                                ins = dve.scalar_tensor_tensor(xs, rows[u][:, k, t, :], gate, xs, ALU.mult, ALU.add)
                            added.by(ins)


def grouped_experts(chip, L, top, w_router, bias, vectors, b2, w_in, w_out, act_fn, glu=None):
    NB = blocks_of(top)
    with ExitStack() as ctx:
        slot_y = chip.nc.dram_tensor(f"{L}_slot_y", (NB * GB, D), F32, kind="Internal").ap()
        xn_all, cols = normalise_and_route(chip, ctx, L, w_router, vectors, rows_out=True)
        _, picks, pick_gates = route(chip, ctx, L, E8, bias, top=top, b2=b2)
        slots, expert, block_cols = place(chip, ctx, L, top, picks, cols)
        send_to_slots(chip, ctx, L, top, xn_all, slots)
        block_experts(chip, L, NB, slot_y, expert, block_cols, w_in, w_out, act_fn, glu=glu)
        fetch_answers(chip, L, top, slot_y, slots, pick_gates)


def top2_glu_experts(chip, w):
    flat = lambda a: a.rearrange("e o f -> (e o) f")
    grouped_experts(chip, "l0f", 2, w["router_w"], None, {"sv": by_tile(flat(w["sv"])), "s": by_tile(flat(w["s"]))}, None,
                    w["w"], w["w1"], ACT.Gelu_apprx_tanh, glu=(w["wv"], w["s1"]))


def switch_experts(chip, w):
    grouped_experts(chip, "l1f", 1, w["Wr"], w["br"], {"b1": by_tile(w["b1"])}, w["b2"], w["W1"], w["W2"], ACT.Relu)


def expert_choice_experts(chip, w):
    with ExitStack() as ctx:
        xnT, _ = normalise_and_route(chip, ctx, "l2f", w["gate_w"], {})
        gates = route(chip, ctx, "l2f", E8, None, capacity=2 * S // E8)
        dense_experts(chip, "l2f", xnT, gates, w["w1"], w["w2"], ACT.Gelu)


def threshold_experts(chip, w):
    with ExitStack() as ctx:
        xnT, cols = normalise_and_route(chip, ctx, "l3f", w["Wgt"], {"b1": by_tile(w["b1"])})
        gates = route(chip, ctx, "l3f", E8 + 1, w["bgt"], threshold=True, b2=w["b2"])
        dense_experts(chip, "l3f", xnT, gates, w["W1"], w["W2"], ACT.Gelu_apprx_tanh, b1=cols["b1"])


def normalise_all(chip, ctx, L):
    return normalise_and_route(chip, ctx, L, None, {})[0]



H3, DK3 = 16, 64
BUCKETS = 32


def relative_position_attention(chip, w):
    nc = chip.nc
    HP = H3 // 2
    UNITS = HP * B
    SPAN = 2 * S - 1
    GW = S + (TPS - 1) * P
    SCALE = float(H3) ** -0.5
    ctx = ExitStack()
    with ctx:
        sb = lambda name, shape: chip.sb(ctx, f"l3a_{name}", shape)
        two = lambda name, shape: [sb(f"{name}{u}", shape) for u in range(2)]
        sem = lambda name: chip.sem(f"l3a_{name}")
        xnT_all = normalise_all(chip, ctx, "l3a")
        by_distance = nc.dram_tensor("l3a_by_distance", (H3, SPAN + 1), F32, kind="Internal").ap()
        by_place = nc.dram_tensor("l3a_by_place", (H3, P, SPAN + 1), F32, kind="Internal").ap()

        w_qk, w_v, w_o = sb("w_qk", [P, 2, H3 * DK3]), sb("w_v", [P, H3 * DK3]), sb("w_o", [P, HP, D])
        xT, wqk = two("xT", [P, S]), two("wqk", [P, 2, P])
        q = two("q", [P, 2, S])
        kT = two("kT", [P, S])
        v = two("v", [P, TPS, 4, DK3])
        oT = two("oT", [P, S])
        bias = two("bias", [P, GW])
        sc, top, pT = two("sc", [P, TPS, S]), two("top", [P, TPS]), two("pT", [P, TPS, S])
        rden = sb("rden", [P, S])

        with ExitStack() as inner, nc.Block() as block:
            table = chip.sb(inner, "l3a_table", [BUCKETS, H3])
            onehot = chip.sb(inner, "l3a_onehot", [BUCKETS, SPAN + 1])
            line = chip.sb(inner, "l3a_line", [H3, SPAN + 1])
            loaded, summed, lined, stored = sem("table_loaded"), sem("summed"), sem("lined"), sem("line_stored")
            weights = sem("weights_loaded")

            @block.sync
            def _(sp):
                sp.dma_start(table[:], w["rel_bias"]).then_inc(loaded, 16)
                sp.dma_start(onehot[:], w["onehot"]).then_inc(loaded, 16)
                sp.wait_ge(lined, 2)
                sp.dma_start(by_distance, line[:]).then_inc(stored, 16)
                sp.wait_ge(stored, 16)
                for h in range(H3):
                    src = bass.AP(by_distance.tensor, h * (SPAN + 1), [[0, P], [1, SPAN + 1]])
                    sp.dma_start(by_place[h], src).then_inc(stored, 16)
                sp.wait_ge(stored, 16 * (1 + H3))

            @block.scalar
            def _(act):
                act.dma_start(w_qk[:, 0, :], w["Wq"]).then_inc(weights, 16)
                act.dma_start(w_qk[:, 1, :], w["Wk"]).then_inc(weights, 16)
                act.dma_start(w_v[:], w["Wv"]).then_inc(weights, 16)
                act.dma_start(w_o[:], w["Wo"].rearrange("(g p) d -> p g d", p=P)).then_inc(weights, 16)
                act.wait_ge(weights, 64)

            @block.tensor
            def _(pe):
                pe.wait_ge(loaded, 32)
                for c in range(2):
                    pe.matmul(chip.psum[c][0:H3, :], table[:], onehot[:, c * S:(c + 1) * S], start=True, stop=True).then_inc(summed, 1)

            @block.vector
            def _(dve):
                for u in range(2):
                    dve.memset(v[u][:, :, 1:3, :], 1.0)
                    dve.memset(q[u][DK3:, 0, :], 0.0)
                    dve.memset(q[u][0:DK3, 1, :], 0.0)
                dve.memset(oT[1][0:DK3, :], 0.0)
                dve.memset(v[1][:, 0, 3, :], 0.0)
                dve.memset(pT[1][:, 0, :], 1.0)
                for c in range(2):
                    dve.wait_ge(summed, c + 1)
                    dve.tensor_copy(line[:, c * S:(c + 1) * S], chip.psum[c][0:H3, :]).then_inc(lined, 1)

        order = [("q", 4), ("k", 4), ("v", 4), ("y", 5)]
        for hh in range(2):
            order += [(("s", hh, t), t % 2) for t in range(TPS)]
            order += [(("t", hh, t), 2 + t % 2) for t in range(TPS)]
            order += [(("av", hh), 6 + hh)]
        bk = Banks(sem, "psum", order)
        ps = lambda job: chip.psum[bk.place[job][0]]
        xT_ready, less_ready = Signal(sem("xT_ready"), 1), Signal(sem("less_ready"), 2)
        bias_loaded = [sem(f"bias_loaded{hh}") for hh in range(2)]
        dve_order = sem("dve_order")
        SEQ_BITS = B.bit_length() - 1
        pair = lambda g: (g >> SEQ_BITS) & (HP - 1)
        sequence = lambda g: g & (B - 1)
        rows = [slice(0, DK3), slice(DK3, P)]

        with nc.Block() as block:
            @block.sync
            def _(sp):
                def load(h, hh):
                    src = bass.AP(by_place.tensor, h * (P * (SPAN + 1)) + (P - 1), [[SPAN, P], [1, GW]])
                    sp.dma_start(bias[hh][:], src).then_inc(bias_loaded[hh], 16)

                for hh in range(2):
                    load(hh, hh)
                with sp.Fori(1, HP + 1) as hp:
                    for hh in range(2):
                        less_ready.wait(sp, hp * B - 1, hh)
                        chip.apart(sp)
                        load((hp & (HP - 1)) * 2 + hh, hh)
                for hh in range(2):
                    sp.wait_ge(bias_loaded[hh], 16 * (HP + 1))

            @block.gpsimd
            def _(pool):
                def prepare(g, u):
                    pool.tensor_copy(wqk[u][:], w_qk[:, :, bass.ds(pair(g) * P, P)])
                    xT_ready.by(pool.tensor_copy(xT[u][:], xnT_all[:, bass.ds(sequence(g) * S, S)]))

                prepare(0, 0)
                with pool.Fori(0, UNITS // 2) as i:
                    for u in range(2):
                        g = i * 2 + u
                        bk.wait_drained(pool, "v", g)
                        prepare(g + 1, 1 - u)

            @block.vector
            def _(dve):
                c = Chain(dve, dve_order, per_turn=2)

                def less_maximum(g, hh):
                    dve.wait_ge(bias_loaded[hh], ((g >> SEQ_BITS) + 1) * 16)
                    chip.apart(dve)
                    for t in range(TPS):
                        job = ("s", hh, t)
                        bk.wait_filled(dve, job, g)
                        chip.apart(dve)
                        b0 = (TPS - 1 - t) * P
                        bk.drain(dve.tensor_tensor_reduce(sc[hh][:, t, :], ps(job)[:], bias[hh][:, b0:b0 + S], 1.0, -3.0e38,
                                                          ALU.add, ALU.max, top[hh][:, t:t + 1]), job)
                    bk.wait_read(dve, ("s", hh, TPS - 2), g)
                    bk.wait_read(dve, ("s", hh, TPS - 1), g)
                    for t in range(TPS):
                        ins = dve.tensor_scalar(sc[hh][:, t, :], sc[hh][:, t, :], top[hh][:, t:t + 1], None, ALU.subtract)
                    less_ready.by(ins)

                def normalise(g, u, hh):
                    job = ("av", hh)
                    bk.wait_filled(dve, job, g)
                    c.link(dve.reciprocal(rden[rows[hh], :], ps(job)[rows[1 - hh], :]))
                    bk.drain(dve.tensor_tensor(oT[u][rows[hh], :], ps(job)[rows[hh], :], rden[rows[hh], :], ALU.mult), job)

                def add(g):
                    bk.wait_filled(dve, "y", g)
                    xs = chip.x[:, bass.ds(sequence(g + (B - 1)) * TPS, TPS), :]
                    bk.drain(dve.tensor_tensor(xs, ps("y")[:].rearrange("p (t d) -> p t d", t=TPS), xs, ALU.add), "y")

                less_maximum(0, 0)
                with dve.Fori(0, UNITS // 2) as i:
                    for u in range(2):
                        g = i * 2 + u
                        c.start(g)
                        less_maximum(g, 1)
                        normalise(g, 1 - u, 1)
                        add(g)
                        less_maximum(g + 1, 0)
                        normalise(g, u, 0)
                        c.end()
                c.start(UNITS)
                normalise(UNITS, 1, 1)
                add(UNITS)

            @block.scalar
            def _(act):
                def take(g, u, job):
                    bk.wait_filled(act, job, g)
                    a = ps(job)
                    if job == "q":
                        act.mul(q[u][rows[0], 0, :], a[rows[0], :], SCALE)
                        ins = act.mul(q[u][rows[1], 1, :], a[rows[1], :], SCALE)
                    elif job == "k":
                        ins = act.copy(kT[u][:], a[:])
                    else:
                        for hh in range(2):
                            ins = act.copy(v[u][:, :, 3 * hh, :], a[:].rearrange("p (t h d) -> p t h d", h=2, d=DK3)[:, :, hh, :])
                    bk.drain(ins, job)

                def exponentials(g, hh):
                    for t in range(TPS):
                        job = ("t", hh, t)
                        bk.wait_filled(act, job, g)
                        bk.drain(act.activation(pT[hh][:, t, :], ps(job)[:], ACT.Exp), job)

                for job in ("q", "k", "v"):
                    take(0, 0, job)
                with act.Fori(0, UNITS // 2) as i:
                    for u in range(2):
                        g = i * 2 + u
                        take(g + 1, 1 - u, "q")
                        exponentials(g, 0)
                        take(g + 1, 1 - u, "k")
                        take(g + 1, 1 - u, "v")
                        exponentials(g, 1)

            @block.tensor
            def _(pe):
                bk.open(pe)

                def project(g, u, job):
                    bk.wait_drained(pe, job, g)
                    if job == "v":
                        for t in range(TPS):
                            ins = pe.matmul(ps(job)[:, t * P:(t + 1) * P], xT[u][:, t * P:(t + 1) * P],
                                            w_v[:, bass.ds(pair(g) * P, P)], start=True, stop=True)
                    else:
                        xT_ready.wait(pe, g, 0)
                        ins = pe.matmul(ps(job)[:], wqk[u][:, int(job == "k"), :], xT[u][:], start=True, stop=True)
                    bk.fill(ins, job)

                def scores(g, u, hh):
                    bk.wait_read(pe, "k", g)
                    for t in range(TPS):
                        job = ("s", hh, t)
                        bk.wait_drained(pe, job, g)
                        bk.fill(pe.matmul(ps(job)[:], q[u][:, hh, t * P:(t + 1) * P], kT[u][:], start=True, stop=True), job)

                def turn_scores(g, hh):
                    less_ready.wait(pe, g, hh)
                    for kt in range(TPS):
                        job = ("t", hh, kt)
                        bk.wait_drained(pe, job, g)
                        for t in range(TPS):
                            ins = pe.transpose(ps(job)[:, t * P:(t + 1) * P], sc[hh][:, t, kt * P:(kt + 1) * P], chip.ident[:])
                        bk.fill(ins, job)

                def weigh(g, u, hh):
                    job = ("av", hh)
                    bk.wait_drained(pe, job, g + hh)
                    bk.wait_read(pe, "v", g)
                    for kt in range(TPS):
                        bk.wait_read(pe, ("t", hh, kt), g)
                        ins = pe.matmul(ps(job)[:], v[u][:, kt, 2 * hh:2 * hh + 2, :].rearrange("p a d -> p (a d)"),
                                        pT[hh][:, kt, :], start=(kt == 0), stop=(kt == TPS - 1))
                    bk.fill(ins, job)

                def answer(g, u):
                    bk.wait_read(pe, ("av", 0), g - 1)
                    bk.wait_read(pe, ("av", 1), g)
                    bk.wait_drained(pe, "y", g)
                    for t in range(TPS):
                        ins = pe.matmul(ps("y")[:, t * D:(t + 1) * D], oT[u][:, t * P:(t + 1) * P],
                                        w_o[:, bass.ds(pair(g + (UNITS - 1)), 1), :].rearrange("p a d -> p (a d)"), start=True, stop=True)
                    bk.fill(ins, "y")

                job = ("av", 1)
                bk.wait_drained(pe, job, 0)
                bk.fill(pe.matmul(ps(job)[:], v[1][:, 0, 2:4, :].rearrange("p a d -> p (a d)"), pT[1][:, 0, :], start=True, stop=True), job)
                for job in ("q", "k", "v"):
                    project(0, 0, job)
                scores(0, 0, 0)
                with pe.Fori(0, UNITS // 2) as i:
                    for u in range(2):
                        g = i * 2 + u
                        scores(g, u, 1)
                        project(g + 1, 1 - u, "q")
                        turn_scores(g, 0)
                        project(g + 1, 1 - u, "k")
                        weigh(g, u, 0)
                        answer(g, 1 - u)
                        scores(g + 1, 1 - u, 0)
                        project(g + 1, 1 - u, "v")
                        turn_scores(g, 1)
                        weigh(g, u, 1)
                answer(UNITS, 1)


def buckets_by_distance():
    half, exact = BUCKETS // 2, BUCKETS // 4
    hot = np.zeros((BUCKETS, 2 * S), np.float32)
    for n in range(2 * S - 1):
        far = abs(n - (S - 1))
        if far < exact:
            bucket = far
        else:
            bucket = exact
            while bucket < half - 1 and far * far >= exact * exact * 2 ** (bucket + 1 - exact):
                bucket += 1
        hot[bucket + half * (n > S - 1), n] = 1.0
    return hot



def feature_attention(chip, w):
    nc = chip.nc
    H, DH = 16, 8
    M = w["proj"].shape[1]
    HM = H * M
    NCH = HM // P
    HC = H // NCH
    DC = HC * DH
    CW = DC + HC
    DN = float(DH) ** -0.25
    RATIO = float(M) ** -0.5
    EPS = 1e-4
    HALF = TPS // 2
    ctx = ExitStack()
    with ctx:
        sb = lambda name, shape: chip.sb(ctx, f"l1a_{name}", shape)
        two = lambda name, shape: [sb(f"{name}{u}", shape) for u in range(U)]
        sem = lambda name: chip.sem(f"l1a_{name}")
        wq, wk, wv, wo, wfc = (sb(n, [P, D]) for n in ("wq", "wk", "wv", "wo", "wfc"))
        bq, bk_, bo = (sb(n, [P, 1]) for n in ("bq", "bk", "bo"))
        bv, bfc = sb("bv", [P, D]), sb("bfc", [P, D])
        proj, spread = sb("proj", [DH, M]), sb("spread", [DH, P])
        head_of, half_head, own = sb("head_of", [P, H]), sb("half_head", [P, H]), sb("own", [P, CW])
        feat = sb("feat", [P, H, M])
        stats, mv = two("stats", [P, TPS, 6]), two("mv", [P, TPS, 2])
        std, rstd = two("std", [P, TPS]), two("rstd", [P, TPS])
        xn, xnT = two("xn", [P, TPS, D]), two("xnT", [P, S])
        qk = [[sb(f"{n}{u}", [P, S]) for n in ("q", "k")] for u in range(U)]
        sqs = [[sb(f"{n}{u}", [P, S]) for n in ("qsq", "ksq")] for u in range(U)]
        v = two("v", [P, TPS, NCH, DC + 1])
        mq, mk = two("mq", [P, TPS, H]), two("mk", [P, TPS, H])
        dg, mkr = two("dg", [P, 2, TPS, H]), two("mkr", [P, H])
        mk1, mkd = two("mk1", [H, 1]), two("mkd", [H, H])
        f = [[sb(f"f{n}{u}", [P, TPS, H, M]) for n in "qk"] for u in range(U)]
        cx = two("cx", [P, NCH, CW])
        fT = two("fT", [P, NCH, S])
        rden, o, oT = two("rden", [P, TPS, NCH, HC]), two("o", [P, TPS, D]), two("oT", [P, S])
        hT, y = two("hT", [P, S]), two("y", [P, TPS, D])

        order = [(("xT", u), 6 + u) for u in range(U)]
        for u in range(U):
            order += [(("q", u), 6), (("k", u), 7), (("v", u), 4)]
        for u in range(U):
            order += [(("dg", u), 5)] + [(("f", u, n, c), 2 * n + c) for n in range(2) for c in range(2)]
            order += [(("mT", u), 4), (("mb", u), 5)]
        order += [(("cx", u), 4) for u in range(U)]
        order += [(("fT", u, c), 6 + c) for u in range(U) for c in range(NCH)]
        order += [(("o", u, c), c) for u in range(U) for c in range(2)]
        order += [(("oT", u), 2) for u in range(U)] + [(("hT", u), 3) for u in range(U)] + [(("y", u), 5) for u in range(U)]
        bk = Banks(sem, "psum", order)
        ps = lambda job: chip.psum[bk.place[job][0]]
        weights, feat_filled, feat_ready = sem("weights_loaded"), sem("feat_filled"), sem("feat_ready")
        step = lambda name, n=1: Signal(sem(name), U * n)
        mv_ready, std_ready, xn_ready = step("mv_ready"), step("std_ready"), step("xn_ready")
        qk_ready, sq_ready, shifted, f_exp, f_ready = (step("qk_ready", 2), step("sq_ready", 2), step("shifted", 2),
                                                       step("f_exp", 2), step("f_ready", 2))
        mkr_ready, mkd_ready, cx_ready, o_ready = step("mkr_ready"), step("mkd_ready"), step("cx_ready"), step("o_ready")
        dve_order = sem("dve_order")
        TURNS = B // U
        NWT = 5 + 3 + 2 + 2 + 3

        with nc.Block() as block:
            @block.sync
            def _(sp):
                for t, n in ((wq, "Wq"), (wk, "Wk"), (wv, "Wv"), (wo, "Wo"), (wfc, "Wfc"), (proj, "proj"), (spread, "spread"),
                             (head_of, "head_of"), (half_head, "half_head"), (own, "own")):
                    sp.dma_start(t[:], w[n]).then_inc(weights, 16)
                for t, n in ((bq, "bq"), (bk_, "bk"), (bo, "bo")):
                    sp.dma_start(t[:], w[n].rearrange("(p o) -> p o", o=1)).then_inc(weights, 16)
                for t, n in ((bv, "bv"), (bfc, "bfc")):
                    sp.dma_start(t[:], w[n].partition_broadcast(P)).then_inc(weights, 16)

            @block.vector
            def _(dve):
                c = Chain(dve, dve_order, per_turn=U * 10)
                for u in range(U):
                    dve.memset(v[u][:, :, :, DC:], 1.0)
                dve.wait_ge(weights, 16 * NWT)
                dve.wait_ge(feat_filled, 1)
                dve.tensor_tensor(feat[:], bcast(head_of[:], n_after=M), bcast(chip.psum[0][:, 0:M], n_before=H),
                                  ALU.mult).then_inc(feat_ready, 1)
                with dve.Fori(0, TURNS) as i:
                    c.start(i)
                    for u in range(U):
                        mv_ready.by(ln_statistics(chip, dve, c, lambda t: one_tile(chip.x, i, u, t), stats[u], mv[u], TPS))
                    for u in range(U):
                        std_ready.wait(dve, i, u)
                        c.link(dve.reciprocal(rstd[u][:], std[u][:]))
                        for t in range(TPS):
                            ins = dve.tensor_scalar(xn[u][:, t, :], one_tile(chip.x, i, u, t), mv[u][:, t, 0:1],
                                                    rstd[u][:, t:t + 1], ALU.subtract, ALU.mult)
                        xn_ready.by(ins)
                    for u in range(U):
                        for n, (nm, b_) in enumerate((("q", bq), ("k", bk_))):
                            bk.wait_filled(dve, (nm, u), i)
                            qk_ready.by(dve.tensor_scalar(qk[u][n][:], ps((nm, u))[:], b_[:], DN, ALU.add, ALU.mult))
                            qk_ready.wait(dve, i, 2 * u + n)
                            bk.drain(dve.tensor_tensor(sqs[u][n][:], qk[u][n][:], qk[u][n][:], ALU.mult), (nm, u))
                        bk.wait_filled(dve, ("v", u), i)
                        for c2 in range(NCH):
                            ins = dve.tensor_tensor(v[u][:, :, c2, 0:DC],
                                                    ps(("v", u))[:].rearrange("p (t c d) -> p t c d", t=TPS, c=NCH)[:, :, c2, :],
                                                    bcast(bv[:, c2 * DC:(c2 + 1) * DC], n_before=TPS), ALU.add)
                        bk.drain(ins, ("v", u))
                    for u in range(U):
                        bk.wait_filled(dve, ("dg", u), i)
                        bk.drain(dve.tensor_copy(dg[u][:], ps(("dg", u))[:, 0:2 * TPS * H].rearrange("p (n t h) -> p n t h", n=2, h=H)), ("dg", u))
                        bk.wait_read(dve, ("dg", u), i)
                        for n, m in ((0, mq), (1, mk)):
                            for c2 in range(2):
                                bk.wait_filled(dve, ("f", u, n, c2), i)
                                fp = ps(("f", u, n, c2))[:].rearrange("p (t h m) -> p t h m", t=HALF, h=H)
                                c.link(dve.tensor_reduce(m[u][:, c2 * HALF:(c2 + 1) * HALF, :], fp, AX_X, ALU.max))
                        mkr_ready.by(dve.tensor_reduce(mkr[u][:], mk[u][:].rearrange("p t h -> p h t"), AX_X, ALU.max))
                        c.link(dve.tensor_tensor(mq[u][:], mq[u][:], dg[u][:, 0], ALU.add))
                        for c2 in range(2):
                            fp = ps(("f", u, 0, c2))[:].rearrange("p (t m) -> p t m", m=M)
                            ts = slice(c2 * HALF, (c2 + 1) * HALF)
                            ins = dve.tensor_tensor(f[u][0][:, ts].rearrange("p t h m -> p (t h) m"), fp,
                                                    bcast(mq[u][:, ts].rearrange("p t h -> p (t h)"), n_after=M), ALU.subtract)
                            bk.drain(ins, ("f", u, 0, c2))
                        bk.wait_read(dve, ("f", u, 0, 1), i)
                        dve.sem_inc(shifted.sem, 1)
                        bk.wait_filled(dve, ("mT", u), i)
                        ins = dve.tensor_reduce(mk1[u][:], ps(("mT", u))[0:H, 0:P], AX_X, ALU.max)
                        bk.drain(ins, ("mT", u))
                        bk.wait_read(dve, ("mT", u), i)
                        mkd_ready.by(dve.tensor_scalar(mkd[u][:], chip.ident[0:H, 0:H], mk1[u][:], None, ALU.mult))
                        bk.wait_filled(dve, ("mb", u), i)
                        ins = dve.tensor_tensor(mk[u][:], dg[u][:, 1], bcast(ps(("mb", u))[:, 0:H], n_before=TPS), ALU.add)
                        bk.drain(ins, ("mb", u))
                        bk.wait_read(dve, ("mb", u), i)
                        for c2 in range(2):
                            fp = ps(("f", u, 1, c2))[:].rearrange("p (t m) -> p t m", m=M)
                            ts = slice(c2 * HALF, (c2 + 1) * HALF)
                            ins = dve.tensor_tensor(f[u][1][:, ts].rearrange("p t h m -> p (t h) m"), fp,
                                                    bcast(mk[u][:, ts].rearrange("p t h -> p (t h)"), n_after=M), ALU.subtract)
                            bk.drain(ins, ("f", u, 1, c2))
                        bk.wait_read(dve, ("f", u, 1, 1), i)
                        dve.sem_inc(shifted.sem, 1)
                    for u in range(U):
                        for n in range(2):
                            f_exp.wait(dve, i, 2 * u + n)
                            f_ready.by(dve.tensor_scalar(f[u][n][:], f[u][n][:], EPS, RATIO, ALU.add, ALU.mult))
                    for u in range(U):
                        bk.wait_filled(dve, ("cx", u), i)
                        for c2 in range(NCH):
                            a = ps(("cx", u))[:, c2 * (DC + 1):(c2 + 1) * (DC + 1)]
                            dve.tensor_tensor(cx[u][:, c2, 0:DC], a[:, 0:DC], own[:, 0:DC], ALU.mult)
                            ins = dve.tensor_tensor(cx[u][:, c2, DC:], a[:, DC:].to_broadcast([P, HC]), own[:, DC:], ALU.mult)
                        bk.drain(ins, ("cx", u))
                    for u in range(U):
                        for c2 in range(2):
                            job = ("o", u, c2)
                            bk.wait_filled(dve, job, i)
                            a = ps(job)[:, 0:HALF * NCH * CW].rearrange("p (t w) -> p t w", w=CW)
                            rd = rden[u][:, c2 * HALF:(c2 + 1) * HALF].rearrange("p t c h -> p (t c) h")
                            c.link(dve.reciprocal(rd, a[:, :, DC:]))
                            for k in range(HALF * NCH):
                                t, ch = c2 * HALF + k // NCH, k % NCH
                                ins = dve.tensor_tensor(o[u][:, t, ch * DC:(ch + 1) * DC].rearrange("p (h d) -> p h d", d=DH),
                                                        a[:, k, 0:DC].rearrange("p (h d) -> p h d", d=DH),
                                                        bcast(rd[:, k, :], n_after=DH), ALU.mult)
                            bk.drain(ins, job)
                    for u in range(U):
                        job = ("y", u)
                        bk.wait_filled(dve, job, i)
                        ins = dve.tensor_tensor(y[u][:], ps(job)[:].rearrange("p (t d) -> p t d", t=TPS), bcast(bfc[:], n_before=TPS), ALU.add)
                        bk.drain(ins, job)
                        bk.wait_read(dve, job, i)
                        xs = seq_tiles(chip.x, i, u)
                        c.link(dve.scalar_tensor_tensor(xs, y[u][:], 0.0, xs, ALU.max, ALU.add))
                c.end()

            @block.scalar
            def _(act):
                act.wait_ge(weights, 16 * NWT)
                with act.Fori(0, TURNS) as i:
                    for u in range(U):
                        mv_ready.wait(act, i, u)
                        std_ready.by(act.activation(std[u][:], mv[u][:, :, 1], ACT.Sqrt, bias=chip.ln_eps[:]))
                    for u in range(U):
                        bk.wait_filled(act, ("xT", u), i)
                        bk.drain(act.copy(xnT[u][:], ps(("xT", u))[:]), ("xT", u))
                    for u in range(U):
                        for n in range(2):
                            shifted.wait(act, i, 2 * u + n)
                            f_exp.by(act.activation(f[u][n][:], f[u][n][:], ACT.Exp))
                    for u in range(U):
                        for c2 in range(NCH):
                            bk.wait_filled(act, ("fT", u, c2), i)
                            bk.drain(act.copy(fT[u][:, c2, :], ps(("fT", u, c2))[:]), ("fT", u, c2))
                    for u in range(U):
                        bk.wait_filled(act, ("oT", u), i)
                        bk.drain(act.copy(oT[u][:], ps(("oT", u))[:]), ("oT", u))
                    for u in range(U):
                        bk.wait_filled(act, ("hT", u), i)
                        bk.drain(act.activation(hT[u][:], ps(("hT", u))[:], ACT.Identity, bias=bo[:]), ("hT", u))

            @block.tensor
            def _(pe):
                bk.open(pe)
                pe.wait_ge(weights, 16 * NWT)
                pe.matmul(chip.psum[0][:, 0:M], spread[:], proj[:], start=True, stop=True).then_inc(feat_filled, 1)
                pe.wait_ge(feat_ready, 1)
                chip.apart(pe)
                with pe.Fori(0, TURNS) as i:
                    for u in range(U):
                        xn_ready.wait(pe, i, u)
                        bk.wait_drained(pe, ("xT", u), i)
                        for t in range(TPS):
                            ins = pe.transpose(ps(("xT", u))[:, t * P:(t + 1) * P], xn[u][:, t, :], chip.ident[:])
                        bk.fill(ins, ("xT", u))
                    for u in range(U):
                        bk.wait_read(pe, ("xT", u), i)
                        for nm, wt in (("q", wq), ("k", wk)):
                            bk.wait_drained(pe, (nm, u), i)
                            bk.fill(pe.matmul(ps((nm, u))[:], wt[:], xnT[u][:], start=True, stop=True), (nm, u))
                        bk.wait_drained(pe, ("v", u), i)
                        for t in range(TPS):
                            ins = pe.matmul(ps(("v", u))[:, t * D:(t + 1) * D], xnT[u][:, t * P:(t + 1) * P], wv[:], start=True, stop=True)
                        bk.fill(ins, ("v", u))
                    for u in range(U):
                        bk.wait_read(pe, ("k", u), i)
                        bk.wait_drained(pe, ("dg", u), i)
                        for n in range(2):
                            for t in range(TPS):
                                ins = pe.matmul(ps(("dg", u))[:, (n * TPS + t) * H:(n * TPS + t + 1) * H],
                                                sqs[u][n][:, t * P:(t + 1) * P], half_head[:], start=True, stop=True)
                        bk.fill(ins, ("dg", u))
                        for n in range(2):
                            for c2 in range(2):
                                job = ("f", u, n, c2)
                                bk.wait_drained(pe, job, i)
                                for tt in range(HALF):
                                    t = c2 * HALF + tt
                                    ins = pe.matmul(ps(job)[:, tt * HM:(tt + 1) * HM], qk[u][n][:, t * P:(t + 1) * P],
                                                    feat[:].rearrange("p h m -> p (h m)"), start=True, stop=True)
                                bk.fill(ins, job)
                        mkr_ready.wait(pe, i, u)
                        bk.wait_drained(pe, ("mT", u), i)
                        bk.fill(pe.transpose(ps(("mT", u))[0:H, 0:P], mkr[u][:], chip.ident[:]), ("mT", u))
                        mkd_ready.wait(pe, i, u)
                        bk.wait_drained(pe, ("mb", u), i)
                        bk.fill(pe.matmul(ps(("mb", u))[:, 0:H], chip.ones[0:H, :], mkd[u][:], start=True, stop=True), ("mb", u))
                    for u in range(U):
                        f_ready.wait(pe, i, 2 * u + 1)
                        bk.wait_read(pe, ("v", u), i)
                        bk.wait_drained(pe, ("cx", u), i)
                        for c2 in range(NCH):
                            for t in range(TPS):
                                ins = pe.matmul(ps(("cx", u))[:, c2 * (DC + 1):(c2 + 1) * (DC + 1)],
                                                f[u][1][:, t, c2 * HC:(c2 + 1) * HC, :].rearrange("p h m -> p (h m)"),
                                                v[u][:, t, c2, :], start=(t == 0), stop=(t == TPS - 1))
                        bk.fill(ins, ("cx", u))
                    for u in range(U):
                        f_ready.wait(pe, i, 2 * u)
                        for c2 in range(NCH):
                            bk.wait_drained(pe, ("fT", u, c2), i)
                            for t in range(TPS):
                                ins = pe.transpose(ps(("fT", u, c2))[:, t * P:(t + 1) * P],
                                                   f[u][0][:, t, c2 * HC:(c2 + 1) * HC, :].rearrange("p h m -> p (h m)"), chip.ident[:])
                            bk.fill(ins, ("fT", u, c2))
                    for u in range(U):
                        bk.wait_read(pe, ("cx", u), i)
                        for c2 in range(NCH):
                            bk.wait_read(pe, ("fT", u, c2), i)
                        for c2 in range(2):
                            job = ("o", u, c2)
                            bk.wait_drained(pe, job, i)
                            for k in range(HALF * NCH):
                                t, ch = c2 * HALF + k // NCH, k % NCH
                                ins = pe.matmul(ps(job)[:, k * CW:(k + 1) * CW], fT[u][:, ch, t * P:(t + 1) * P], cx[u][:, ch, :],
                                                start=True, stop=True)
                            bk.fill(ins, job)
                    for u in range(U):
                        for c2 in range(2):
                            bk.wait_read(pe, ("o", u, c2), i)
                        bk.wait_drained(pe, ("oT", u), i)
                        for t in range(TPS):
                            ins = pe.transpose(ps(("oT", u))[:, t * P:(t + 1) * P], o[u][:, t, :], chip.ident[:])
                        bk.fill(ins, ("oT", u))
                    for u in range(U):
                        bk.wait_read(pe, ("oT", u), i)
                        bk.wait_drained(pe, ("hT", u), i)
                        bk.fill(pe.matmul(ps(("hT", u))[:], wo[:], oT[u][:], start=True, stop=True), ("hT", u))
                    for u in range(U):
                        bk.wait_read(pe, ("hT", u), i)
                        bk.wait_drained(pe, ("y", u), i)
                        for t in range(TPS):
                            ins = pe.matmul(ps(("y", u))[:, t * D:(t + 1) * D], hT[u][:, t * P:(t + 1) * P], wfc[:], start=True, stop=True)
                        bk.fill(ins, ("y", u))



def selective_scan(chip, w):
    nc = chip.nc
    W = 4
    DI, N, R = 256, 16, 8
    CH = DI // P
    TAPS = 4
    FINISH_AT, ADD_AT = 2, 5
    AHEAD = 4
    PART = 32
    ctx = ExitStack()
    with ctx:
        sb = lambda name, shape, dt=F32: chip.sb(ctx, f"l2a_{name}", shape, dt)
        each = lambda name, shape, dt=F32: [sb(f"{name}{u}", shape, dt) for u in range(W)]
        sem = lambda name: chip.sem(f"l2a_{name}")
        w_in, w_x, w_dt, w_out = sb("w_in", [P, 2 * DI]), sb("w_x", [P, CH, R + 2 * N]), sb("w_dt", [R, DI]), sb("w_out", [P, CH, D])
        ln_w, ln_b = sb("ln_w", [P, 1]), sb("ln_b", [P, 1])
        conv_w, conv_b, b_dt, d_par = sb("conv_w", [P, CH, TAPS]), sb("conv_b", [P, CH]), sb("b_dt", [P, CH]), sb("d_par", [P, CH])
        a_log, a_neg = sb("a_log", [P, CH, N]), sb("a_neg", [P, CH, N])
        part_of = sb("part_of", [P, 2 * N])
        pick = sb("pick", [P, 2 * N, P], BF16)
        stats, mv, std, rstd = (each(n, [P, TPS, k]) for n, k in (("stats", 6), ("mv", 2), ("std", 1), ("rstd", 1)))
        stats2, mv2, std2, rstd2 = (each(n, [P, TPS, k]) for n, k in (("stats2", 6), ("mv2", 2), ("std2", 1), ("rstd2", 1)))
        rows = each("rows", [P, TPS, D])
        turned = each("turned", [P, S])
        xi = each("xi", [P, CH, S + TAPS - 1])
        work = each("work", [P, CH, S])
        xc, sz, dt = each("xc", [P, CH, S]), each("sz", [P, CH, S]), each("dt", [P, CH, S])
        bc = each("bc", [P, S], BF16)
        mid = [sb(f"mid{u}", [2 * N, S], BF16) for u in range(W)]
        NB, NH = 3, 2
        dA, dBu = ([sb(f"{n}{k}", [P, CH, S]) for k in range(NB)] for n in ("dA", "dBu"))
        bs = [sb(f"bs{k}", [P, S]) for k in range(NB)]
        h, hc = ([sb(f"{n}{k}", [P, CH, S]) for k in range(NH)] for n in ("h", "hc"))
        xn = [a[:, 0, :].rearrange("p (t d) -> p t d", d=D) for a in work]
        dtr = [a[0:R, :] for a in turned]
        left = [a[0:2 * N].rearrange("p t d -> p (t d)") for a in rows]
        y_bank = lambda u: 4 + 2 * (u % 2)

        order = [(("xT", u), 4 + u) for u in range(W)]
        order += [(("in", u, j), (2 * CH * u + j) % 4) for u in range(W) for j in range(2 * CH)]
        order += [(("bc", u), 4 + u) for u in range(W)]
        order += [(("dt", u, j), (CH * u + j) % 4) for u in range(W) for j in range(CH)]
        states = [(u, n) for u in range(W) for n in range(N)]
        for m in range(len(states)):
            order += [(("B", m), m % 2), (("C", m), 2 + m % 2)]
        for u in range(W):
            order += [(("y", u, j), y_bank(u) + j) for j in range(CH)] + [(("out", u), y_bank(u))]
        bk = Banks(sem, "psum", order)
        ps = lambda job: chip.psum[bk.place[job][0]]
        weights, a_ready, zeroed, pick_ready = sem("weights_loaded"), sem("a_ready"), sem("zeroed"), sem("pick_ready")
        step = lambda name, n=1: Signal(sem(name), W * n)
        mv_ready, std_ready, mv2_ready, std2_ready, xm_ready = (step("mv_ready"), step("std_ready"), step("mv2_ready"),
                                                                step("std2_ready"), step("xm_ready"))
        conv_ready, xc_ready, dt_log, dt_ready, du_ready = (step("conv_ready"), step("xc_ready"), step("dt_log"),
                                                            step("dt_ready"), step("du_ready"))
        hi_ready, left_ready, mid_ready, left2_ready, parts_ready = (step("hi_ready"), step("left_ready"), step("mid_ready"),
                                                                     step("left2_ready"), step("parts_ready"))
        raw_ready, xn_used = step("raw_ready"), step("xn_used")
        dA_ready, dBu_ready, h_ready = step("dA_ready", N), step("dBu_ready", N), step("h_ready", N)
        hc_summed, yT_ready = step("hc_summed", N - 1), step("yT_ready")
        dve_order, act_order = sem("dve_order"), sem("act_order")
        TURNS = B // W
        NWT = 6 + CH * 7
        M = len(states)
        tile_of = lambda i, u, t: chip.x[:, bass.ds((i * W + u) * TPS + t, 1), :].rearrange("p a d -> p (a d)")
        tiles_of = lambda i, u: chip.x[:, bass.ds((i * W + u) * TPS, TPS), :]
        each_u = range(W)

        with nc.Block() as block:
            @block.sync
            def _(sp):
                sp.dma_start(w_in[:], w["W_in"]).then_inc(weights, 16)
                sp.dma_start(w_dt[:], w["W_dt"]).then_inc(weights, 16)
                sp.dma_start(part_of[:], w["part_of"]).then_inc(weights, 16)
                sp.dma_start(w_out[:], w["W_out"].rearrange("(c p) d -> p c d", p=P)).then_inc(weights, 16)
                col = lambda a: a.rearrange("(p o) -> p o", o=1)
                sp.dma_start(ln_w[:], col(w["ln_w"])).then_inc(weights, 16)
                sp.dma_start(ln_b[:], col(w["ln_b"])).then_inc(weights, 16)
                for c in range(CH):
                    rows_ = slice(c * P, (c + 1) * P)
                    sp.dma_start(w_x[:, c, 0:2 * N], w["W_xproj"][rows_, R:]).then_inc(weights, 16)
                    sp.dma_start(w_x[:, c, 2 * N:], w["W_xproj"][rows_, 0:R]).then_inc(weights, 16)
                    sp.dma_start(conv_w[:, c, :], w["conv_w"][rows_, 0, :]).then_inc(weights, 16)
                    sp.dma_start(a_log[:, c, :], w["A_log"][rows_, :]).then_inc(weights, 16)
                    for t, n in ((conv_b, "conv_b"), (b_dt, "b_dt"), (d_par, "D_param")):
                        sp.dma_start(t[:, c:c + 1], col(w[n][rows_])).then_inc(weights, 16)

            @block.gpsimd
            def _(pool):
                for k in range(NB):
                    pool.memset(dA[k][:, :, 0:1], 0.0)
                for u in each_u:
                    ins = pool.memset(xi[u][:, :, 0:TAPS - 1], 0.0)
                ins.then_inc(zeroed, 1)
                with pool.Fori(0, TURNS) as i:
                    for m, (u, n) in enumerate(states):
                        q = m % NB
                        if n == 0:
                            du_ready.wait(pool, i, u)
                        bk.wait_read(pool, ("B", m), i)
                        if m >= NB:
                            h_ready.wait(pool, i, m - NB)
                        dBu_ready.by(pool.tensor_tensor(dBu[q][:], work[u][:], bcast(bs[q][:], n_before=CH), ALU.mult))

            @block.scalar
            def _(act):
                act.wait_ge(weights, 16 * NWT)
                act.wait_ge(zeroed, 1)
                act.activation(a_neg[:], a_log[:], ACT.Exp).then_inc(a_ready, 1)
                act.wait_ge(a_ready, 1)
                act.mul(a_neg[:], a_neg[:], -1.0).then_inc(a_ready, 1)
                act.wait_ge(a_ready, 2)
                c = Chain(act, act_order, per_turn=2)
                with act.Fori(0, TURNS) as i:
                    c.start(i)
                    for u in each_u:
                        mv_ready.wait(act, i, u)
                        std_ready.by(act.activation(std[u][:, :, 0], mv[u][:, :, 1], ACT.Sqrt, bias=chip.ln_eps[:]))
                    for u in each_u:
                        mv2_ready.wait(act, i, u)
                        std2_ready.by(act.activation(std2[u][:, :, 0], mv2[u][:, :, 1], ACT.Sqrt, bias=chip.ln_eps[:]))
                    for u in each_u:
                        bk.wait_filled(act, ("xT", u), i)
                        bk.drain(act.activation(turned[u][:], ps(("xT", u))[:], ACT.Identity, bias=ln_b[:], scale=ln_w[:]), ("xT", u))
                    for u in range(W + 1):
                        for j in range(CH if u < W else 0):
                            bk.wait_filled(act, ("in", u, j), i)
                            bk.drain(act.copy(xi[u][:, j, TAPS - 1:], ps(("in", u, j))[:]), ("in", u, j))
                        for j in range(CH if u < W else 0):
                            bk.wait_filled(act, ("in", u, CH + j), i)
                            bk.drain(act.activation(sz[u][:, j, :], ps(("in", u, CH + j))[:], ACT.Silu), ("in", u, CH + j))
                        if u:
                            conv_ready.wait(act, i, u - 1)
                            for j in range(CH):
                                ins = act.activation(xc[u - 1][:, j, :], work[u - 1][:, j, :], ACT.Silu, bias=conv_b[:, j:j + 1])
                            xc_ready.by(ins)
                    for u in each_u:
                        bk.wait_filled(act, ("bc", u), i)
                        act.copy(dtr[u], ps(("bc", u))[2 * N:2 * N + R, :])
                        hi_ready.by(act.copy(bc[u][0:2 * N, :], ps(("bc", u))[0:2 * N, :]))
                    for u in each_u:
                        left_ready.wait(act, i, u)
                        mid_ready.by(act.copy(mid[u][:], left[u]))
                    for u in each_u:
                        left2_ready.wait(act, i, u)
                        act.copy(bc[u][PART:PART + 2 * N, :], mid[u][:])
                        parts_ready.by(act.copy(bc[u][2 * PART:2 * PART + 2 * N, :], left[u]))
                    for u in each_u:
                        raw_ready.wait(act, i, u)
                        ins = act.activation(work[u][:], dt[u][:], ACT.Abs)
                    c.link(ins)
                    for u in each_u:
                        ins = act.activation(work[u][:], work[u][:], ACT.Exp, scale=-1.0)
                    c.link(ins)
                    for u in each_u:
                        dt_log.by(act.activation(work[u][:], work[u][:], ACT.Ln, bias=1.0))
                    for m, (u, n) in enumerate(states):
                        q = m % NB
                        bk.wait_filled(act, ("B", m), i)
                        if m >= NB:
                            dBu_ready.wait(act, i, m - NB)
                        bk.drain(act.copy(bs[q][:], ps(("B", m))[:]), ("B", m))
                        if n == 0:
                            dt_ready.wait(act, i, u)
                        if m >= NB:
                            h_ready.wait(act, i, m - NB)
                        for j in range(CH):
                            ins = act.activation(dA[q][:, j, 1:], dt[u][:, j, 1:], ACT.Exp, scale=a_neg[:, j, n:n + 1])
                        dA_ready.by(ins)
                c.end()

            @block.vector
            def _(dve):
                for u in each_u:
                    dve.memset(bc[u][:], 0.0)
                dve.wait_ge(weights, 16 * NWT)
                dve.tensor_copy(pick[:], bcast(part_of[:], n_after=P)).then_inc(pick_ready, 1)
                c = Chain(dve, dve_order, per_turn=W * (5 + CH * (TAPS - 1)))
                with dve.Fori(0, TURNS) as i:
                    c.start(i)
                    for u in each_u:
                        mv_ready.by(ln_statistics(chip, dve, c, lambda t: tile_of(i, u, t), stats[u], mv[u], TPS))
                    for u in each_u:
                        std_ready.wait(dve, i, u)
                        c.link(dve.reciprocal(rstd[u][:], std[u][:]))
                        for t in range(TPS):
                            ins = dve.tensor_scalar(xn[u][:, t, :], tile_of(i, u, t), mv[u][:, t, 0:1], rstd[u][:, t, :],
                                                    ALU.subtract, ALU.mult)
                        c.link(ins)
                        mv2_ready.by(ln_statistics(chip, dve, c, lambda t: xn[u][:, t, :], stats2[u], mv2[u], TPS))
                    for u in each_u:
                        std2_ready.wait(dve, i, u)
                        c.link(dve.reciprocal(rstd2[u][:], std2[u][:]))
                        for t in range(TPS):
                            ins = dve.tensor_scalar(rows[u][:, t, :], xn[u][:, t, :], mv2[u][:, t, 0:1], rstd2[u][:, t, :],
                                                    ALU.subtract, ALU.mult)
                        xm_ready.by(ins)
                        xn_used.by(dve.tensor_tensor(tiles_of(i, u), tiles_of(i, u), xn[u], ALU.add))
                    for u in each_u:
                        xn_used.wait(dve, i, u)
                        for j in range(CH):
                            bk.wait_read(dve, ("in", u, j), i)
                            c.link(dve.tensor_scalar(work[u][:, j, :], xi[u][:, j, 0:S], conv_w[:, j, 0:1], None, ALU.mult))
                            for k in range(1, TAPS):
                                ins = dve.scalar_tensor_tensor(work[u][:, j, :], xi[u][:, j, k:k + S], conv_w[:, j, k:k + 1],
                                                               work[u][:, j, :], ALU.mult, ALU.add)
                                if k < TAPS - 1:
                                    c.link(ins)
                        conv_ready.by(ins)
                    for u in each_u:
                        hi_ready.wait(dve, i, u)
                        ins = dve.tensor_tensor(left[u], ps(("bc", u))[0:2 * N, :], bc[u][0:2 * N, :], ALU.subtract)
                        bk.drain(ins, ("bc", u))
                        bk.wait_read(dve, ("bc", u), i)
                        dve.sem_inc(left_ready.sem, 1)
                    for u in each_u:
                        mid_ready.wait(dve, i, u)
                        left2_ready.by(dve.tensor_tensor(left[u], left[u], mid[u][:], ALU.subtract))
                    for u in each_u:
                        for j in range(CH):
                            bk.wait_filled(dve, ("dt", u, j), i)
                            bk.drain(dve.tensor_scalar(dt[u][:, j, :], ps(("dt", u, j))[:], b_dt[:, j:j + 1], None, ALU.add), ("dt", u, j))
                        for j in range(CH):
                            bk.wait_read(dve, ("dt", u, j), i)
                        dve.sem_inc(raw_ready.sem, 1)
                    for u in each_u:
                        dt_log.wait(dve, i, u)
                        dt_ready.by(dve.scalar_tensor_tensor(dt[u][:], dt[u][:], 0.0, work[u][:], ALU.max, ALU.add))
                        dt_ready.wait(dve, i, u)
                        du_ready.by(dve.tensor_tensor(work[u][:], dt[u][:], xc[u][:], ALU.mult))

                    def recur(m):
                        q = m % NB
                        if m >= NH:
                            bk.wait_read(dve, ("C", m - NH), i)
                        dA_ready.wait(dve, i, m)
                        dBu_ready.wait(dve, i, m)
                        h_ready.by(dve.tensor_tensor_scan(h[m % NH][:].rearrange("p c s -> p (c s)"), dA[q][:].rearrange("p c s -> p (c s)"),
                                                          dBu[q][:].rearrange("p c s -> p (c s)"), 0.0, ALU.mult, ALU.add))

                    def finish(u):
                        for j in range(CH):
                            bk.wait_filled(dve, ("y", u, j), i)
                            ins = dve.scalar_tensor_tensor(xc[u][:, j, :], xc[u][:, j, :], d_par[:, j:j + 1], ps(("y", u, j))[:], ALU.mult, ALU.add)
                            bk.drain(ins, ("y", u, j))
                        for j in range(CH):
                            bk.wait_read(dve, ("y", u, j), i)
                        yT_ready.by(dve.tensor_tensor(xc[u][:], xc[u][:], sz[u][:], ALU.mult))

                    def add(u):
                        bk.wait_filled(dve, ("out", u), i)
                        ins = dve.tensor_tensor(tiles_of(i, u), ps(("out", u))[:].rearrange("p (t d) -> p t d", t=TPS), tiles_of(i, u), ALU.add)
                        bk.drain(ins, ("out", u))

                    recur(0)
                    for m, (u, n) in enumerate(states):
                        if m + 1 < M:
                            recur(m + 1)
                        bk.wait_filled(dve, ("C", m), i)
                        h_ready.wait(dve, i, m)
                        if n >= NH:
                            hc_summed.wait(dve, i, u * (N - 1) + n - NH)
                        elif u and n < NH:
                            if n == 0:
                                hc_summed.wait(dve, i, (u - 1) * (N - 1) + N - 2)
                            else:
                                for j in range(CH):
                                    bk.wait_filled(dve, ("y", u - 1, j), i)
                        ins = dve.tensor_tensor(hc[m % NH][:], h[m % NH][:], bcast(ps(("C", m))[:], n_before=CH), ALU.mult)
                        bk.drain(ins, ("C", m))
                        if u and n == FINISH_AT:
                            finish(u - 1)
                        if u and n == ADD_AT:
                            add(u - 1)
                    finish(W - 1)
                    add(W - 1)
                c.end()

            @block.tensor
            def _(pe):
                bk.open(pe)
                pe.wait_ge(weights, 16 * NWT)
                pe.wait_ge(pick_ready, 1)

                def one(job, i, *mms):
                    bk.wait_drained(pe, job, i)
                    for k, (out, lhsT, rhs) in enumerate(mms):
                        ins = pe.matmul(out, lhsT, rhs, start=(k == 0), stop=(k == len(mms) - 1))
                    bk.fill(ins, job)

                with pe.Fori(0, TURNS) as i:
                    for u in each_u:
                        xm_ready.wait(pe, i, u)
                        bk.wait_drained(pe, ("xT", u), i)
                        for t in range(TPS):
                            ins = pe.transpose(ps(("xT", u))[:, t * P:(t + 1) * P], rows[u][:, t, :], chip.ident[:])
                        bk.fill(ins, ("xT", u))
                    for u in each_u:
                        bk.wait_read(pe, ("xT", u), i)
                        for j in range(2 * CH):
                            one(("in", u, j), i, (ps(("in", u, j))[:], w_in[:, j * P:(j + 1) * P], turned[u][:]))
                    for u in each_u:
                        xc_ready.wait(pe, i, u)
                        one(("bc", u), i, *((ps(("bc", u))[0:2 * N + R, :], w_x[:, j, :], xc[u][:, j, :]) for j in range(CH)))
                    for u in each_u:
                        hi_ready.wait(pe, i, u)
                        for j in range(CH):
                            one(("dt", u, j), i, (ps(("dt", u, j))[:], w_dt[:, j * P:(j + 1) * P], dtr[u]))

                    def spread(nm, m):
                        if m < M:
                            u, n = states[m]
                            if n == 0:
                                parts_ready.wait(pe, i, u)
                            one((nm, m), i, (ps((nm, m))[:], pick[:, N * (nm == "C") + n, :], bc[u][:]))

                    def project(u):
                        yT_ready.wait(pe, i, u)
                        bk.wait_drained(pe, ("out", u), i)
                        for t in range(TPS):
                            for j in range(CH):
                                ins = pe.matmul(ps(("out", u))[:, t * D:(t + 1) * D], xc[u][:, j, t * P:(t + 1) * P], w_out[:, j, :],
                                                start=(j == 0), stop=(j == CH - 1))
                        bk.fill(ins, ("out", u))

                    for m in range(AHEAD):
                        spread("B", m)
                    spread("C", 0)
                    for m, (u, n) in enumerate(states):
                        spread("B", m + AHEAD)
                        spread("C", m + 1)
                        bk.wait_read(pe, ("C", m), i)
                        for j in range(CH):
                            if n == 0:
                                bk.wait_drained(pe, ("y", u, j), i)
                            ins = pe.matmul(ps(("y", u, j))[:], chip.ident[:], hc[m % NH][:, j, :], start=(n == 0), stop=(n == N - 1))
                            if n == N - 1:
                                bk.fill(ins, ("y", u, j))
                        if n < N - 1:
                            hc_summed.by(ins)
                        if u and n == FINISH_AT:
                            project(u - 1)
                    project(W - 1)



def build(nc, a, out, stages=range(8)):
    with ExitStack() as ctx:
        chip = Chip(nc, ctx)
        load_stage(chip, a["L0_attn_x"], a["ident"], a["before"], a["count"])
        chip.end_layer()
        part = lambda p: {k[len(p):]: v for k, v in a.items() if k.startswith(p)}
        layers = ((cosine_attention, "L0_attn_"), (top2_glu_experts, "L0_ffn_"),
                  (feature_attention, "L1_attn_"), (switch_experts, "L1_ffn_"),
                  (selective_scan, "L2_attn_"), (expert_choice_experts, "L2_ffn_"),
                  (relative_position_attention, "L3_attn_"), (threshold_experts, "L3_ffn_"))
        for n in stages:
            layer, prefix = layers[n]
            layer(chip, part(prefix))
            chip.end_layer()
        store_stage(chip, out)


def laid_out(inputs):
    a = {k: np.asarray(v) for k, v in inputs.items()}
    for k in ("L0_attn_Wq", "L0_attn_Wk", "L0_attn_Wv", "L0_attn_W1", "L0_attn_W2", "L0_attn_W3",
              "L1_attn_Wq", "L1_attn_Wk", "L1_attn_Wv", "L1_attn_Wo", "L1_attn_Wfc", "L1_attn_proj"):
        a[k] = a[k].T
    a["L3_ffn_Wgt"] = np.concatenate([a.pop("L3_ffn_Wg"), a.pop("L3_ffn_Wt")], axis=1)
    a["L3_ffn_bgt"] = np.concatenate([a.pop("L3_ffn_bg"), a.pop("L3_ffn_bt")])
    a["L3_attn_onehot"] = buckets_by_distance()
    row, head = np.arange(P)[:, None], np.arange(16)[None, :]
    a["L1_attn_spread"] = (np.arange(8)[:, None] == np.arange(P)[None, :] % 8).astype(np.float32)
    a["L1_attn_head_of"] = (row // 8 == head).astype(np.float32)
    a["L1_attn_half_head"] = np.where(row // 8 == head, np.float32(0.5), np.float32(0))
    a["L1_attn_own"] = (row // 16 == np.concatenate([np.arange(64) // 8, np.arange(8)])[None, :]).astype(np.float32)
    a["L2_attn_part_of"] = np.concatenate([np.eye(32), np.eye(32), np.eye(32), np.zeros((32, 32))]).astype(np.float32)
    a["ident"] = np.eye(P, dtype=np.float32)
    a["before"] = np.triu(np.ones((P, P), np.float32), 1)
    a["count"] = np.arange(P, dtype=np.float32)
    return {k: np.ascontiguousarray(v) for k, v in a.items()}


def make_program(nc, inputs, stages=range(8)):
    arrays, aps = {}, {}
    for name, v in laid_out(inputs).items():
        arrays[f"in_{name}_dram"] = v
        aps[name] = nc.dram_tensor(f"in_{name}_dram", v.shape, mybir.dt.from_np(v.dtype), kind="ExternalInput").ap()
    out = nc.dram_tensor("out_0_dram", (B, S, D), F32, kind="ExternalOutput").ap()
    build(nc, aps, out, stages)
    return arrays


def kernel(**inputs):
    import concourse.bacc as _bacc
    from concourse.bass_utils import run_bass_kernel_spmd as _run

    nc = _bacc.Bacc("TRN2", target_bir_lowering=False, num_devices=1)
    arrays = make_program(nc, inputs)
    r = _run(nc, [arrays], core_ids=[0])
    return r.results[0]["out_0_dram"]
```
